# Optimizing a Trainium2 kernel written in Bass

```python
import numpy as np
import jax
import jax.numpy as jnp

def _softmax(x, axis=-1):
    return jax.nn.softmax(x, axis=axis)

def _gelu(x):
    return jax.nn.gelu(x, approximate=True)

def _silu(x):
    return jax.nn.silu(x)

def _sigmoid(x):
    return jax.nn.sigmoid(x)

def _layernorm(x, axis=-1, eps=1e-05):
    m = jnp.mean(x, axis=axis, keepdims=True)
    v = jnp.var(x, axis=axis, keepdims=True)
    return (x - m) / jnp.sqrt(v + eps)

def _scatter_add(tgt, idx, src, axis=0):
    return tgt.at[idx].add(src)

def _segment_sum(src, seg, n):
    return jax.ops.segment_sum(src, seg, n)
kernel_name = 'mk_flamingo_gated_d1_seqx_r4_7ec5dc'

def setup_inputs(seed: int=0):
    np.random.seed(seed)
    _w = jnp.asarray

    def _rec_inputs():
        import jax
        import jax.numpy as jnp
        _rk = jax.random.key(seed)
        x = -0.0003929 + 0.9999 * jax.random.normal(jax.random.fold_in(_rk, 1), (32, 112, 256), jnp.float32)
        _lenS = 112 - jax.random.randint(jax.random.fold_in(_rk, 7), (32,), 0, max(1, 112 // 4) + 1, jnp.int32)
        _lenS2 = 375 - jax.random.randint(jax.random.fold_in(_rk, 8), (32,), 0, max(1, 375 // 4) + 1, jnp.int32)
        _ctx_512P = jax.random.normal(jax.random.fold_in(_rk, 11), (32, 16, 128), jnp.float32)
        _ctx_512c = jax.random.dirichlet(jax.random.fold_in(_rk, 511), 0.3 * jnp.ones((16,), jnp.float32), (32, 375))
        _ctx_512t = jnp.einsum('bsk,bkd->bsd', _ctx_512c, _ctx_512P)
        _ctx_512t = _ctx_512t * jax.lax.rsqrt(jnp.mean(jnp.square(_ctx_512t)) + 1e-12) * 0.953939
        ctx_512 = -1.39393e-06 + 0.999914 * (_ctx_512t + 0.3 * jax.random.normal(jax.random.fold_in(_rk, 611), (32, 375, 128), jnp.float32))
        _g = jax.random.normal(jax.random.fold_in(_rk, 9001), (2, 1), jnp.float32)
        _g = jnp.sign(_g) * jnp.maximum(jnp.abs(_g), 1.0) + (_g == 0) * 1.0
        g_xattn = _g[0]
        g_ffn = _g[1]
        return (x, ctx_512, g_xattn, g_ffn)
    x, ctx_512, g_xattn, g_ffn = _rec_inputs()

    def _L0_xattn_setup():
        import jax, jax.numpy as jnp
        import numpy as np
        HEADS = 16
        D_MODEL = 256
        IMG_MODEL = 128
        D_K = D_MODEL // HEADS
        key = jax.random.key(seed)
        ks = jax.random.split(key, 12)
        B, LQ, LKV = (8, 512, 256)
        s_dm = 1.0 / np.sqrt(D_MODEL)
        s_im = 1.0 / np.sqrt(IMG_MODEL)
        return {'q': jax.random.normal(ks[0], (B, LQ, D_MODEL), jnp.float32), 'k': jax.random.normal(ks[1], (B, LKV, IMG_MODEL), jnp.float32), 'v': jax.random.normal(ks[2], (B, LKV, IMG_MODEL), jnp.float32), 'Wq': jax.random.normal(ks[3], (D_MODEL, D_MODEL), jnp.float32) * s_dm, 'bq': jnp.zeros((D_MODEL,), jnp.float32), 'Wk': jax.random.normal(ks[4], (IMG_MODEL, D_MODEL), jnp.float32) * s_im, 'bk': jnp.zeros((D_MODEL,), jnp.float32), 'Wv': jax.random.normal(ks[5], (IMG_MODEL, D_MODEL), jnp.float32) * s_im, 'bv': jnp.zeros((D_MODEL,), jnp.float32), 'Wo': jax.random.normal(ks[6], (D_MODEL, D_MODEL), jnp.float32) * s_dm, 'bo': jnp.zeros((D_MODEL,), jnp.float32)}
    _L0_xattn_all = _L0_xattn_setup()
    _L0_xattn_in = {k: v for k, v in _L0_xattn_all.items() if k in ('Wq', 'bq', 'Wk', 'bk', 'Wv', 'bv', 'Wo', 'bo')}
    del _L0_xattn_all

    def _L0_ffn_setup():
        import jax, jax.numpy as jnp
        import numpy as np
        B, L, H, E, FF, C = (4, 512, 256, 8, 1024, 2)
        key = jax.random.key(seed)
        ks = jax.random.split(key, 6)
        s = 0.02
        return {'x': jax.random.normal(ks[0], (B, L, H), dtype=jnp.float32), 'Wg': jax.random.normal(ks[1], (H, E), dtype=jnp.float32) * s, 'W1': jax.random.normal(ks[2], (E, H, FF), dtype=jnp.float32) * s, 'b1': jnp.zeros((E, FF), dtype=jnp.float32), 'W2': jax.random.normal(ks[3], (E, FF, H), dtype=jnp.float32) * s, 'b2': jnp.zeros((E, H), dtype=jnp.float32)}
    _L0_ffn_all = _L0_ffn_setup()
    _L0_ffn_in = {k: v for k, v in _L0_ffn_all.items() if k in ('Wg', 'W1', 'b1', 'W2', 'b2')}
    del _L0_ffn_all
    return {'x': x, 'ctx_512': ctx_512, 'g_xattn': g_xattn, 'g_ffn': g_ffn, 'L0_xattn_Wq': _L0_xattn_in['Wq'], 'L0_xattn_bq': _L0_xattn_in['bq'], 'L0_xattn_Wk': _L0_xattn_in['Wk'], 'L0_xattn_bk': _L0_xattn_in['bk'], 'L0_xattn_Wv': _L0_xattn_in['Wv'], 'L0_xattn_bv': _L0_xattn_in['bv'], 'L0_xattn_Wo': _L0_xattn_in['Wo'], 'L0_xattn_bo': _L0_xattn_in['bo'], 'L0_ffn_Wg': _L0_ffn_in['Wg'], 'L0_ffn_W1': _L0_ffn_in['W1'], 'L0_ffn_b1': _L0_ffn_in['b1'], 'L0_ffn_W2': _L0_ffn_in['W2'], 'L0_ffn_b2': _L0_ffn_in['b2']}

def reference(x, ctx_512, g_xattn, g_ffn, L0_xattn_Wq, L0_xattn_bq, L0_xattn_Wk, L0_xattn_bk, L0_xattn_Wv, L0_xattn_bv, L0_xattn_Wo, L0_xattn_bo, L0_ffn_Wg, L0_ffn_W1, L0_ffn_b1, L0_ffn_W2, L0_ffn_b2):
    import jax
    import jax.numpy as jnp

    def _L0_xattn_ref(q, k, v, Wq, bq, Wk, bk, Wv, bv, Wo, bo):
        import jax, jax.numpy as jnp
        import numpy as np
        HEADS = 16
        D_MODEL = 256
        IMG_MODEL = 128
        D_K = D_MODEL // HEADS
        B, LQ, _ = q.shape
        LKV = k.shape[1]
        qh = (q @ Wq + bq).reshape(B, LQ, HEADS, D_K).transpose(0, 2, 1, 3)
        kh = (k @ Wk + bk).reshape(B, LKV, HEADS, D_K).transpose(0, 2, 1, 3)
        vh = (v @ Wv + bv).reshape(B, LKV, HEADS, D_K).transpose(0, 2, 1, 3)
        scale = 1.0 / np.sqrt(D_K)
        scores = jnp.einsum('bhqd,bhkd->bhqk', qh, kh) * scale
        attn = jax.nn.softmax(scores, axis=-1)
        out = jnp.einsum('bhqk,bhkd->bhqd', attn, vh)
        concat = out.transpose(0, 2, 1, 3).reshape(B, LQ, D_MODEL)
        return concat @ Wo + bo

    def _L0_ffn_ref(x, Wg, W1, b1, W2, b2):
        import jax, jax.numpy as jnp
        import numpy as np
        B, L, H, E, FF, C = (4, 512, 256, 8, 1024, 2)
        b, l, h = x.shape
        e = Wg.shape[1]
        n = b * l
        k = min(max(int(n * C / e), 1), n)
        xt = x.reshape(n, h)
        S = jax.nn.sigmoid(xt @ Wg).T
        G, I = jax.lax.top_k(S, k)
        ex = xt[I]
        hid = jax.nn.gelu(jnp.einsum('ekh,ehf->ekf', ex, W1) + b1[:, None, :], approximate=False)
        out = (jnp.einsum('ekf,efh->ekh', hid, W2) + b2[:, None, :]) * G[..., None]
        new_x = jnp.zeros_like(xt).at[I.reshape(-1)].add(out.reshape(-1, h))
        return new_x.reshape(b, l, h)
    x = x + jnp.tanh(g_xattn[0]) * _L0_xattn_ref(_layernorm(x, axis=-1), ctx_512, ctx_512, L0_xattn_Wq, L0_xattn_bq, L0_xattn_Wk, L0_xattn_bk, L0_xattn_Wv, L0_xattn_bv, L0_xattn_Wo, L0_xattn_bo)
    x = x + jnp.tanh(g_ffn[0]) * _L0_ffn_ref(_layernorm(x, axis=-1), L0_ffn_Wg, L0_ffn_W1, L0_ffn_b1, L0_ffn_W2, L0_ffn_b2)
    return x

_drawn_inputs = setup_inputs


def setup_inputs(seed=0):
    import zlib

    import numpy as np

    out = dict(_drawn_inputs(seed))
    spreads = {'L0_xattn_bq': (0.0, 0.394),
     'L0_xattn_bk': (0.0, 0.8),
     'L0_xattn_bv': (0.0, 0.1),
     'L0_xattn_bo': (0.0, 0.1),
     'L0_ffn_b1': (0.0, 0.292),
     'L0_ffn_b2': (0.0, 0.1)}
    factors = {}
    for name, (base, spread) in spreads.items():
        noise = np.random.default_rng([zlib.crc32(name.encode()), seed]).standard_normal(out[name].shape)
        drawn = base * np.exp(spread * noise) if base else spread * noise
        out[name] = jnp.asarray(drawn.astype(out[name].dtype))
    for name, factor in factors.items():
        out[name] = (out[name] * factor).astype(out[name].dtype)
    return out
```

```python
import concourse.bass as bass
from concourse import mybir
from contextlib import ExitStack

F32 = mybir.dt.float32
F32R = mybir.dt.float32r
BF16 = mybir.dt.bfloat16
I32 = mybir.dt.int32
ALU = mybir.AluOpType
ACT = mybir.ActivationFunctionType
AXX = mybir.AxisListType.X

B, LQ, D = 32, 112, 256
LK, C = 375, 128
H, DK = 16, 16
NE, FF = 8, 1024
TOK = B * LQ
CAP = TOK * 2 // NE
EPS = 1e-5

KCH = [(0, 128), (128, 128), (256, LK - 256)]
KPAD = 384
K_SLOT = [0, 0, 0, 1, 1, 2]
Q_SLOT = [0, 1, 2, 0, 1, 0]
ROWS = 16 * len(K_SLOT)
VW = 64


def wait(eng, sem, count):
    if not (isinstance(count, int) and count <= 0):
        eng.wait_ge(sem, count)


def wait_alone(eng, sem, count, passed):
    wait(eng, sem, count)
    if not isinstance(count, int):
        eng.sem_inc(passed, 1)


class Sems:

    def __init__(self, nc, ctx, stage):
        self.nc, self.ctx, self.stage, self.made = nc, ctx, stage, {}

    def __call__(self, name):
        if name not in self.made:
            self.made[name] = self.ctx.enter_context(self.nc.semaphore(f"{self.stage}_{name}"))
        return self.made[name]


def queries(nc, T, x):
    G, NB = B // 4, 4 * LQ
    with ExitStack() as ctx:
        sem = Sems(nc, ctx, "q")

        def sb(name, shape, dt=F32):
            return ctx.enter_context(nc.sbuf_tensor("q_" + name, shape, dt))

        def banks(name, n=2):
            return [ctx.enter_context(nc.psum_tensor(f"q_{name}{i}", [128, 512], F32)) for i in range(n)]

        xin = [sb(f"xin{i}", [LQ, 4, D]) for i in range(2)]
        xn = [sb(f"xn{i}", [LQ, 4, D]) for i in range(2)]
        st = sb("st", [LQ, 4, 6])
        mv = sb("mv", [LQ, 4, 2])
        std = sb("std", [LQ, 4])
        y0 = sb("y0", [LQ, 4])
        yt = sb("yt", [LQ, 4])
        rstd = sb("rstd", [LQ, 4])
        xnT = sb("xnT", [128, 2, NB])
        q32 = [sb(f"q32_{i}", [128, 2, NB]) for i in range(2)]
        pT = banks("pT")
        pQ = banks("pQ")
        x_loaded = [sem("x_loaded0"), sem("x_loaded1")]
        chain, var_ready, std_ready, xn_ready = sem("chain"), sem("var_ready"), sem("std_ready"), sem("xn_ready")
        xt_ready, xt_copied, q_ready, q_copied = sem("xt_ready"), sem("xt_copied"), sem("q_ready"), sem("q_copied")
        cut, q_cut, passed, passed_p = sem("cut"), sem("q_cut"), sem("passed"), sem("passed_p")
        block = ctx.enter_context(nc.Block())

        @block.sync
        def _(sp):
            with sp.Fori(0, G // 2) as i:
                for r in range(2):
                    sp.wait_ge(xn_ready, i * 2 + r + 1)
                    sp.dma_start(xin[r][:], x[bass.ds(i * 8 + r * 4, 4)].rearrange("b p d -> p b d"))\
                      .then_inc(x_loaded[r], 16)

        @block.vector
        def _(dve):
            dve.sem_inc(xn_ready, 2)
            with dve.Fori(0, G // 2) as i:
                for r in range(2):
                    at = [0]

                    def link(ins):
                        at[0] += 1
                        ins.then_inc(chain, 1)
                        wait_alone(dve, chain, i * 26 + 13 * r + at[0], passed)

                    dve.wait_ge(x_loaded[r], i * 16 + 16)
                    for b in range(4):
                        ins = dve.bn_stats(st[:, b, :], xin[r][:, b, :])
                        if b < 3:
                            ins.then_inc(chain, 1)
                            at[0] += 1
                        else:
                            link(ins)
                    for b in range(4):
                        ins = dve.bn_aggr(mv[:, b, :], st[:, b, :])
                        if b < 3:
                            ins.then_inc(chain, 1)
                            at[0] += 1
                        else:
                            link(ins)
                    link(dve.tensor_scalar(yt[:], mv[:, :, 1], EPS, None, ALU.add))
                    dve.sem_inc(var_ready, 1)
                    dve.wait_ge(std_ready, i * 2 + r + 1)
                    link(dve.reciprocal(y0[:], std[:]))
                    link(dve.tensor_tensor(rstd[:], y0[:], y0[:], ALU.mult))
                    link(dve.scalar_tensor_tensor(rstd[:], rstd[:], -0.5, yt[:], ALU.mult, ALU.mult))
                    link(dve.scalar_tensor_tensor(rstd[:], rstd[:], 1.5, y0[:], ALU.add, ALU.mult))
                    wait(dve, xt_ready, i * 2 + r + 1)
                    for b in range(4):
                        ins = dve.tensor_scalar(xn[r][:, b, :], xin[r][:, b, :], mv[:, b, 0:1], rstd[:, b:b + 1],
                                                ALU.subtract, ALU.mult)
                    ins.then_inc(xn_ready, 1)

        @block.gpsimd
        def _(pool):
            with pool.Fori(0, G // 2) as i:
                for r in range(2):
                    qs = T.qp[:, :, :, bass.ds(i * 2 * NB + r * NB, NB)]
                    wait_alone(pool, q_copied, i * 4 + 2 * r + 2, passed_p)
                    pool.tensor_copy(qs[:, 0], q32[r][:]).then_inc(cut, 1)
                    wait_alone(pool, cut, i * 6 + 3 * r + 1, passed_p)
                    pool.tensor_tensor(q32[r][:], q32[r][:], qs[:, 0], ALU.subtract).then_inc(cut, 1)
                    wait_alone(pool, cut, i * 6 + 3 * r + 2, passed_p)
                    pool.tensor_copy(qs[:, 1], q32[r][:]).then_inc(cut, 1)
                    wait_alone(pool, cut, i * 6 + 3 * r + 3, passed_p)
                    pool.tensor_tensor(qs[:, 2], q32[r][:], qs[:, 1], ALU.subtract).then_inc(q_cut, 1)

        @block.scalar
        def _(act):
            act.sem_inc(q_cut, 2)
            with act.Fori(0, G // 2) as i:
                for r in range(2):
                    act.wait_ge(var_ready, i * 2 + r + 1)
                    act.activation(std[:], yt[:], ACT.Sqrt).then_inc(std_ready, 1)
                    for k in range(2):
                        act.wait_ge(xt_ready, i * 2 + r + 3)
                        act.activation(xnT[:, k, :], pT[k][:, 0:NB], ACT.Copy).then_inc(xt_copied, 1)
                    act.wait_ge(q_cut, i * 2 + r + 1)
                    for t in range(2):
                        act.wait_ge(q_ready, i * 4 + 2 * r + t + 1)
                        act.activation(q32[r][:, t, :], pQ[t][:, 0:NB], ACT.Identity, bias=T.bq[:, t:t + 1],
                                       scale=float(DK) ** -0.5).then_inc(q_copied, 1)

        @block.tensor
        def _(pe):
            pe.sem_inc(xt_ready, 2)
            with pe.Fori(0, G // 2) as i:
                for r in range(2):
                    pe.wait_ge(xn_ready, i * 2 + r + 3)
                    for k in range(2):
                        for b in range(4):
                            last = pe.transpose(pT[k][:, b * LQ:(b + 1) * LQ], xn[r][:, b, k * 128:(k + 1) * 128],
                                                T.ident[0:LQ, 0:LQ])
                    last.then_inc(xt_ready, 1)
                    pe.wait_ge(xt_copied, i * 4 + 2 * r + 2)
                    for t in range(2):
                        for k in range(2):
                            last = pe.matmul(pQ[t][:, 0:NB], T.wq[:, k, t, :], xnT[:, k, :], start=(k == 0),
                                             stop=(k == 1))
                        last.then_inc(q_ready, 1)
                    pe.wait_ge(q_copied, i * 4 + 2 * r + 2)


def attention(nc, T, x, ctx_in, x1_out, xn_out):
    with ExitStack() as ctx:
        sem = Sems(nc, ctx, "a")

        def sb(name, shape, dt=F32):
            return ctx.enter_context(nc.sbuf_tensor("a_" + name, shape, dt))

        def banks(name, n=2):
            return [ctx.enter_context(nc.psum_tensor(f"a_{name}{i}", [128, 512], F32)) for i in range(n)]

        craw = [sb(f"craw{i}", [128, 3, C]) for i in range(2)]
        cT = [sb(f"cT{i}", [128, LK]) for i in range(4)]
        k32 = sb("k32", [128, 2, LK])
        kp = [sb(f"kp{i}", [128, 3, 2, LK], BF16) for i in range(2)]
        kst = [sb(f"kst{i}", [ROWS + 2, H, KPAD], BF16) for i in range(4)]
        qst = sb("qst", [ROWS + 2, H, 4 * LQ], BF16)
        V = [sb(f"V{i}", [128, 3, H // 2, VW]) for i in range(2)]
        P = [sb(f"P{i}", [128, 3, 4 * LQ]) for i in range(2)]
        O = sb("O", [128, 2, 4 * LQ])
        nm = sb("nm", [LQ, H])
        mm = sb("mm", [LQ, 2, H], BF16)
        mT = sb("mT", [2 * H, LQ], BF16)
        rd = [sb(f"rd{i}", [LQ, 2, 2, 2]) for i in range(2)]
        cc = [sb(f"cc{i}", [LQ, D]) for i in range(2)]
        ccT = sb("ccT", [128, 2 * LQ])
        xb = [sb(f"xb{i}", [LQ, D]) for i in range(2)]
        x1 = [sb(f"x1_{i}", [LQ, D]) for i in range(2)]
        x2 = [sb(f"x2_{i}", [LQ, D]) for i in range(2)]
        x2T = sb("x2T", [128, 2 * LQ])
        stats, mv = sb("stats", [LQ, 6]), sb("mv", [LQ, 2])
        var, y, yy = sb("var", [LQ, 1]), sb("y", [LQ, 1]), sb("yy", [LQ, 1])
        pT = banks("pT")
        pS = banks("pS")
        pO = banks("pO")
        pM = banks("pM")

        ctx_loaded = [sem("ctx_loaded0"), sem("ctx_loaded1")]
        kst_loaded = [sem(f"kst_loaded{i}") for i in range(4)]
        qst_loaded = [sem("qst_loaded0"), sem("qst_loaded1")]
        mrow_loaded = [sem("mrow_loaded0"), sem("mrow_loaded1")]
        t_ready, s_ready, o_ready = sem("t_ready"), sem("s_ready"), sem("o_ready")
        ct_ready, k_ready, v_ready = sem("ct_ready"), sem("k_ready"), sem("v_ready")
        ot_ready, mt_ready = sem("ot_ready"), sem("mt_ready")
        exp_done, ct_copied, k_copied, o_copied, mt_copied = (sem("exp_done"), sem("ct_copied"), sem("k_copied"),
                                                            sem("o_copied"), sem("mt_copied"))
        s_used, m_split, v_copied, ot_used = sem("s_used"), sem("m_split"), sem("v_copied"), sem("ot_used")
        k_cut, kchain, filled = sem("k_cut"), sem("kchain"), sem("filled")
        cct_ready, cct_copied, wo_ready, x1_ready = sem("cct_ready"), sem("cct_copied"), sem("wo_ready"), sem("x1_ready")
        xt_ready, xt_copied, lg_ready, lg_copied = sem("xt_ready"), sem("xt_copied"), sem("lg_ready"), sem("lg_copied")
        wo_read, x2_ready, ln = sem("wo_read"), sem("x2_ready"), sem("ln")
        xb_loaded = [sem("xb_loaded0"), sem("xb_loaded1")]
        stored = [sem("stored0"), sem("stored1")]
        passed_dve = sem("passed_dve")
        passed, passed_sp = sem("passed"), sem("passed_sp")
        m_high, rd_ready = sem("m_high"), sem("rd_ready")

        S_HEADS = [[0], [1, 2], [3], [4], [5, 6], [7]]

        def run(eng, step):
            def static(m):
                step(m // 4, m % 4, lambda off: 0 <= m + off < B)

            for m in range(-4, 1):
                static(m)
            with eng.Fori(0, B // 4 - 2) as i:
                for r in range(1, 5):
                    step(i, r, lambda off: True)
            for m in range(B - 7, B + 1):
                static(m)

        def count(i, r, off, per, add):
            return i * (4 * per) + ((r + off) * per + add)

        def fills(i, r, off, every, per, add=0):
            return i * (4 // every * per) + ((r + off) // every * per + add)

        PIECES = [(ct_copied, 4, 1, 1), (k_copied, 4, 2, 1), (k_copied, 4, 2, 2), (v_copied, 2, 2, 1),
                  (v_copied, 2, 2, 2), (ot_used, 0, 2, 1), (ot_used, 0, 2, 2), (xt_copied, -1, 1, 1),
                  (mt_copied, 2, 1, 1), (cct_copied, 0, 1, 1), (wo_read, 0, 1, 1), (lg_copied, -1, 1, 1)]

        block = ctx.enter_context(nc.Block())

        @block.sync
        def _(sp):
            def step(i, r, live):
                if live(4):
                    wait_alone(sp, ct_ready, count(i, r, 2, 1, 1), passed_sp)
                    n = count(i, r, 4, LK, 0)
                    buf, src = r % 2, ctx_in.rearrange("b k c -> (b k) c")
                    sp.dma_start(craw[buf][:, 0:2, :], src[bass.ds(n, 256)].rearrange("(c p) d -> p c d", c=2))\
                      .then_inc(ctx_loaded[buf], 16)
                    sp.dma_start(craw[buf][0:KCH[2][1], 2, :], src[bass.ds(n + 256, KCH[2][1])])\
                      .then_inc(ctx_loaded[buf], 16)
                if r % 2 == 1 and live(3):
                    half = (r + 3) % 4 // 2
                    cols = slice(half * 2 * LQ, (half + 1) * 2 * LQ)
                    wait_alone(sp, t_ready, count(i, r, 0, 12, 12), passed_sp)
                    for s in range(len(Q_SLOT)):
                        src = T.qp[:, Q_SLOT[s], :, bass.ds(count(i, r, 3, LQ, 0), 2 * LQ)]
                        sp.dma_start(qst[16 * s:16 * s + 16, :, cols], src).then_inc(qst_loaded[half], 16)
                if live(3):
                    wait_alone(sp, k_cut, count(i, r, 3, 1, 1), passed_sp)
                    wait_alone(sp, mt_copied, count(i, r, 1, 1, 1), passed_sp)
                    for s in range(len(K_SLOT)):
                        sp.dma_start(kst[(r + 3) % 4][16 * s:16 * s + 16, :, 0:LK], kp[(r + 3) % 2][:, K_SLOT[s]])\
                          .then_inc(kst_loaded[(r + 3) % 4], 16)
                if live(1):
                    wait_alone(sp, x1_ready, count(i, r, -1, 1, 1), passed_sp)
                    sp.dma_start(xb[(r + 1) % 2][:], x[bass.ds(count(i, r, 1, LQ, 0), LQ)])\
                      .then_inc(xb_loaded[(r + 1) % 2], 16)
                if live(-1):
                    wait_alone(sp, x2_ready, count(i, r, -1, 1, 1), passed_sp)
                    rows = bass.ds(count(i, r, -1, LQ, 0), LQ)
                    sp.dma_start(x1_out[rows], x1[(r - 1) % 2][:]).then_inc(stored[(r - 1) % 2], 16)
                    sp.dma_start(xn_out[rows], x2[(r - 1) % 2][:]).then_inc(stored[(r - 1) % 2], 16)
                if live(2):
                    wait(sp, mt_copied, count(i, r, 2, 1, 1))
                    c0 = (r + 2) % 4 * LQ
                    sp.dma_start(qst[ROWS:ROWS + 2, :, c0:c0 + LQ], mT[:]).then_inc(mrow_loaded[(r + 2) % 2], 16)

            run(sp, step)
            for p in range(2):
                sp.wait_ge(stored[p], B // 2 * 32)

        @block.gpsimd
        def _(pool):
            def step(i, r, live):
                if not live(4):
                    return
                out, at = kp[(r + 4) % 2], [0]
                wait(pool, k_copied, count(i, r, 4, 2, 2))
                wait_alone(pool, kst_loaded[(r + 2) % 4], fills(i, r, 2, 4, 96, 96), passed)

                def link(ins):
                    at[0] += 1
                    ins.then_inc(kchain, 1)
                    wait_alone(pool, kchain, count(i, r, 4, 3, at[0]), passed)

                link(pool.tensor_copy(out[:, 0], k32[:]))
                link(pool.tensor_tensor(k32[:], k32[:], out[:, 0], ALU.subtract))
                link(pool.tensor_copy(out[:, 1], k32[:]))
                pool.tensor_tensor(out[:, 2], k32[:], out[:, 1], ALU.subtract).then_inc(k_cut, 1)

            run(pool, step)

        @block.scalar
        def _(act):
            def step(i, r, live):
                for u in range(12):
                    if live(1):
                        act.wait_ge(t_ready, count(i, r, 1, 12, u + 1))
                        quad, c = divmod(u, 3)
                        act.activation(P[quad % 2][:, c, :], pT[u % 2][:, 0:4 * LQ], ACT.Exp).then_inc(exp_done, 1)
                    if u == 7 and live(-1):
                        act.wait_ge(xt_ready, count(i, r, -1, 1, 1))
                        act.activation(x2T[:], pM[1][:, 0:2 * LQ], ACT.Copy).then_inc(xt_copied, 1)
                    if u == 11 and live(-1):
                        act.wait_ge(lg_ready, count(i, r, -1, 1, 1))
                        act.activation(T.lg[:, bass.ds(count(i, r, -1, NE, 0), NE)], pM[1][0:LQ, 0:NE], ACT.Copy)\
                           .then_inc(lg_copied, 1)
                    if u == 9 and live(0):
                        act.wait_ge(cct_ready, count(i, r, 0, 1, 1))
                        act.activation(ccT[:], pM[1][:, 0:2 * LQ], ACT.Copy).then_inc(cct_copied, 1)
                    if u == 0 and live(4):
                        act.wait_ge(ct_ready, count(i, r, 4, 1, 1))
                        act.activation(cT[r % 4][:], pM[0][:, 0:LK], ACT.Copy).then_inc(ct_copied, 1)
                    if u in (1, 2) and live(4):
                        t = u - 1
                        wait(act, k_cut, count(i, r, 4, 1, 0))
                        act.wait_ge(k_ready, count(i, r, 4, 2, t + 1))
                        act.activation(k32[:, t, :], pM[u % 2][:, 0:LK], ACT.Identity, bias=T.bk[:, t:t + 1])\
                           .then_inc(k_copied, 1)
                    if u == 3 and live(0):
                        act.wait_ge(o_ready, count(i, r, 0, 2, 2))
                        act.activation(O[:, 1, :], pO[1][:, 0:4 * LQ], ACT.Copy).then_inc(o_copied, 1)
                    if u == 9 and live(1):
                        act.wait_ge(o_ready, count(i, r, 1, 2, 1))
                        act.activation(O[:, 0, :], pO[0][:, 0:4 * LQ], ACT.Copy).then_inc(o_copied, 1)
                    if u == 8 and live(2):
                        act.wait_ge(mt_ready, count(i, r, 2, 1, 1))
                        wait(act, mrow_loaded[(r + 1) % 2], fills(i, r, 1, 2, 16, 16))
                        act.activation(mT[:], pM[0][0:2 * H, 0:LQ // 2].bitcast(BF16), ACT.Copy).then_inc(mt_copied, 1)

            run(act, step)

        @block.vector
        def _(dve):
            for b in range(4):
                dve.memset(kst[b][:, :, LK:KPAD], 0.0).then_inc(filled, 1)
                dve.memset(kst[b][ROWS:ROWS + 2, :, 0:LK], 1.0).then_inc(filled, 1)
            for b in range(2):
                dve.memset(V[b][:], 0.0).then_inc(filled, 1)
            dve.wait_ge(filled, 10)
            for b in range(2):
                for s in range(2):
                    dve.memset(V[b][:, :, :, 17 * s + 16:17 * s + 17], 1.0).then_inc(filled, 1)
            dve.wait_ge(filled, 14)

            def score_max(i, r, off, h):
                dve.wait_ge(s_ready, count(i, r, off, H, h + 1))
                if h == 0:
                    wait(dve, m_split, count(i, r, off, 1, 0))
                dve.tensor_reduce(nm[:, h:h + 1], pS[h % 2][0:LQ, 0:LK], AXX, ALU.max, negate=True).then_inc(s_used, 1)

            def layernorm(i, r, k):
                p, yb = (r - 1) % 2, y[:].bitcast(I32)
                if k == 0:
                    wait_alone(dve, ln, count(i, r, -1, 14, 1), passed_dve)
                    ins = dve.bn_aggr(mv[:], stats[:])
                else:
                    dve.wait_ge(ln, count(i, r, -1, 14, k + 1))
                if k == 1:
                    ins = dve.tensor_scalar(var[:], mv[:, 1:2], EPS, None, ALU.add)
                elif k == 2:
                    ins = dve.tensor_scalar(yb, var[:].bitcast(I32), 1, None, ALU.logical_shift_right)
                elif k == 3:
                    ins = dve.tensor_scalar(yb, yb, -1.0, float(0x5f3759df), ALU.mult, ALU.add)
                elif k == 13:
                    ins = dve.tensor_scalar(x2[p][:], x1[p][:], mv[:, 0:1], y[:], ALU.subtract, ALU.mult)
                elif k % 3 == 1:
                    ins = dve.tensor_tensor(yy[:], y[:], y[:], ALU.mult)
                elif k % 3 == 2:
                    ins = dve.scalar_tensor_tensor(yy[:], yy[:], -0.5, var[:], ALU.mult, ALU.mult)
                elif k:
                    ins = dve.scalar_tensor_tensor(y[:], yy[:], 1.5, y[:], ALU.add, ALU.mult)
                ins.then_inc(x2_ready if k == 13 else ln, 1)

            def step(i, r, live):
                for u in range(12):
                    if u < 7 and live(-1):
                        layernorm(i, r, 2 * u)
                    if u < 6 and live(2):
                        for h in S_HEADS[u]:
                            score_max(i, r, 2, h + 8)
                    if u >= 6 and live(3):
                        for h in S_HEADS[u - 6]:
                            score_max(i, r, 3, h)
                    if u < 7 and live(-1):
                        layernorm(i, r, 2 * u + 1)
                    if u == 5 and live(2):
                        dve.wait_ge(s_used, count(i, r, 2, H, H))
                        wait(dve, mt_ready, count(i, r, 2, 1, 0))
                        dve.tensor_copy(mm[:, 0, :], nm[:]).then_inc(m_high, 1)
                        dve.wait_ge(m_high, count(i, r, 2, 1, 1))
                        dve.tensor_tensor(mm[:, 1, :], nm[:], mm[:, 0, :], ALU.subtract).then_inc(m_split, 1)
                    if u in (3, 4) and live(2):
                        v = V[(r + 2) % 2]
                        dve.wait_ge(v_ready, count(i, r, 2, 2, u - 2))
                        for c in ((0, 1) if u == 3 else (2,)):
                            n = KCH[c][1]
                            o = v[0:n, c, :, 0:34].rearrange("p g (s w) -> p g s w", s=2)[:, :, :, 0:DK]
                            src = pM[u % 2][0:n, (c % 2) * D:(c % 2 + 1) * D]
                            ins = dve.tensor_tensor(o, src.rearrange("p (g s w) -> p g s w", g=8, s=2),
                                                    T.bv[0:n].rearrange("p (g s w) -> p g s w", g=8, s=2), ALU.add)
                        ins.then_inc(v_copied, 1)
                    if u in (5, 6) and live(0):
                        hb = u - 5
                        dve.wait_ge(ot_ready, count(i, r, 0, 2, hb + 1))
                        src = pM[u % 2][0:LQ, 0:512].rearrange("p (i s j w) -> p s i j w", i=2, s=2, j=2)
                        out = cc[r % 2][:, hb * 128:(hb + 1) * 128]\
                            .rearrange("p (i j s w) -> p s i j w", i=2, j=2, s=2)
                        for s in range(2):
                            dve.reciprocal(rd[hb][:, s], src[:, s, :, :, 17 * s + DK]).then_inc(rd_ready, 1)
                        dve.wait_ge(rd_ready, count(i, r, 0, 4, 2 * hb + 2))
                        for s in range(2):
                            ins = dve.tensor_tensor(out[:, s], src[:, s, :, :, 17 * s:17 * s + DK],
                                                    rd[hb][:, s].unsqueeze(3).to_broadcast([LQ, 2, 2, DK]), ALU.mult)
                        ins.then_inc(ot_used, 1)

                    if u == 10 and live(0):
                        xo, p = x1[r % 2], r % 2
                        wait(dve, stored[p], fills(i, r, -2, 2, 32, 32))
                        dve.wait_ge(wo_ready, count(i, r, 0, 1, 1))
                        dve.tensor_tensor(xo[:], pM[0][0:LQ, 0:D], T.bo[:], ALU.add).then_inc(wo_read, 1)
                        dve.wait_ge(wo_read, count(i, r, 0, 1, 1))
                        dve.wait_ge(xb_loaded[p], fills(i, r, 0, 2, 16, 16))
                        dve.scalar_tensor_tensor(xo[:], xo[:], T.gx[0:LQ], xb[p][:], ALU.mult, ALU.add).then_inc(x1_ready, 1)
                        dve.wait_ge(x1_ready, count(i, r, 0, 1, 1))
                        dve.bn_stats(stats[:], xo[:]).then_inc(ln, 1)

            run(dve, step)

        @block.tensor
        def _(pe):
            pe.wait_ge(filled, 14)

            def bank_free(i, r, u, live):
                back, k = 0, u - 2
                while back < 6:
                    if k < 0:
                        back, k = back + 1, k + 12
                    sem_, off, per, nth = PIECES[k]
                    if live(off - back):
                        wait(pe, sem_, count(i, r, off - back, per, nth))
                        return
                    k -= 2

            def piece(i, r, u, bank):
                if u == 7:
                    pe.wait_ge(x2_ready, count(i, r, -1, 1, 1))
                    for k in range(2):
                        last = pe.transpose(bank[:, k * LQ:(k + 1) * LQ], x2[(r - 1) % 2][:, k * 128:(k + 1) * 128],
                                            T.ident[0:LQ, 0:LQ])
                    last.then_inc(xt_ready, 1)
                elif u == 0:
                    pe.wait_ge(ctx_loaded[r % 2], fills(i, r, 4, 2, 32, 32))
                    for c, (k0, n) in enumerate(KCH):
                        last = pe.transpose(bank[:, k0:k0 + n], craw[r % 2][0:n, c, :], T.ident[0:n, 0:n])
                    last.then_inc(ct_ready, 1)
                elif u in (1, 2):
                    pe.wait_ge(ct_copied, count(i, r, 4, 1, 1))
                    pe.matmul(bank[:, 0:LK], T.wk[:, u - 1, :], cT[r % 4][:], start=True, stop=True)\
                      .then_inc(k_ready, 1)
                elif u in (3, 4):
                    for c in ((0, 1) if u == 3 else (2,)):
                        k0, n = KCH[c]
                        last = pe.matmul(bank[0:n, (c % 2) * D:(c % 2 + 1) * D], cT[(r + 2) % 4][:, k0:k0 + n], T.wv[:],
                                         start=True, stop=True)
                    last.then_inc(v_ready, 1)
                elif u in (5, 6):
                    pe.wait_ge(o_copied, count(i, r, 0, 2, u - 4))
                    for k in range(4):
                        last = pe.transpose(bank[0:LQ, k * 128:(k + 1) * 128], O[:, u - 5, k * LQ:(k + 1) * LQ],
                                            T.ident[:])
                    last.then_inc(ot_ready, 1)
                elif u == 8:
                    pe.wait_ge(m_split, count(i, r, 2, 1, 1))
                    pe.transpose(bank[0:2 * H, 0:LQ // 2].bitcast(BF16), mm[:].rearrange("p a h -> p (a h)"),
                                 T.identb[0:LQ, 0:LQ]).then_inc(mt_ready, 1)
                elif u == 9:
                    pe.wait_ge(ot_used, count(i, r, 0, 2, 2))
                    for k in range(2):
                        last = pe.transpose(bank[:, k * LQ:(k + 1) * LQ], cc[r % 2][:, k * 128:(k + 1) * 128],
                                            T.ident[0:LQ, 0:LQ])
                    last.then_inc(cct_ready, 1)
                elif u == 10:
                    pe.wait_ge(cct_copied, count(i, r, 0, 1, 1))
                    for k in range(2):
                        last = pe.matmul(bank[0:LQ, 0:D], ccT[:, k * LQ:(k + 1) * LQ], T.wo[:, k, :], start=(k == 0),
                                         stop=(k == 1))
                    last.then_inc(wo_ready, 1)
                else:
                    pe.wait_ge(xt_copied, count(i, r, -1, 1, 1))
                    for k in range(2):
                        last = pe.matmul(bank[0:LQ, 0:NE], x2T[:, k * LQ:(k + 1) * LQ], T.wg[:, k, :], start=(k == 0),
                                         stop=(k == 1))
                    last.then_inc(lg_ready, 1)

            def step(i, r, live):
                for u in range(12):
                    quad, c = divmod(u, 3)
                    if live(1):
                        if u == 0:
                            pe.wait_ge(mrow_loaded[(r + 1) % 2], fills(i, r, 1, 2, 16, 16))
                        wait(pe, exp_done, count(i, r, 1, 12, u - 1))
                        cols = slice((r + 1) % 4 * LQ, ((r + 1) % 4 + 1) * LQ)
                        for j in range(4):
                            h = 4 * quad + j
                            last = pe.matmul(pT[u % 2][:, j * LQ:(j + 1) * LQ],
                                             kst[(r + 1) % 4][:, h, c * 128:(c + 1) * 128], qst[:, h, cols],
                                             start=True, stop=True)
                        last.then_inc(t_ready, 1)
                    off, heads = (2, [h + 8 for h in S_HEADS[u]]) if u < 6 else (3, S_HEADS[u - 6])
                    if live(off):
                        if u == 6:
                            pe.wait_ge(kst_loaded[(r + 3) % 4], fills(i, r, 3, 4, 96, 96))
                            pe.wait_ge(qst_loaded[(r + 3) % 4 // 2], fills(i, r, 3, 4, 96, 96))
                        cols = slice((r + off) % 4 * LQ, ((r + off) % 4 + 1) * LQ)
                        for h in heads:
                            wait(pe, s_used, count(i, r, off, H, h - 1))
                            pe.matmul(pS[h % 2][0:LQ, 0:LK], qst[0:ROWS, h, cols], kst[(r + off) % 4][0:ROWS, h, 0:LK],
                                      start=True, stop=True).then_inc(s_ready, 1)
                    q2, b2 = (quad - 1, 1) if quad else (3, 0)
                    if live(b2):
                        pe.wait_ge(exp_done, count(i, r, b2, 12, 3 * q2 + c + 1))
                        if q2 == 0 and c == 0:
                            pe.wait_ge(v_copied, count(i, r, b2, 2, 2))
                        if q2 % 2 == 0 and c == 0:
                            wait(pe, o_copied, count(i, r, b2, 2, -1 + q2 // 2))
                        n = KCH[c][1]
                        for jt in range(2):
                            last = pe.matmul(pO[q2 // 2][64 * jt:64 * jt + VW, q2 % 2 * 2 * LQ:(q2 % 2 + 1) * 2 * LQ],
                                             V[(r + b2) % 2][0:n, c, 2 * q2 + jt, :],
                                             P[q2 % 2][0:n, c, jt * 2 * LQ:(jt + 1) * 2 * LQ],
                                             start=(c == 0), stop=(c == 2), skip_group_check=True)
                        if q2 % 2 == 1 and c == 2:
                            last.then_inc(o_ready, 1)
                    if live(PIECES[u][1]):
                        bank_free(i, r, u, live)
                        piece(i, r, u, pM[u % 2])

            run(pe, step)


class Tiles:
    pass


def constants(nc, T, ctx, Wq, bq, Wk, bk, Wv, bv, Wo, bo, Wg, g_xattn, g_ffn):
    def sb(name, shape, dt=F32):
        return ctx.enter_context(nc.sbuf_tensor(name, shape, dt))

    T.ident, T.identb = sb("ident", [128, 128]), sb("identb", [128, 128], BF16)
    T.wq, T.wk, T.wv = sb("wq", [128, 2, 2, 128]), sb("wk", [128, 2, 128]), sb("wv", [128, D])
    T.wo, T.wg = sb("wo", [128, 2, D]), sb("wg", [128, 2, NE])
    T.bq, T.bk, T.bv, T.bo = sb("bq", [128, 2]), sb("bk", [128, 2]), sb("bv", [128, D]), sb("bo", [LQ, D])
    T.gx, T.gf = sb("gx", [128, 1]), sb("gf", [128, 1])
    with ExitStack() as own:
        sem = Sems(nc, own, "c")
        wq_raw = own.enter_context(nc.sbuf_tensor("wq_raw", [128, 2, D], F32))
        wk_raw = own.enter_context(nc.sbuf_tensor("wk_raw", [128, D], F32))
        bq_raw = own.enter_context(nc.sbuf_tensor("bq_raw", [128, 2], F32))
        g_raw = own.enter_context(nc.sbuf_tensor("g_raw", [128, 2], F32))
        loaded, bq_loaded, zeroed = sem("loaded"), sem("bq_loaded"), sem("zeroed")
        block = own.enter_context(nc.Block())

        @block.sync
        def _(sp):
            sp.dma_start(wq_raw[:], Wq.rearrange("(k p) n -> p k n", p=128)).then_inc(loaded, 16)
            sp.dma_start(wk_raw[:], Wk).then_inc(loaded, 16)
            sp.dma_start(T.wv[:], Wv).then_inc(loaded, 16)
            sp.dma_start(T.wo[:], Wo.rearrange("(k p) n -> p k n", p=128)).then_inc(loaded, 16)
            sp.dma_start(T.wg[:], Wg.rearrange("(k p) n -> p k n", p=128)).then_inc(loaded, 16)
            sp.wait_ge(loaded, 8 * 16 + 2 * 16)

        @block.scalar
        def _(act):
            act.dma_start(bq_raw[:], bq.rearrange("(h t d) -> d h t", h=8, t=2),
                          allow_slow_non_contiguous=True).then_inc(bq_loaded, 16)
            act.dma_start(T.bk[:], bk.rearrange("(h t d) -> d h t", h=8, t=2),
                          allow_slow_non_contiguous=True).then_inc(loaded, 16)
            act.dma_start(T.bv[:], bv.partition_broadcast(128)).then_inc(loaded, 16)
            act.dma_start(T.bo[:], bo.partition_broadcast(LQ)).then_inc(loaded, 16)
            act.dma_start(g_raw[:, 0:1], g_xattn.partition_broadcast(128)).then_inc(loaded, 16)
            act.dma_start(g_raw[:, 1:2], g_ffn.partition_broadcast(128)).then_inc(loaded, 16)
            act.wait_ge(bq_loaded, 16)
            act.activation(T.bq[:], bq_raw[:], ACT.Copy, scale=float(DK) ** -0.5)
            act.wait_ge(loaded, 10 * 16)
            act.activation(T.gx[:], g_raw[:, 0:1], ACT.Tanh)
            act.activation(T.gf[:], g_raw[:, 1:2], ACT.Tanh)

        @block.gpsimd
        def _(pool):
            for m in (T.ident, T.identb):
                pool.memset(m[:], 0.0).then_inc(zeroed, 1)
            pool.wait_ge(zeroed, 2)
            for m in (T.ident, T.identb):
                pool.affine_select(out=m[:], in_=m[:], compare_op=ALU.not_equal, fill=1.0, base=0,
                                   pattern=[[-1, 128]], channel_multiplier=1)

        @block.vector
        def _(dve):
            dve.wait_ge(loaded, 10 * 16)
            for k in range(2):
                dve.tensor_copy(T.wq[:, k].rearrange("p t (d h) -> p t d h", h=8),
                                wq_raw[:, k].rearrange("p (h t d) -> p t d h", h=8, t=2))
            dve.tensor_copy(T.wk[:].rearrange("p t (d h) -> p t d h", h=8),
                            wk_raw[:].rearrange("p (h t d) -> p t d h", h=8, t=2))


def routing(nc, T):
    NG, EB = CAP // 128, NE * B
    HALF = EB // 2
    BIG = 4096.0
    with ExitStack() as ctx:
        sem = Sems(nc, ctx, "r")

        def sb(name, shape, dt=F32):
            return ctx.enter_context(nc.sbuf_tensor("r_" + name, shape, dt))

        def banks(name, n=2):
            return [ctx.enter_context(nc.psum_tensor(f"r_{name}{i}", [128, 512], F32)) for i in range(n)]

        en = sb("en", [LQ, EB])
        S = sb("S", [LQ, EB])
        S1, S2, S3 = (sb(f"S{i}", [LQ, EB], BF16) for i in (1, 2, 3))
        Sr = sb("Sr", [LQ, EB])
        ST = sb("ST", [128, 2, LQ])
        junk = sb("junk", [128, 2, LQ])
        cand, e2, z, dz, ok = (sb(n, [128, 2]) for n in ("cand", "e2", "z", "dz", "ok"))
        cnt, ceq, row = (sb(n, [128, 2], BF16) for n in ("cnt", "ceq", "row"))
        need, off = sb("need", [128, 2]), sb("off", [128, 2])
        gt, eq, cum, sel, ones = (sb(n, [128, 2, LQ]) for n in ("gt", "eq", "cum", "sel", "ones"))
        same, below = sb("same", [128, 128], BF16), sb("below", [128, 128], BF16)
        pi, hi_i, lo_i = (sb(n, [LQ, EB], I32) for n in ("pi", "hi_i", "lo_i"))
        hi, lo = sb("hi", [LQ, EB]), sb("lo", [LQ, EB])
        iota_b, iota_g, iota_p, iota_l = (sb("iota_b", [LQ, B]), sb("iota_g", [LQ, NG]), sb("iota_p", [LQ, 1]),
                                          sb("iota_l", [LQ, 128], BF16))
        A = sb("A", [LQ, EB, 5, NG], BF16)
        hot = sb("hot", [LQ, EB, NG], BF16)
        L = [sb(f"L{i}", [LQ, B, 128], BF16) for i in range(2)]
        rt = sb("rt", [128, NE, 5, NG])
        pT, pC, pP, pR = banks("pT", 1)[0], banks("pC", 1)[0], banks("pP", 1)[0], banks("pR", 1)[0]
        v, pe_done, act_done, consts = sem("v"), sem("pe_done"), sem("act_done"), sem("consts")
        counted, summed, l_ready, l_used = sem("counted"), sem("summed"), sem("l_ready"), sem("l_used")
        block = ctx.enter_context(nc.Block())
        MANT = 23

        @block.gpsimd
        def _(pool):
            def then(ins):
                ins.then_inc(consts, 1)
                then.n += 1
                pool.wait_ge(consts, then.n)
            then.n = 0

            then(pool.iota(iota_b[:], pattern=[[1, B]], base=0, channel_multiplier=0, allow_small_or_imprecise_dtypes=True))
            then(pool.iota(iota_g[:], pattern=[[1, NG]], base=0, channel_multiplier=0, allow_small_or_imprecise_dtypes=True))
            then(pool.iota(iota_p[:], pattern=[[0, 1]], base=0, channel_multiplier=1, allow_small_or_imprecise_dtypes=True))
            then(pool.iota(iota_l[:], pattern=[[1, 128]], base=0, channel_multiplier=0, allow_small_or_imprecise_dtypes=True))
            then(pool.memset(ones[:], 1.0))
            then(pool.memset(same[:], 1.0))
            blocks = same[:].rearrange("p (e b) -> p e b", b=B)
            then(pool.affine_select(out=blocks, in_=blocks, compare_op=ALU.is_ge, fill=0.0, base=0,
                                    pattern=[[-B, 128 // B], [0, B]], channel_multiplier=1))
            then(pool.affine_select(out=blocks, in_=blocks, compare_op=ALU.is_ge, fill=0.0, base=B - 1,
                                    pattern=[[B, 128 // B], [0, B]], channel_multiplier=-1))
            then(pool.affine_select(out=below[:], in_=same[:], compare_op=ALU.is_ge, fill=0.0, base=-1,
                                    pattern=[[1, 128]], channel_multiplier=-1))

        @block.scalar
        def _(act):
            act.wait_ge(v, 1)
            act.activation(en[:].rearrange("p (e b) -> p e b", e=NE), en[:].rearrange("p (e b) -> p e b", e=NE), ACT.Exp, scale=-1.0)\
               .then_inc(act_done, 1)

        @block.tensor
        def _(pe):
            pe.wait_ge(v, 4)
            for h in range(2):
                last = pe.transpose(pT[:, h * LQ:(h + 1) * LQ], Sr[:, h * HALF:(h + 1) * HALF], T.ident[0:LQ, 0:LQ])
            last.then_inc(pe_done, 1)
            pe.wait_ge(consts, 9)

            def total(k):
                pe.wait_ge(counted, k)
                pe.matmul(pC[:, 0:2], same[:], cnt[:], start=True, stop=True).then_inc(summed, 1)

            for k in range(7):
                total(k + 1)
            with pe.Fori(0, MANT) as i:
                total(i + 8)
            pe.wait_ge(counted, 31)
            pe.matmul(pC[:, 0:2], same[:], cnt[:], start=True, stop=True)
            pe.matmul(pC[:, 2:4], below[:], ceq[:], start=True, stop=True).then_inc(summed, 1)
            pe.wait_ge(counted, 32)
            pe.matmul(pC[:, 4:6], below[:], row[:], start=True, stop=True).then_inc(summed, 1)
            pe.wait_ge(counted, 33)
            for h in range(2):
                last = pe.transpose(pP[0:LQ, h * HALF:(h + 1) * HALF], sel[:, h, :], T.ident[:])
            last.then_inc(summed, 1)
            for e in range(NE):
                pe.wait_ge(l_ready, e + 1)
                for b in range(B):
                    last = pe.matmul(pR[:, e * 35:(e + 1) * 35], L[e % 2][:, b, :],
                                     A[:, e * B + b].rearrange("p c g -> p (c g)"), start=(b == 0), stop=(b == B - 1))
                last.then_inc(l_used, 1)

        @block.vector
        def _(dve):
            n = [0]

            def link(ins):
                n[0] += 1
                ins.then_inc(v, 1)
                dve.wait_ge(v, n[0])

            link(dve.tensor_scalar(en[:].rearrange("p (e b) -> p e b", e=NE), T.lg[:].rearrange("p (b e) -> p e b", e=NE),
                                   -87.0, None, ALU.max))
            dve.wait_ge(act_done, 1)
            link(dve.tensor_scalar(en[:], en[:], 1.0, None, ALU.add))
            link(dve.reciprocal(S[:], en[:]))
            link(dve.tensor_scalar(Sr[:], S[:], 2.0 ** -126, None, ALU.max))
            link(dve.tensor_copy(S1[:], S[:]))
            link(dve.tensor_tensor(S[:], S[:], S1[:], ALU.subtract))
            link(dve.tensor_copy(S2[:], S[:]))
            link(dve.tensor_tensor(S3[:], S[:], S2[:], ALU.subtract))
            dve.wait_ge(pe_done, 1)
            link(dve.tensor_copy(ST[:].rearrange("p h t -> p (h t)"), pT[:, 0:2 * LQ]))
            link(dve.memset(cand[:], 2.0 ** -62))

            def counts():
                for h in range(2):
                    ins = dve.tensor_scalar(junk[:, h], ST[:, h], cand[:, h:h + 1], None, ALU.is_ge, ALU.add,
                                            accum_out=cnt[:, h:h + 1])
                return ins

            for k in range(7):
                bit = 64 >> k
                nxt = bit // 2
                counts().then_inc(counted, 1)
                if nxt:
                    link(dve.tensor_scalar(z[:], cand[:], 2.0 ** (nxt - bit), None, ALU.mult))
                    link(dve.scalar_tensor_tensor(dz[:], cand[:], 2.0 ** nxt, z[:], ALU.mult, ALU.subtract))
                else:
                    link(dve.tensor_scalar(z[:], cand[:], 0.5, None, ALU.mult))
                    link(dve.tensor_tensor(dz[:], cand[:], z[:], ALU.subtract))
                dve.wait_ge(summed, k + 1)
                link(dve.scalar_tensor_tensor(ok[:], pC[:, 0:2], float(CAP), dz[:], ALU.is_ge, ALU.mult))
                link(dve.tensor_tensor(cand[:], ok[:], z[:], ALU.add))
            link(dve.tensor_scalar(e2[:], cand[:], 0.5, None, ALU.mult))
            link(dve.tensor_tensor(cand[:], cand[:], e2[:], ALU.add))
            base = n[0]
            with dve.Fori(0, MANT) as i:
                counts().then_inc(counted, 1)

                def step(ins, k):
                    ins.then_inc(v, 1)
                    dve.wait_ge(v, i * 5 + (base + k))

                step(dve.scalar_tensor_tensor(z[:], e2[:], -0.5, cand[:], ALU.mult, ALU.add), 1)
                step(dve.tensor_scalar(dz[:], e2[:], 1.0, None, ALU.mult), 2)
                step(dve.tensor_scalar(e2[:], e2[:], 0.5, None, ALU.mult), 3)
                dve.wait_ge(summed, i + 8)
                step(dve.scalar_tensor_tensor(ok[:], pC[:, 0:2], float(CAP), dz[:], ALU.is_ge, ALU.mult), 4)
                step(dve.tensor_tensor(cand[:], ok[:], z[:], ALU.add), 5)
            n[0] = base + 5 * MANT
            link(dve.tensor_tensor(cand[:], cand[:], e2[:], ALU.subtract))
            for h in range(2):
                dve.tensor_scalar(gt[:, h], ST[:, h], cand[:, h:h + 1], None, ALU.is_gt, ALU.add, accum_out=cnt[:, h:h + 1])
                ins = dve.tensor_scalar(eq[:, h], ST[:, h], cand[:, h:h + 1], None, ALU.is_equal, ALU.add,
                                        accum_out=ceq[:, h:h + 1])
            ins.then_inc(counted, 1)
            dve.wait_ge(counted, 31)
            for h in range(2):
                ins = dve.tensor_tensor_scan(cum[:, h], ones[:, h], eq[:, h], 0.0, ALU.mult, ALU.add)
            link(ins)
            dve.wait_ge(summed, 31)
            link(dve.tensor_scalar(need[:], pC[:, 0:2], -1.0, float(CAP), ALU.mult, ALU.add))
            link(dve.tensor_copy(off[:], pC[:, 2:4]))
            for h in range(2):
                ins = dve.tensor_scalar(cum[:, h], cum[:, h], off[:, h:h + 1], need[:, h:h + 1], ALU.add, ALU.is_le)
            link(ins)
            link(dve.tensor_tensor(cum[:], cum[:], eq[:], ALU.mult))
            link(dve.tensor_tensor(sel[:], cum[:], gt[:], ALU.add))
            for h in range(2):
                ins = dve.tensor_tensor_scan(cum[:, h], ones[:, h], sel[:, h], 0.0, ALU.mult, ALU.add)
            link(ins)
            dve.tensor_copy(row[:], cum[:, :, LQ - 1]).then_inc(counted, 1)
            dve.wait_ge(summed, 32)
            link(dve.tensor_scalar(off[:], pC[:, 4:6], -(BIG + 1.0), None, ALU.add))
            for h in range(2):
                ins = dve.scalar_tensor_tensor(sel[:, h], cum[:, h], off[:, h:h + 1], sel[:, h], ALU.add, ALU.mult)
            link(ins)
            dve.tensor_scalar(sel[:], sel[:], BIG, None, ALU.add).then_inc(counted, 1)
            dve.wait_ge(summed, 33)
            link(dve.tensor_copy(pi[:], pP[0:LQ, 0:EB]))
            link(dve.tensor_scalar(hi_i[:], pi[:], 7, None, ALU.logical_shift_right))
            link(dve.tensor_scalar(lo_i[:], pi[:], 127, None, ALU.bitwise_and))
            link(dve.tensor_copy(hi[:], hi_i[:]))
            link(dve.tensor_copy(lo[:], lo_i[:]))

            def wide(ap):
                return ap.unsqueeze(2).to_broadcast([LQ, EB, NG])

            dve.wait_ge(consts, 9)
            link(dve.tensor_tensor(hot[:], wide(hi[:]), iota_g[:].unsqueeze(1).to_broadcast([LQ, EB, NG]), ALU.is_equal))
            link(dve.tensor_tensor(A[:, :, 1, :], hot[:], wide(S1[:]), ALU.mult))
            for e in range(NE):
                ins = dve.tensor_tensor(A[:, e * B:(e + 1) * B, 0, :], hot[:, e * B:(e + 1) * B],
                                        iota_b[:].unsqueeze(2).to_broadcast([LQ, B, NG]), ALU.mult)
            link(ins)
            link(dve.tensor_tensor(A[:, :, 2, :], hot[:], wide(S2[:]), ALU.mult))
            link(dve.tensor_tensor(A[:, :, 3, :], hot[:], wide(S3[:]), ALU.mult))
            link(dve.tensor_scalar(A[:, :, 4, :], hot[:], iota_p[:], None, ALU.mult))
            for e in range(NE):
                if e >= 2:
                    dve.wait_ge(l_used, e - 1)
                for b in range(B):
                    ins = dve.tensor_scalar(L[e % 2][:, b, :], iota_l[:], lo[:, e * B + b:e * B + b + 1], None, ALU.is_equal)
                ins.then_inc(l_ready, 1)
            dve.wait_ge(l_used, NE)
            link(dve.tensor_copy(rt[:].rearrange("p e c g -> p (e c g)"), pR[:, 0:NE * 35]))
            link(dve.scalar_tensor_tensor(T.idx[:], rt[:, :, 0, :], float(LQ), rt[:, :, 4, :], ALU.mult, ALU.add))
            link(dve.tensor_tensor(T.gate[:], rt[:, :, 1, :], rt[:, :, 2, :], ALU.add))
            link(dve.tensor_tensor(T.gate[:], T.gate[:], rt[:, :, 3, :], ALU.add))
            link(dve.tensor_scalar(T.gate[:], T.gate[:], T.gf[:], None, ALU.mult))


def experts(nc, T, xn, W1, b1, W2, b2, out):
    NG = CAP // 128
    CHUNK = [(0, 4), (4, NG)]
    with ExitStack() as ctx:
        sem = Sems(nc, ctx, "e")

        def sb(name, shape, dt=F32):
            return ctx.enter_context(nc.sbuf_tensor("e_" + name, shape, dt))

        def banks(name, n=2):
            return [ctx.enter_context(nc.psum_tensor(f"e_{name}{i}", [128, 512], F32)) for i in range(n)]

        w1, w2 = sb("w1", [128, 2, FF]), sb("w2", [128, 8, D])
        w1h, w1l = ([sb(f"w1{p}{i}", [128, 2, FF], F32R) for i in range(2)] for p in "hl")
        w2h, w2l = ([sb(f"w2{p}{i}", [128, 8, D], F32R) for i in range(2)] for p in "hl")
        b1raw, b1s = sb("b1raw", [64, 128]), sb("b1s", [128, 64])
        b1s_of = [sb(f"b1e{i}", [128, 8]) for i in range(2)]
        b2s = [sb(f"b2s{i}", [128, D]) for i in range(2)]
        idx, gate = [sb(f"idx{i}", [128, NG], I32) for i in range(2)], [sb(f"gate{i}", [128, NG]) for i in range(2)]
        ex = sb("ex", [128, NG, D])
        exh, exl = sb("exh", [128, 2, CAP], F32R), sb("exl", [128, 2, CAP], F32R)
        hid = [sb(f"hid{i}", [128, 512]) for i in range(2)]
        hh, hl = sb("hh", [128, 8, CAP], F32R), sb("hl", [128, 8, CAP], F32R)
        y = [sb(f"y{i}", [128, D]) for i in range(NG)]
        p1, p2, pT = banks("p1"), banks("p2"), banks("pT")
        w_loaded, w_high, w_low = sem("w_loaded"), sem("w_high"), sem("w_low")
        b1_loaded, b1_t, b1_c, b1_e = sem("b1_loaded"), sem("b1_t"), sem("b1_c"), sem("b1_e")
        b2_loaded = [sem("b2_loaded0"), sem("b2_loaded1")]
        idx_ready, gathered, added = sem("idx_ready"), sem("gathered"), sem("added")
        xt_ready, xh_done, xl_done = sem("xt_ready"), sem("xh_done"), sem("xl_done")
        h_ready, gelu_done, hh_done, hl_done = sem("h_ready"), sem("gelu_done"), sem("hh_done"), sem("hl_done")
        y_ready, y_read, y_done, passed = sem("y_ready"), sem("y_read"), sem("y_done"), sem("passed")
        block = ctx.enter_context(nc.Block())

        def run(eng, step):
            def static(s):
                step(s // 2, s % 2, lambda off: 0 <= s + off < NE)

            static(-1)
            static(0)
            with eng.Fori(0, (NE - 2) // 2) as i:
                for r in (1, 2):
                    step(i, r, lambda off: True)
            static(NE - 1)

        def count(i, r, off, per, add):
            return i * (2 * per) + ((r + off) * per + add)

        def fills(i, r, off, per, add=0):
            return i * per + ((r + off) // 2 * per + add)

        @block.sync
        def _(sp):
            sp.dma_start(b1raw[:], b1.rearrange("e (c p) -> (e c) p", p=128)).then_inc(b1_loaded, 16)

            def step(i, r, live):
                if live(1):
                    wait_alone(sp, w_high, count(i, r, 0, 4, 4), passed)
                    wait_alone(sp, w_low, count(i, r, 0, 4, 4), passed)
                    e1, e2 = bass.ds(count(i, r, 1, D, 0), D), bass.ds(count(i, r, 1, FF, 0), FF)
                    sp.dma_start(w1[:], W1.rearrange("e p f -> (e p) f")[e1].rearrange("(k p) f -> p k f", k=2))\
                      .then_inc(w_loaded, 16)
                    sp.dma_start(w2[:], W2.rearrange("e f d -> (e f) d")[e2].rearrange("(k p) d -> p k d", k=8))\
                      .then_inc(w_loaded, 16)
                    wait_alone(sp, y_read, count(i, r, -1, NG, NG), passed)
                    sp.dma_start(b2s[(r + 1) % 2][:], b2[bass.ds(count(i, r, 1, 1, 0), 1)].rearrange("a d -> (a d)")
                                 .partition_broadcast(128)).then_inc(b2_loaded[(r + 1) % 2], 16)

            run(sp, step)

        @block.gpsimd
        def _(pool):
            def step(i, r, live):
                if live(1):
                    p = (r + 1) % 2
                    wait_alone(pool, y_done, count(i, r, -1, NG, NG), passed)
                    wait_alone(pool, added, count(i, r, -1, 16 * NG, 16 * NG), passed)
                    e7 = bass.ds(count(i, r, 1, NG, 0), NG)
                    pool.tensor_copy(idx[p][:], T.idx[:].rearrange("p e g -> p (e g)")[:, e7]).then_inc(idx_ready, 1)
                    pool.tensor_copy(gate[p][:], T.gate[:].rearrange("p e g -> p (e g)")[:, e7]).then_inc(idx_ready, 1)
                    wait_alone(pool, idx_ready, count(i, r, 1, 2, 2), passed)
                    wait_alone(pool, xt_ready, count(i, r, 0, 4, 4), passed)
                    for g in range(NG):
                        pool.indirect_dma_start(out=ex[:, g, :], out_offset=None, in_=xn,
                                                in_offset=bass.IndirectOffsetOnAxis(ap=idx[p][:, g:g + 1], axis=0))\
                            .then_inc(gathered, 16)
                    for k in range(4):
                        src, h, l = ((w1, w1h[p], w1l[p]) if k < 2 else (w2, w2h[p], w2l[p]))
                        part = (slice(None), k) if k < 2 else (slice(None), slice(4 * (k - 2), 4 * (k - 1)))
                        wait_alone(pool, w_high, count(i, r, 1, 4, k + 1), passed)
                        pool.tensor_tensor(l[part], src[part], h[part].bitcast(F32), ALU.subtract).then_inc(w_low, 1)
                if live(0):
                    for g in range(NG):
                        wait_alone(pool, y_read, count(i, r, 0, NG, g + 1), passed)
                        pool.tensor_scalar(y[g][:], y[g][:], gate[r % 2][:, g:g + 1], None, ALU.mult).then_inc(y_done, 1)
                    wait_alone(pool, added, count(i, r, -1, 16 * NG, 16 * NG), passed)
                    for g in range(NG):
                        wait_alone(pool, y_done, count(i, r, 0, NG, g + 1), passed)
                        pool.indirect_dma_start(out=out, out_offset=bass.IndirectOffsetOnAxis(ap=idx[r % 2][:, g:g + 1], axis=0),
                                                in_=y[g][:], in_offset=None, compute_op=ALU.add).then_inc(added, 16)

            run(pool, step)
            pool.wait_ge(added, NE * NG * 16)

        @block.scalar
        def _(act):
            act.wait_ge(b1_t, 1)
            act.activation(b1s[:], pT[0][:, 0:64], ACT.Copy).then_inc(b1_c, 1)
            act.wait_ge(b1_c, 1)

            def step(i, r, live):
                if live(0):
                    b1e = b1s_of[r % 2]
                    act.activation(b1e[:], b1s[:, bass.ds(count(i, r, 0, 8, 0), 8)], ACT.Copy).then_inc(b1_e, 1)
                    act.wait_ge(b1_e, count(i, r, 0, 1, 1))
                    for c, (g0, g1) in enumerate(CHUNK):
                        n = (g1 - g0) * 128
                        for f in range(8):
                            k = 8 * c + f
                            act.wait_ge(h_ready, count(i, r, 0, 16, k + 1))
                            if k >= 2:
                                act.wait_ge(hl_done, count(i, r, 0, 16, k - 1))
                            act.activation(hid[f % 2][:, 0:n], p1[f % 2][:, 0:n], ACT.Gelu, bias=b1e[:, f:f + 1])\
                               .then_inc(gelu_done, 1)
                if live(1):
                    p = (r + 1) % 2
                    act.wait_ge(w_loaded, count(i, r, 1, 32, 32))
                    for k in range(4):
                        src, h = ((w1, w1h[p]) if k < 2 else (w2, w2h[p]))
                        part = (slice(None), k) if k < 2 else (slice(None), slice(4 * (k - 2), 4 * (k - 1)))
                        act.activation(h[part], src[part], ACT.Copy).then_inc(w_high, 1)
                    for k in range(4):
                        c, kk = divmod(k, 2)
                        g0, g1 = CHUNK[c]
                        act.wait_ge(xt_ready, count(i, r, 1, 4, k + 1))
                        act.activation(exh[:, kk, g0 * 128:g1 * 128], pT[kk][:, 0:(g1 - g0) * 128], ACT.Copy)\
                           .then_inc(xh_done, 1)

            run(act, step)

        @block.vector
        def _(dve):
            def step(i, r, live):
                if live(0):
                    for c, (g0, g1) in enumerate(CHUNK):
                        n = (g1 - g0) * 128
                        for f in range(8):
                            k, cols = 8 * c + f, slice(g0 * 128, g1 * 128)
                            dve.wait_ge(gelu_done, count(i, r, 0, 16, k + 1))
                            dve.tensor_copy(hh[:, f, cols], hid[f % 2][:, 0:n]).then_inc(hh_done, 1)
                            dve.wait_ge(hh_done, count(i, r, 0, 16, k + 1))
                            dve.tensor_tensor(hl[:, f, cols], hid[f % 2][:, 0:n], hh[:, f, cols].bitcast(F32),
                                              ALU.subtract).then_inc(hl_done, 1)
                    dve.wait_ge(b2_loaded[r % 2], fills(i, r, 0, 16, 16))

                    def results(g0, g1):
                        for g in range(g0, g1):
                            dve.wait_ge(y_ready, count(i, r, 0, NG, g + 1))
                            wait(dve, added, count(i, r, -1, 16 * NG, 16 * NG))
                            dve.tensor_tensor(y[g][:], p2[g % 2][:, 0:D], b2s[r % 2][:], ALU.add).then_inc(y_read, 1)

                    results(0, 4)
                if live(1):
                    for k in range(4):
                        c, kk = divmod(k, 2)
                        g0, g1 = CHUNK[c]
                        dve.wait_ge(xh_done, count(i, r, 1, 4, k + 1))
                        dve.tensor_tensor(exl[:, kk, g0 * 128:g1 * 128], pT[kk][:, 0:(g1 - g0) * 128],
                                          exh[:, kk, g0 * 128:g1 * 128].bitcast(F32), ALU.subtract).then_inc(xl_done, 1)
                if live(0):
                    results(4, NG)

            run(dve, step)

        @block.tensor
        def _(pe):
            pe.wait_ge(b1_loaded, 16)
            pe.transpose(pT[0][:, 0:64], b1raw[:], T.ident[0:64, 0:64]).then_inc(b1_t, 1)
            pe.wait_ge(b1_c, 1)

            def step(i, r, live):
                if live(0):
                    wh, wl, p = w1h[r % 2], w1l[r % 2], r % 2
                    pe.wait_ge(w_low, count(i, r, 0, 4, 4))
                    for c, (g0, g1) in enumerate(CHUNK):
                        n, cols = (g1 - g0) * 128, slice(g0 * 128, g1 * 128)
                        pe.wait_ge(xl_done, count(i, r, 0, 4, 2 * c + 2))
                        for f in range(8):
                            if 8 * c + f >= 2:
                                pe.wait_ge(gelu_done, count(i, r, 0, 16, 8 * c + f - 1))
                            fs, j = slice(f * 128, (f + 1) * 128), 0
                            for k in range(2):
                                for w, v in ((wh, exh), (wh, exl), (wl, exh)):
                                    last = pe.matmul(p1[f % 2][:, 0:n], w[:, k, fs], v[:, k, cols], start=(j == 0), stop=(j == 5))
                                    j += 1
                            last.then_inc(h_ready, 1)

                def second(g0, g1):
                    for g in range(g0, g1):
                        if g in (0, 4):
                            pe.wait_ge(hl_done, count(i, r, 0, 16, 8 if g == 0 else 16))
                        wait(pe, y_read, count(i, r, 0, NG, g - 1))
                        j, rows = 0, slice(g * 128, (g + 1) * 128)
                        for f in range(8):
                            for v, w in ((hh, w2h[r % 2]), (hh, w2l[r % 2]), (hl, w2h[r % 2])):
                                last = pe.matmul(p2[g % 2][:, 0:D], v[:, f, rows], w[:, f, :], start=(j == 0), stop=(j == 23))
                                j += 1
                        last.then_inc(y_ready, 1)

                if live(0):
                    second(0, 4)
                if live(1):
                    pe.wait_ge(gathered, count(i, r, 1, 16 * NG, 16 * NG))
                    for k in range(4):
                        c, kk = divmod(k, 2)
                        wait(pe, xl_done, count(i, r, 1, 4, k - 1))
                        for g in range(*CHUNK[c]):
                            last = pe.transpose(pT[kk][:, (g - CHUNK[c][0]) * 128:(g - CHUNK[c][0] + 1) * 128],
                                                ex[:, g, kk * 128:(kk + 1) * 128], T.ident[:])
                        last.then_inc(xt_ready, 1)
                if live(0):
                    second(4, NG)

            run(pe, step)


def flamingo_gated_layer(nc, x, ctx_512, g_xattn, g_ffn, Wq, bq, Wk, bk, Wv, bv, Wo, bo, Wg, W1, b1, W2, b2, out):
    T = Tiles()
    x, out = x.rearrange("b p d -> (b p) d"), out.rearrange("b p d -> (b p) d")
    xn = nc.dram_tensor("xn_scratch", [TOK, D], F32, kind="Internal").ap()
    with ExitStack() as ctx:
        constants(nc, T, ctx, Wq, bq, Wk, bk, Wv, bv, Wo, bo, Wg, g_xattn, g_ffn)
        T.lg = ctx.enter_context(nc.sbuf_tensor("lg", [LQ, B * NE], F32))
        T.idx = ctx.enter_context(nc.sbuf_tensor("idx", [128, NE, CAP // 128], I32))
        T.gate = ctx.enter_context(nc.sbuf_tensor("gate", [128, NE, CAP // 128], F32))
        with ExitStack() as own:
            T.qp = own.enter_context(nc.sbuf_tensor("qp", [128, 3, 2, TOK], BF16))
            queries(nc, T, x.rearrange("(b p) d -> b p d", p=LQ))
            attention(nc, T, x, ctx_512, out, xn)
        routing(nc, T)
        experts(nc, T, xn, W1, b1, W2, b2, out)


_INS = ['x', 'ctx_512', 'g_xattn', 'g_ffn', 'L0_xattn_Wq', 'L0_xattn_bq', 'L0_xattn_Wk', 'L0_xattn_bk', 'L0_xattn_Wv',
        'L0_xattn_bv', 'L0_xattn_Wo', 'L0_xattn_bo', 'L0_ffn_Wg', 'L0_ffn_W1', 'L0_ffn_b1', 'L0_ffn_W2', 'L0_ffn_b2']
_OUTS = [((B, LQ, D), 'float32')]


def kernel(**inputs):
    import numpy as _np
    import concourse.bacc as _bacc
    from concourse import mybir as _mybir
    from concourse.bass_utils import run_bass_kernel_spmd as _run

    nc = _bacc.Bacc("TRN2", target_bir_lowering=False, num_devices=1)
    arrays, args = {}, []
    for name in _INS:
        a = _np.ascontiguousarray(inputs[name])
        arrays[f"in_{name}_dram"] = a
        args.append(nc.dram_tensor(f"in_{name}_dram", a.shape, _mybir.dt.from_np(a.dtype), kind="ExternalInput").ap())
    for i, (shape, dtype) in enumerate(_OUTS):
        dt = _mybir.dt.from_np(_np.dtype(dtype))
        args.append(nc.dram_tensor(f"out_{i}_dram", shape, dt, kind="ExternalOutput").ap())
    flamingo_gated_layer(nc, *args)
    r = _run(nc, [arrays], core_ids=[0])
    got = tuple(r.results[0][f"out_{i}_dram"] for i in range(len(_OUTS)))
    return got[0]
```

```python
import concourse.bass as bass
from concourse import mybir
from contextlib import ExitStack

F32 = mybir.dt.float32
F32R = mybir.dt.float32r
BF16 = mybir.dt.bfloat16
I32 = mybir.dt.int32
ALU = mybir.AluOpType
ACT = mybir.ActivationFunctionType
AXX = mybir.AxisListType.X

B, LQ, D = 32, 112, 256
LK, C = 375, 128
H, DK = 16, 16
NE, FF = 8, 1024
TOK = B * LQ
CAP = TOK * 2 // NE
EPS = 1e-5

KCH = [(0, 128), (128, 128), (256, LK - 256)]
PAIRED = LK - LK % 2
KPAD = 384
K_SLOT = [0, 0, 0, 1, 1, 2]
Q_SLOT = [0, 1, 2, 0, 1, 0]
ROWS = 16 * len(K_SLOT)
VW = 64


def wait(eng, sem, count):
    if not (isinstance(count, int) and count <= 0):
        eng.wait_ge(sem, count)


def wait_alone(eng, sem, count, passed):
    wait(eng, sem, count)
    if not isinstance(count, int):
        eng.sem_inc(passed, 1)


class Sems:

    def __init__(self, nc, ctx, stage):
        self.nc, self.ctx, self.stage, self.made = nc, ctx, stage, {}

    def __call__(self, name):
        if name not in self.made:
            self.made[name] = self.ctx.enter_context(self.nc.semaphore(f"{self.stage}_{name}"))
        return self.made[name]


def queries(nc, T, x):
    G, NB = B // 4, 4 * LQ
    with ExitStack() as ctx:
        sem = Sems(nc, ctx, "q")

        def sb(name, shape, dt=F32):
            return ctx.enter_context(nc.sbuf_tensor("q_" + name, shape, dt))

        def banks(name, n=2):
            return [ctx.enter_context(nc.psum_tensor(f"q_{name}{i}", [128, 512], F32)) for i in range(n)]

        xin = [sb(f"xin{i}", [LQ, 4, D]) for i in range(2)]
        xn = [sb(f"xn{i}", [LQ, 4, D]) for i in range(2)]
        st = sb("st", [LQ, 4, 6])
        mv = [sb(f"mv{i}", [LQ, 4, 2]) for i in range(2)]
        yt = [sb(f"yt{i}", [LQ, 4]) for i in range(2)]
        std = sb("std", [LQ, 4])
        y0 = sb("y0", [LQ, 4])
        rstd = sb("rstd", [LQ, 4])
        xnT = sb("xnT", [128, 2, NB])
        q32 = [sb(f"q32_{i}", [128, 2, NB]) for i in range(2)]
        pT = banks("pT")
        pQ = banks("pQ")
        x_loaded = [sem("x_loaded0"), sem("x_loaded1")]
        chain, var_ready, std_ready, xn_ready = sem("chain"), sem("var_ready"), sem("std_ready"), sem("xn_ready")
        xt_ready, xt_copied, q_ready, q_copied = sem("xt_ready"), sem("xt_copied"), sem("q_ready"), sem("q_copied")
        q_high, q_rest, q_mid, q_cut = sem("q_high"), sem("q_rest"), sem("q_mid"), sem("q_cut")
        passed, passed_p = sem("passed"), sem("passed_p")
        block = ctx.enter_context(nc.Block())

        def groups(eng, body):
            body(0, 0)
            with eng.Fori(0, G // 2 - 1) as i:
                for r in range(2):
                    body(i * 2 + 1 + r, 1 - r)
            body(G - 1, 1)

        def tokens(g):
            return bass.ds(g * NB, NB)

        @block.sync
        def _(sp):
            def group(g, r):
                wait(sp, xn_ready, g + 1)
                sp.dma_start(xin[r][:], x[bass.ds(g * 4, 4)].rearrange("b p d -> p b d")).then_inc(x_loaded[r], 16)

            groups(sp, group)

        @block.vector
        def _(dve):
            STATS, NORM = 9, 4

            def statistics(g, g16, r):
                dve.wait_ge(x_loaded[r], g16)
                for b in range(4):
                    dve.bn_stats(st[:, b, :], xin[r][:, b, :]).then_inc(chain, 1)
                wait_alone(dve, chain, g * (STATS + NORM) + 4, passed)
                for b in range(4):
                    dve.bn_aggr(mv[r][:, b, :], st[:, b, :]).then_inc(chain, 1)
                wait_alone(dve, chain, g * (STATS + NORM) + 8, passed)
                dve.tensor_scalar(yt[r][:], mv[r][:, :, 1], EPS, None, ALU.add).then_inc(chain, 1)
                wait_alone(dve, chain, g * (STATS + NORM) + 9, passed)
                dve.sem_inc(var_ready, 1)

            def middle(g, r):
                dve.wait_ge(q_rest, g + 1)
                dve.tensor_copy(T.qp[:, 1, :, tokens(g)], q32[r][:]).then_inc(q_mid, 1)

            def group(g, r):
                links = g * (STATS + NORM) + STATS
                dve.wait_ge(std_ready, g + 1)
                dve.reciprocal(y0[:], std[:]).then_inc(chain, 1)
                wait_alone(dve, chain, links + 1, passed)
                dve.tensor_tensor(rstd[:], y0[:], y0[:], ALU.mult).then_inc(chain, 1)
                wait_alone(dve, chain, links + 2, passed)
                dve.scalar_tensor_tensor(rstd[:], rstd[:], -0.5, yt[r][:], ALU.mult, ALU.mult).then_inc(chain, 1)
                wait_alone(dve, chain, links + 3, passed)
                dve.scalar_tensor_tensor(rstd[:], rstd[:], 1.5, y0[:], ALU.add, ALU.mult).then_inc(chain, 1)
                wait_alone(dve, chain, links + 4, passed)
                wait(dve, xt_ready, g + 1)
                for b in range(4):
                    last = dve.tensor_scalar(xn[r][:, b, :], xin[r][:, b, :], mv[r][:, b, 0:1], rstd[:, b:b + 1],
                                             ALU.subtract, ALU.mult)
                last.then_inc(xn_ready, 1)
                if not (isinstance(g, int) and g == G - 1):
                    statistics(g + 1, loads(g, r), 1 - r)
                if not (isinstance(g, int) and g == 0):
                    middle(g - 1, 1 - r)

            def loads(g, r):
                return (g + 2 + r) * 8

            dve.sem_inc(xn_ready, 2)
            statistics(0, 16, 0)
            groups(dve, group)
            middle(G - 1, 1)

        @block.gpsimd
        def _(pool):
            def rest(g, r):
                wait_alone(pool, q_high, g + 1, passed_p)
                pool.tensor_tensor(q32[r][:], q32[r][:], T.qp[:, 0, :, tokens(g)], ALU.subtract).then_inc(q_rest, 1)

            def low(g, r):
                wait_alone(pool, q_mid, g + 1, passed_p)
                pool.tensor_tensor(T.qp[:, 2, :, tokens(g)], q32[r][:], T.qp[:, 1, :, tokens(g)],
                                   ALU.subtract).then_inc(q_cut, 1)

            def group(g, r):
                rest(g, r)
                if not (isinstance(g, int) and g == 0):
                    low(g - 1, 1 - r)

            groups(pool, group)
            low(G - 1, 1)

        @block.scalar
        def _(act):
            def root(g, r):
                act.wait_ge(var_ready, g + 1)
                act.activation(std[:], yt[r][:], ACT.Sqrt).then_inc(std_ready, 1)

            def group(g, r):
                wait(act, xt_ready, g + 3)
                for k in range(2):
                    act.activation(xnT[:, k, :], pT[k][:, 0:NB], ACT.Copy).then_inc(xt_copied, 1)
                if not (isinstance(g, int) and g == G - 1):
                    act.wait_ge(xn_ready, g + 3)
                    root(g + 1, 1 - r)
                wait(act, q_cut, g + 1)
                for t in range(2):
                    act.wait_ge(q_ready, g * 2 + t + 1)
                    act.activation(q32[r][:, t, :], pQ[t][:, 0:NB], ACT.Identity, bias=T.bq[:, t:t + 1],
                                   scale=float(DK) ** -0.5).then_inc(q_copied, 1)
                act.wait_ge(q_copied, g * 2 + 2)
                act.activation(T.qp[:, 0, :, tokens(g)], q32[r][:], ACT.Copy).then_inc(q_high, 1)

            act.sem_inc(q_cut, 2)
            root(0, 0)
            groups(act, group)

        @block.tensor
        def _(pe):
            def transposes(g, r):
                pe.wait_ge(xn_ready, g + 3)
                for k in range(2):
                    for b in range(4):
                        last = pe.transpose(pT[k][:, b * LQ:(b + 1) * LQ], xn[r][:, b, k * 128:(k + 1) * 128],
                                            T.ident[0:LQ, 0:LQ])
                last.then_inc(xt_ready, 1)

            def group(g, r):
                wait(pe, q_copied, g * 2)
                for k in range(2):
                    pe.wait_ge(xt_copied, g * 2 + 1 + k)
                    for t in range(2):
                        last = pe.matmul(pQ[t][:, 0:NB], T.wq[:, k, t, :], xnT[:, k, :], start=(k == 0),
                                         stop=(k == 1))
                        if k == 1:
                            last.then_inc(q_ready, 1)
                if not (isinstance(g, int) and g == G - 1):
                    transposes(g + 1, 1 - r)

            pe.sem_inc(xt_ready, 2)
            transposes(0, 0)
            groups(pe, group)


def attention(nc, T, x, ctx_in, x1_out, xn_out):
    with ExitStack() as ctx:
        sem = Sems(nc, ctx, "a")

        def sb(name, shape, dt=F32):
            return ctx.enter_context(nc.sbuf_tensor("a_" + name, shape, dt))

        def banks(name, n=2):
            return [ctx.enter_context(nc.psum_tensor(f"a_{name}{i}", [128, 512], F32)) for i in range(n)]

        craw = [sb(f"craw{i}", [128, 3, C]) for i in range(2)]
        cT = [sb(f"cT{i}", [128, LK]) for i in range(4)]
        k32 = sb("k32", [128, 2, LK])
        kp = [sb(f"kp{i}", [128, 3, 2, LK], BF16) for i in range(2)]
        kst, V = T.kst, T.V
        qst = sb("qst", [ROWS + 2, H, 4 * LQ], BF16)
        P = [sb(f"P{i}", [128, 3, 4 * LQ]) for i in range(2)]
        O = sb("O", [128, 2, 4 * LQ])
        nm = sb("nm", [LQ, H])
        mm = sb("mm", [LQ, 2, H], BF16)
        mT = sb("mT", [2 * H, LQ], BF16)
        rd = [sb(f"rd{i}", [LQ, 2, 2, 2]) for i in range(2)]
        cc = [sb(f"cc{i}", [LQ, D]) for i in range(2)]
        ccT = sb("ccT", [128, 2 * LQ])
        xb = [sb(f"xb{i}", [LQ, D]) for i in range(2)]
        x1 = [sb(f"x1_{i}", [LQ, D]) for i in range(2)]
        x2 = [sb(f"x2_{i}", [LQ, D]) for i in range(2)]
        x2T = sb("x2T", [128, 2 * LQ])
        stats, mv = sb("stats", [LQ, 6]), sb("mv", [LQ, 2])
        var, y, yy = sb("var", [LQ, 1]), sb("y", [LQ, 1]), sb("yy", [LQ, 1])
        pT = banks("pT")
        pS = banks("pS")
        pO = banks("pO")
        pM = banks("pM")

        ctx_loaded = [sem("ctx_loaded0"), sem("ctx_loaded1")]
        kst_loaded = [sem(f"kst_loaded{i}") for i in range(4)]
        qst_loaded = [sem("qst_loaded0"), sem("qst_loaded1")]
        mrow_loaded = [sem("mrow_loaded0"), sem("mrow_loaded1")]
        t_ready, s_ready, o_ready = sem("t_ready"), sem("s_ready"), sem("o_ready")
        ct_ready, k_ready, v_ready = sem("ct_ready"), sem("k_ready"), sem("v_ready")
        ot_ready, mt_ready = sem("ot_ready"), sem("mt_ready")
        exp_done, ct_copied, k_copied, o_copied, mt_copied = (sem("exp_done"), sem("ct_copied"), sem("k_copied"),
                                                            sem("o_copied"), sem("mt_copied"))
        s_used, m_split, v_copied, ot_used = sem("s_used"), sem("m_split"), sem("v_copied"), sem("ot_used")
        k_cut, kchain, k_high = sem("k_cut"), sem("kchain"), sem("k_high")
        cct_ready, cct_copied, wo_ready, x1_ready = sem("cct_ready"), sem("cct_copied"), sem("wo_ready"), sem("x1_ready")
        xt_ready, xt_copied, lg_ready, lg_copied = sem("xt_ready"), sem("xt_copied"), sem("lg_ready"), sem("lg_copied")
        wo_read, x2_ready, ln = sem("wo_read"), sem("x2_ready"), sem("ln")
        xb_loaded = [sem("xb_loaded0"), sem("xb_loaded1")]
        stored = [sem("stored0"), sem("stored1")]
        passed_dve = sem("passed_dve")
        passed, passed_sp = sem("passed"), sem("passed_sp")
        m_high, rd_ready = sem("m_high"), sem("rd_ready")

        S_HEADS = [[8], [9, 10], [11, 12], [13], [14], [15], [0, 1], [2], [3], [4], [5, 6], [7]]

        def run(eng, step):
            def static(m):
                step(m // 4, m % 4, lambda off: 0 <= m + off < B)

            for m in range(-4, 1):
                static(m)
            with eng.Fori(0, B // 4 - 2) as i:
                for r in range(1, 5):
                    step(i, r, lambda off: True)
            for m in range(B - 7, B + 1):
                static(m)

        def count(i, r, off, per, add):
            return i * (4 * per) + ((r + off) * per + add)

        def fills(i, r, off, every, per, add=0):
            return i * (4 // every * per) + ((r + off) // every * per + add)

        PIECES = [(ct_copied, 4, 1, 1), (k_copied, 4, 2, 1), (k_copied, 4, 2, 2), (v_copied, 2, 2, 1),
                  (v_copied, 2, 2, 2), (ot_used, 0, 2, 1), (ot_used, 0, 2, 2), (xt_copied, -1, 1, 1),
                  (mt_copied, 2, 1, 1), (cct_copied, 0, 1, 1), (wo_read, 0, 1, 1), (lg_copied, -1, 1, 1)]

        block = ctx.enter_context(nc.Block())

        @block.sync
        def _(sp):
            def step(i, r, live):
                if live(4):
                    wait_alone(sp, ct_ready, count(i, r, 2, 1, 1), passed_sp)
                    n = count(i, r, 4, LK, 0)
                    buf, src = r % 2, ctx_in.rearrange("b k c -> (b k) c")
                    sp.dma_start(craw[buf][:, 0:2, :], src[bass.ds(n, 256)].rearrange("(c p) d -> p c d", c=2))\
                      .then_inc(ctx_loaded[buf], 16)
                    sp.dma_start(craw[buf][0:KCH[2][1], 2, :], src[bass.ds(n + 256, KCH[2][1])])\
                      .then_inc(ctx_loaded[buf], 16)
                if r % 2 == 1 and live(3):
                    half = (r + 3) % 4 // 2
                    cols = slice(half * 2 * LQ, (half + 1) * 2 * LQ)
                    wait_alone(sp, t_ready, count(i, r, 0, 12, 12), passed_sp)
                    for s in range(len(Q_SLOT)):
                        src = T.qp[:, Q_SLOT[s], :, bass.ds(count(i, r, 3, LQ, 0), 2 * LQ)]
                        sp.dma_start(qst[16 * s:16 * s + 16, :, cols], src).then_inc(qst_loaded[half], 16)
                if live(3):
                    wait_alone(sp, k_cut, count(i, r, 3, 1, 1), passed_sp)
                    wait_alone(sp, mt_copied, count(i, r, 1, 1, 1), passed_sp)
                    for s in range(len(K_SLOT)):
                        sp.dma_start(kst[(r + 3) % 4][16 * s:16 * s + 16, :, 0:LK], kp[(r + 3) % 2][:, K_SLOT[s]])\
                          .then_inc(kst_loaded[(r + 3) % 4], 16)
                if live(1):
                    wait_alone(sp, x1_ready, count(i, r, -1, 1, 1), passed_sp)
                    sp.dma_start(xb[(r + 1) % 2][:], x[bass.ds(count(i, r, 1, LQ, 0), LQ)])\
                      .then_inc(xb_loaded[(r + 1) % 2], 16)
                if live(-1):
                    wait_alone(sp, x2_ready, count(i, r, -1, 1, 1), passed_sp)
                    rows = bass.ds(count(i, r, -1, LQ, 0), LQ)
                    sp.dma_start(x1_out[rows], x1[(r - 1) % 2][:]).then_inc(stored[(r - 1) % 2], 16)
                    sp.dma_start(xn_out[rows], x2[(r - 1) % 2][:]).then_inc(stored[(r - 1) % 2], 16)
                if live(2):
                    wait(sp, mt_copied, count(i, r, 2, 1, 1))
                    c0 = (r + 2) % 4 * LQ
                    sp.dma_start(qst[ROWS:ROWS + 2, :, c0:c0 + LQ], mT[:]).then_inc(mrow_loaded[(r + 2) % 2], 16)

            run(sp, step)
            for p in range(2):
                sp.wait_ge(stored[p], B // 2 * 32)

        @block.gpsimd
        def _(pool):
            def step(i, r, live):
                if not live(4):
                    return
                out, at = kp[(r + 4) % 2], [0]
                wait(pool, k_high, count(i, r, 4, 1, 1))

                def link(ins):
                    at[0] += 1
                    ins.then_inc(kchain, 1)
                    wait_alone(pool, kchain, count(i, r, 4, 2, at[0]), passed)

                link(pool.tensor_tensor(k32[:], k32[:], out[:, 0], ALU.subtract))
                link(pool.tensor_copy(out[:, 1], k32[:]))
                pool.tensor_tensor(out[:, 2], k32[:], out[:, 1], ALU.subtract).then_inc(k_cut, 1)

            run(pool, step)

        @block.scalar
        def _(act):
            def step(i, r, live):
                for u in range(12):
                    if live(1):
                        act.wait_ge(t_ready, count(i, r, 1, 12, u + 1))
                        quad, c = divmod(u, 3)
                        act.activation(P[quad % 2][:, c, :], pT[u % 2][:, 0:4 * LQ], ACT.Exp).then_inc(exp_done, 1)
                    if u == 7 and live(-1):
                        act.wait_ge(xt_ready, count(i, r, -1, 1, 1))
                        act.activation(x2T[:], pM[1][:, 0:2 * LQ], ACT.Copy).then_inc(xt_copied, 1)
                    if u == 11 and live(-1):
                        act.wait_ge(lg_ready, count(i, r, -1, 1, 1))
                        act.activation(T.lg[:, bass.ds(count(i, r, -1, NE, 0), NE)], pM[1][0:LQ, 0:NE], ACT.Copy)\
                           .then_inc(lg_copied, 1)
                    if u == 9 and live(0):
                        act.wait_ge(cct_ready, count(i, r, 0, 1, 1))
                        act.activation(ccT[:], pM[1][:, 0:2 * LQ], ACT.Copy).then_inc(cct_copied, 1)
                    if u == 0 and live(4):
                        act.wait_ge(ct_ready, count(i, r, 4, 1, 1))
                        act.activation(cT[r % 4][:], pM[0][:, 0:LK], ACT.Copy).then_inc(ct_copied, 1)
                    if u in (1, 2) and live(4):
                        t = u - 1
                        wait(act, k_cut, count(i, r, 4, 1, 0))
                        act.wait_ge(k_ready, count(i, r, 4, 2, t + 1))
                        act.activation(k32[:, t, :], pM[u % 2][:, 0:LK], ACT.Identity, bias=T.bk[:, t:t + 1])\
                           .then_inc(k_copied, 1)
                    if u == 2 and live(4):
                        act.wait_ge(k_copied, count(i, r, 4, 2, 2))
                        wait(act, kst_loaded[(r + 2) % 4], fills(i, r, 2, 4, 96, 96))
                        act.activation(kp[r % 2][:, 0], k32[:], ACT.Copy).then_inc(k_high, 1)
                    if u in (3, 4) and live(2):
                        act.wait_ge(v_ready, count(i, r, 2, 2, u - 2))
                        for c in ((0, 1) if u == 3 else (2,)):
                            n = KCH[c][1]
                            v = V[(r + 2) % 2][0:n, c, :, 0:34].rearrange("p g (s w) -> p g s w", s=2)[:, :, :, 0:DK]
                            src = pM[u % 2][0:n, (c % 2) * D:(c % 2 + 1) * D]
                            ins = act.activation(v, src.rearrange("p (g s w) -> p g s w", g=8, s=2), ACT.Copy)
                        ins.then_inc(v_copied, 1)
                    if u == 3 and live(0):
                        act.wait_ge(o_ready, count(i, r, 0, 2, 2))
                        act.activation(O[:, 1, :], pO[1][:, 0:4 * LQ], ACT.Copy).then_inc(o_copied, 1)
                    if u == 9 and live(1):
                        act.wait_ge(o_ready, count(i, r, 1, 2, 1))
                        act.activation(O[:, 0, :], pO[0][:, 0:4 * LQ], ACT.Copy).then_inc(o_copied, 1)
                    if u == 8 and live(2):
                        act.wait_ge(mt_ready, count(i, r, 2, 1, 1))
                        wait(act, mrow_loaded[(r + 1) % 2], fills(i, r, 1, 2, 16, 16))
                        act.activation(mT[:], pM[0][0:2 * H, 0:LQ // 2].bitcast(BF16), ACT.Copy).then_inc(mt_copied, 1)

            run(act, step)

        @block.vector
        def _(dve):
            def score_max(i, r, off, h):
                dve.wait_ge(s_ready, count(i, r, off, H, h + 1))
                if h == 0:
                    wait(dve, m_split, count(i, r, off, 1, 0))
                dve.tensor_reduce(nm[:, h:h + 1], pS[h % 2][0:LQ, 0:LK], AXX, ALU.max, negate=True).then_inc(s_used, 1)

            def layernorm(i, r, k):
                p, yb = (r - 1) % 2, y[:].bitcast(I32)
                if k == 0:
                    wait_alone(dve, ln, count(i, r, -1, 14, 1), passed_dve)
                    ins = dve.bn_aggr(mv[:], stats[:])
                else:
                    dve.wait_ge(ln, count(i, r, -1, 14, k + 1))
                if k == 1:
                    ins = dve.tensor_scalar(var[:], mv[:, 1:2], EPS, None, ALU.add)
                elif k == 2:
                    ins = dve.tensor_scalar(yb, var[:].bitcast(I32), 1, None, ALU.logical_shift_right)
                elif k == 3:
                    ins = dve.tensor_scalar(yb, yb, -1.0, float(0x5f3759df), ALU.mult, ALU.add)
                elif k == 13:
                    ins = dve.tensor_scalar(x2[p][:], x1[p][:], mv[:, 0:1], y[:], ALU.subtract, ALU.mult)
                elif k % 3 == 1:
                    ins = dve.tensor_tensor(yy[:], y[:], y[:], ALU.mult)
                elif k % 3 == 2:
                    ins = dve.scalar_tensor_tensor(yy[:], yy[:], -0.5, var[:], ALU.mult, ALU.mult)
                elif k:
                    ins = dve.scalar_tensor_tensor(y[:], yy[:], 1.5, y[:], ALU.add, ALU.mult)
                ins.then_inc(x2_ready if k == 13 else ln, 1)

            def step(i, r, live):
                for u in range(12):
                    if u < 7 and live(-1):
                        layernorm(i, r, 2 * u)
                    if u < 6 and live(2):
                        for h in S_HEADS[u]:
                            score_max(i, r, 2, h)
                    if u >= 6 and live(3):
                        for h in S_HEADS[u]:
                            score_max(i, r, 3, h)
                    if u < 7 and live(-1):
                        layernorm(i, r, 2 * u + 1)
                    if u == 5 and live(2):
                        dve.wait_ge(s_used, count(i, r, 2, H, H))
                        wait(dve, mt_ready, count(i, r, 2, 1, 0))
                        dve.tensor_copy(mm[:, 0, :], nm[:]).then_inc(m_high, 1)
                        dve.wait_ge(m_high, count(i, r, 2, 1, 1))
                        dve.tensor_tensor(mm[:, 1, :], nm[:], mm[:, 0, :], ALU.subtract).then_inc(m_split, 1)
                    if u in (5, 6) and live(0):
                        hb = u - 5
                        dve.wait_ge(ot_ready, count(i, r, 0, 2, hb + 1))
                        src = pM[u % 2][0:LQ, 0:512].rearrange("p (i s j w) -> p s i j w", i=2, s=2, j=2)
                        out = cc[r % 2][:, hb * 128:(hb + 1) * 128]\
                            .rearrange("p (i j s w) -> p s i j w", i=2, j=2, s=2)
                        for s in range(2):
                            dve.reciprocal(rd[hb][:, s], src[:, s, :, :, 17 * s + DK]).then_inc(rd_ready, 1)
                        dve.wait_ge(rd_ready, count(i, r, 0, 4, 2 * hb + 2))
                        for s in range(2):
                            ins = dve.tensor_tensor(out[:, s], src[:, s, :, :, 17 * s:17 * s + DK],
                                                    rd[hb][:, s].unsqueeze(3).to_broadcast([LQ, 2, 2, DK]), ALU.mult)
                        ins.then_inc(ot_used, 1)

                    if u == 10 and live(0):
                        xo, p = x1[r % 2], r % 2
                        wait(dve, stored[p], fills(i, r, -2, 2, 32, 32))
                        dve.wait_ge(wo_ready, count(i, r, 0, 1, 1))
                        dve.tensor_tensor(xo[:], pM[0][0:LQ, 0:D], T.bo[:], ALU.add).then_inc(wo_read, 1)
                        dve.wait_ge(wo_read, count(i, r, 0, 1, 1))
                        dve.wait_ge(xb_loaded[p], fills(i, r, 0, 2, 16, 16))
                        dve.scalar_tensor_tensor(xo[:], xo[:], T.gx[0:LQ], xb[p][:], ALU.mult, ALU.add).then_inc(x1_ready, 1)
                        dve.wait_ge(x1_ready, count(i, r, 0, 1, 1))
                        dve.bn_stats(stats[:], xo[:]).then_inc(ln, 1)

            run(dve, step)

        @block.tensor
        def _(pe):
            def bank_free(i, r, u, live):
                back, k = 0, u - 2
                while back < 6:
                    if k < 0:
                        back, k = back + 1, k + 12
                    sem_, off, per, nth = PIECES[k]
                    if live(off - back):
                        wait(pe, sem_, count(i, r, off - back, per, nth))
                        return
                    k -= 2

            def piece(i, r, u, bank):
                if u == 7:
                    pe.wait_ge(x2_ready, count(i, r, -1, 1, 1))
                    for k in range(2):
                        last = pe.transpose(bank[:, k * LQ:(k + 1) * LQ], x2[(r - 1) % 2][:, k * 128:(k + 1) * 128],
                                            T.ident[0:LQ, 0:LQ])
                    last.then_inc(xt_ready, 1)
                elif u == 0:
                    pe.wait_ge(ctx_loaded[r % 2], fills(i, r, 4, 2, 32, 32))
                    for c, (k0, n) in enumerate(KCH):
                        last = pe.transpose(bank[:, k0:k0 + n], craw[r % 2][0:n, c, :], T.ident[0:n, 0:n])
                    last.then_inc(ct_ready, 1)
                elif u in (1, 2):
                    pe.wait_ge(ct_copied, count(i, r, 4, 1, 1))
                    pe.matmul(bank[:, 0:LK], T.wk[:, u - 1, :], cT[r % 4][:], start=True, stop=True)\
                      .then_inc(k_ready, 1)
                elif u in (3, 4):
                    for c in ((0, 1) if u == 3 else (2,)):
                        k0, n = KCH[c]
                        last = pe.matmul(bank[0:n, (c % 2) * D:(c % 2 + 1) * D], cT[(r + 2) % 4][:, k0:k0 + n], T.wv[:],
                                         start=True, stop=True)
                    last.then_inc(v_ready, 1)
                elif u in (5, 6):
                    pe.wait_ge(o_copied, count(i, r, 0, 2, u - 4))
                    for k in range(4):
                        last = pe.transpose(bank[0:LQ, k * 128:(k + 1) * 128], O[:, u - 5, k * LQ:(k + 1) * LQ],
                                            T.ident[:])
                    last.then_inc(ot_ready, 1)
                elif u == 8:
                    pe.wait_ge(m_split, count(i, r, 2, 1, 1))
                    pe.transpose(bank[0:2 * H, 0:LQ // 2].bitcast(BF16), mm[:].rearrange("p a h -> p (a h)"),
                                 T.identb[0:LQ, 0:LQ]).then_inc(mt_ready, 1)
                elif u == 9:
                    pe.wait_ge(ot_used, count(i, r, 0, 2, 2))
                    for k in range(2):
                        last = pe.transpose(bank[:, k * LQ:(k + 1) * LQ], cc[r % 2][:, k * 128:(k + 1) * 128],
                                            T.ident[0:LQ, 0:LQ])
                    last.then_inc(cct_ready, 1)
                elif u == 10:
                    pe.wait_ge(cct_copied, count(i, r, 0, 1, 1))
                    for k in range(2):
                        last = pe.matmul(bank[0:LQ, 0:D], ccT[:, k * LQ:(k + 1) * LQ], T.wo[:, k, :], start=(k == 0),
                                         stop=(k == 1))
                    last.then_inc(wo_ready, 1)
                else:
                    pe.wait_ge(xt_copied, count(i, r, -1, 1, 1))
                    for k in range(2):
                        last = pe.matmul(bank[0:LQ, 0:NE], x2T[:, k * LQ:(k + 1) * LQ], T.wg[:, k, :], start=(k == 0),
                                         stop=(k == 1))
                    last.then_inc(lg_ready, 1)

            def step(i, r, live):
                for u in range(12):
                    quad, c = divmod(u, 3)
                    if live(1):
                        if u == 0:
                            pe.wait_ge(mrow_loaded[(r + 1) % 2], fills(i, r, 1, 2, 16, 16))
                        wait(pe, exp_done, count(i, r, 1, 12, u - 1))
                        cols = slice((r + 1) % 4 * LQ, ((r + 1) % 4 + 1) * LQ)
                        for j in range(4):
                            h = 4 * quad + j
                            last = pe.matmul(pT[u % 2][:, j * LQ:(j + 1) * LQ],
                                             kst[(r + 1) % 4][:, h, c * 128:(c + 1) * 128], qst[:, h, cols],
                                             start=True, stop=True)
                        last.then_inc(t_ready, 1)
                    off, heads = 2 if u < 6 else 3, S_HEADS[u]
                    if live(off):
                        if u == 6:
                            pe.wait_ge(kst_loaded[(r + 3) % 4], fills(i, r, 3, 4, 96, 96))
                            pe.wait_ge(qst_loaded[(r + 3) % 4 // 2], fills(i, r, 3, 4, 96, 96))
                        cols = slice((r + off) % 4 * LQ, ((r + off) % 4 + 1) * LQ)
                        for h in heads:
                            wait(pe, s_used, count(i, r, off, H, h - 1))
                            pe.matmul(pS[h % 2][0:LQ, 0:LK], qst[0:ROWS, h, cols], kst[(r + off) % 4][0:ROWS, h, 0:LK],
                                      start=True, stop=True).then_inc(s_ready, 1)
                    q2, b2 = (quad - 1, 1) if quad else (3, 0)
                    if live(b2):
                        pe.wait_ge(exp_done, count(i, r, b2, 12, 3 * q2 + c + 1))
                        if q2 == 0 and c == 0:
                            pe.wait_ge(v_copied, count(i, r, b2, 2, 2))
                        if q2 % 2 == 0 and c == 0:
                            wait(pe, o_copied, count(i, r, b2, 2, -1 + q2 // 2))
                        n = KCH[c][1]
                        for jt in range(2):
                            last = pe.matmul(pO[q2 // 2][64 * jt:64 * jt + VW, q2 % 2 * 2 * LQ:(q2 % 2 + 1) * 2 * LQ],
                                             V[(r + b2) % 2][0:n, c, 2 * q2 + jt, :],
                                             P[q2 % 2][0:n, c, jt * 2 * LQ:(jt + 1) * 2 * LQ],
                                             start=(c == 0), stop=(c == 2), skip_group_check=True)
                        if q2 % 2 == 1 and c == 2:
                            last.then_inc(o_ready, 1)
                    if live(PIECES[u][1]):
                        bank_free(i, r, u, live)
                        piece(i, r, u, pM[u % 2])

            run(pe, step)


class Tiles:
    pass


def constants(nc, T, ctx, attn, Wq, bq, Wk, bk, Wv, bv, Wo, bo, Wg, g_xattn, g_ffn):
    def sb(name, shape, dt=F32):
        return ctx.enter_context(nc.sbuf_tensor(name, shape, dt))

    T.ident, T.identb = sb("ident", [128, 128]), sb("identb", [128, 128], BF16)
    T.wq, T.wk, T.wv = sb("wq", [128, 2, 2, 128]), sb("wk", [128, 2, 128]), sb("wv", [128, D])
    T.wo, T.wg = sb("wo", [128, 2, D]), sb("wg", [128, 2, NE])
    T.bq, T.bk, T.bo = sb("bq", [128, 2]), sb("bk", [128, 2]), sb("bo", [LQ, D])
    T.gx, T.gf = sb("gx", [128, 1]), sb("gf", [128, 1])
    T.kst = [attn.enter_context(nc.sbuf_tensor(f"kst{i}", [ROWS + 2, H, KPAD], BF16)) for i in range(4)]
    T.V = [attn.enter_context(nc.sbuf_tensor(f"V{i}", [128, 3, H // 2, VW], F32)) for i in range(2)]
    with ExitStack() as own:
        sem = Sems(nc, own, "c")
        wq_raw = own.enter_context(nc.sbuf_tensor("wq_raw", [128, 2, D], F32))
        wk_raw = own.enter_context(nc.sbuf_tensor("wk_raw", [128, D], F32))
        bq_raw = own.enter_context(nc.sbuf_tensor("bq_raw", [128, 2], F32))
        g_raw = own.enter_context(nc.sbuf_tensor("g_raw", [128, 2], F32))
        bv_raw = own.enter_context(nc.sbuf_tensor("bv_raw", [128, 2], F32))
        bv_wide = own.enter_context(nc.sbuf_tensor("bv_wide", [128, 2, LQ], F32))
        pB = own.enter_context(nc.psum_tensor("c_pB", [128, 512], F32))
        loaded, bq_loaded, zeroed = sem("loaded"), sem("bq_loaded"), sem("zeroed")
        bv_ready, bo_ready, vzeroed = sem("bv_ready"), sem("bo_ready"), sem("vzeroed")
        block = own.enter_context(nc.Block())

        @block.sync
        def _(sp):
            sp.dma_start(wq_raw[:], Wq.rearrange("(k p) n -> p k n", p=128)).then_inc(loaded, 16)
            sp.dma_start(wk_raw[:], Wk).then_inc(loaded, 16)
            sp.dma_start(T.wv[:], Wv).then_inc(loaded, 16)
            sp.dma_start(T.wo[:], Wo.rearrange("(k p) n -> p k n", p=128)).then_inc(loaded, 16)
            sp.dma_start(T.wg[:], Wg.rearrange("(k p) n -> p k n", p=128)).then_inc(loaded, 16)
            sp.wait_ge(loaded, 8 * 16 + 2 * 16)

        @block.scalar
        def _(act):
            act.dma_start(bq_raw[:], bq.rearrange("(h t d) -> d h t", h=8, t=2),
                          allow_slow_non_contiguous=True).then_inc(bq_loaded, 16)
            act.dma_start(T.bk[:], bk.rearrange("(h t d) -> d h t", h=8, t=2),
                          allow_slow_non_contiguous=True).then_inc(loaded, 16)
            act.dma_start(bv_raw[:], bv.rearrange("(k p) -> p k", p=128),
                          allow_slow_non_contiguous=True).then_inc(loaded, 16)
            act.dma_start(T.bo[:], bo.partition_broadcast(LQ)).then_inc(loaded, 16)
            act.dma_start(g_raw[:, 0:1], g_xattn.partition_broadcast(128)).then_inc(loaded, 16)
            act.dma_start(g_raw[:, 1:2], g_ffn.partition_broadcast(128)).then_inc(loaded, 16)
            act.wait_ge(bq_loaded, 16)
            act.activation(T.bq[:], bq_raw[:], ACT.Copy, scale=float(DK) ** -0.5)
            act.wait_ge(loaded, 10 * 16)
            act.activation(T.gx[:], g_raw[:, 0:1], ACT.Tanh)
            act.activation(T.gf[:], g_raw[:, 1:2], ACT.Tanh)

        @block.gpsimd
        def _(pool):
            for m in (T.ident, T.identb):
                pool.memset(m[:], 0.0).then_inc(zeroed, 1)
            for v in T.V:
                pool.memset(v[:], 0.0).then_inc(zeroed, 1)
            for k in T.kst:
                pool.memset(k[:, :, LK:KPAD], 0.0)
            pool.wait_ge(zeroed, 4)
            for v in T.V:
                for s in range(2):
                    pool.memset(v[:, :, :, 17 * s + DK:17 * s + DK + 1], 1.0)
            for m in (T.ident, T.identb):
                pool.affine_select(out=m[:], in_=m[:], compare_op=ALU.not_equal, fill=1.0, base=0,
                                   pattern=[[-1, 128]], channel_multiplier=1)

        @block.tensor
        def _(pe):
            pe.wait_ge(bv_ready, 1)
            pe.wait_ge(loaded, 10 * 16)
            for k in range(2):
                last = pe.matmul(pB[0:LQ, 0:D], bv_wide[:, k, :], T.wo[:, k, :], start=(k == 0), stop=(k == 1))
            last.then_inc(bo_ready, 1)

        @block.vector
        def _(dve):
            one = 0x3F803F80
            for k in T.kst:
                dve.memset(k[ROWS:ROWS + 2, :, 0:PAIRED].bitcast(I32), one)
                dve.memset(k[ROWS:ROWS + 2, :, PAIRED:LK], 1.0)
            dve.wait_ge(loaded, 10 * 16)
            dve.tensor_copy(bv_wide[:], bv_raw[:].unsqueeze(2).to_broadcast([128, 2, LQ])).then_inc(bv_ready, 1)
            dve.wait_ge(bo_ready, 1)
            dve.tensor_tensor(T.bo[:], pB[0:LQ, 0:D], T.bo[:], ALU.add)
            for k in range(2):
                dve.tensor_copy(T.wq[:, k].rearrange("p t (d h) -> p t d h", h=8),
                                wq_raw[:, k].rearrange("p (h t d) -> p t d h", h=8, t=2))
            dve.tensor_copy(T.wk[:].rearrange("p t (d h) -> p t d h", h=8),
                            wk_raw[:].rearrange("p (h t d) -> p t d h", h=8, t=2))


def routing(nc, T):
    NG, EB = CAP // 128, NE * B
    BIG = 4096.0
    with ExitStack() as ctx:
        sem = Sems(nc, ctx, "r")

        def sb(name, shape, dt=F32):
            return ctx.enter_context(nc.sbuf_tensor("r_" + name, shape, dt))

        def banks(name, n=2):
            return [ctx.enter_context(nc.psum_tensor(f"r_{name}{i}", [128, 512], F32)) for i in range(n)]

        en = sb("en", [LQ, EB])
        S = sb("S", [LQ, EB])
        S1, S2, S3 = (sb(f"S{i}", [LQ, EB], BF16) for i in (1, 2, 3))
        Sr = sb("Sr", [LQ, EB])
        ST = sb("ST", [128, 2 * LQ])
        junk = sb("junk", [128, 3, 2 * LQ], BF16)
        tries, gap = sb("tries", [128, 3]), sb("gap", [128, 3])
        held = [sb(f"held{i}", [128, 4]) for i in range(2)]
        power = sb("power", [128, 1])
        factors = sb("factors", [128, 5, 3])
        cnt, ceq, row = sb("cnt", [128, 3], BF16), sb("ceq", [128, 1], BF16), sb("row", [128, 1], BF16)
        need, off = sb("need", [128, 1]), sb("off", [128, 1])
        gt, eq, cum, sel, ones = (sb(n, [128, 2 * LQ]) for n in ("gt", "eq", "cum", "sel", "ones"))
        same, below = sb("same", [128, 128], BF16), sb("below", [128, 128], BF16)
        pi, hi_i, lo_i = (sb(n, [LQ, EB], I32) for n in ("pi", "hi_i", "lo_i"))
        hi, lo = sb("hi", [LQ, EB]), sb("lo", [LQ, EB])
        iota_b, iota_g, iota_p, iota_l = (sb("iota_b", [LQ, B]), sb("iota_g", [LQ, NG]), sb("iota_p", [LQ, 1]),
                                          sb("iota_l", [LQ, 128], BF16))
        A = sb("A", [LQ, EB, 5, NG], BF16)
        hot = sb("hot", [LQ, EB, NG], BF16)
        L = [sb(f"L{i}", [LQ, B, 128], BF16) for i in range(2)]
        rt = sb("rt", [128, NE, 5, NG])
        pT, pC, pP, pR = banks("pT", 1)[0], banks("pC", 1)[0], banks("pP", 1)[0], banks("pR", 1)[0]
        v, pe_done, act_done, consts = sem("v"), sem("pe_done"), sem("act_done"), sem("consts")
        factors_set = sem("factors_set")
        counted, summed, l_ready, l_used = sem("counted"), sem("summed"), sem("l_ready"), sem("l_used")
        block = ctx.enter_context(nc.Block())
        FACTORS = [[2.0 ** 32, 2.0 ** 64, 2.0 ** 96], [2.0 ** 8, 2.0 ** 16, 2.0 ** 24], [4.0, 16.0, 64.0],
                   [1.5, 2.0, 3.0], [0.125, 0.25, 0.375]]
        ROUNDS = 4 + 11

        @block.gpsimd
        def _(pool):
            def then(ins):
                ins.then_inc(consts, 1)
                then.n += 1
                pool.wait_ge(consts, then.n)
            then.n = 0

            for k, row_of in enumerate(FACTORS):
                for j, f in enumerate(row_of):
                    pool.memset(factors[:, k, j:j + 1], f).then_inc(factors_set, 1)
            then(pool.iota(iota_b[:], pattern=[[1, B]], base=0, channel_multiplier=0, allow_small_or_imprecise_dtypes=True))
            then(pool.iota(iota_g[:], pattern=[[1, NG]], base=0, channel_multiplier=0, allow_small_or_imprecise_dtypes=True))
            then(pool.iota(iota_p[:], pattern=[[0, 1]], base=0, channel_multiplier=1, allow_small_or_imprecise_dtypes=True))
            then(pool.iota(iota_l[:], pattern=[[1, 128]], base=0, channel_multiplier=0, allow_small_or_imprecise_dtypes=True))
            then(pool.memset(ones[:], 1.0))
            then(pool.memset(same[:], 1.0))
            Q = B // 2
            blocks = same[:].rearrange("p (e q) -> p e q", q=Q)
            then(pool.affine_select(out=blocks, in_=blocks, compare_op=ALU.is_ge, fill=0.0, base=0,
                                    pattern=[[-Q, NE], [0, Q]], channel_multiplier=1))
            then(pool.affine_select(out=blocks, in_=blocks, compare_op=ALU.is_ge, fill=0.0, base=Q - 1,
                                    pattern=[[Q, NE], [0, Q]], channel_multiplier=-1))
            then(pool.affine_select(out=below[:], in_=same[:], compare_op=ALU.is_ge, fill=0.0, base=-1,
                                    pattern=[[1, 128]], channel_multiplier=-1))

        @block.scalar
        def _(act):
            act.wait_ge(v, 1)
            act.activation(en[:].rearrange("p (e b) -> p e b", e=NE), en[:].rearrange("p (e b) -> p e b", e=NE), ACT.Exp, scale=-1.0)\
               .then_inc(act_done, 1)

        @block.tensor
        def _(pe):
            pe.wait_ge(v, 4)
            for h in range(2):
                last = pe.transpose(pT[:, h * LQ:(h + 1) * LQ], Sr[:, h * 128:(h + 1) * 128], T.ident[0:LQ, 0:LQ])
            last.then_inc(pe_done, 1)
            pe.wait_ge(consts, 9)

            def total(k):
                pe.wait_ge(counted, k)
                pe.matmul(pC[:, 0:3], same[:], cnt[:], start=True, stop=True).then_inc(summed, 1)

            for k in range(5):
                total(k + 1)
            with pe.Fori(0, (ROUNDS - 5) // 2) as i:
                for r in range(2):
                    total(i * 2 + 6 + r)
            pe.wait_ge(counted, ROUNDS + 1)
            pe.matmul(pC[:, 0:1], same[:], cnt[:, 0:1], start=True, stop=True)
            pe.matmul(pC[:, 1:2], below[:], ceq[:], start=True, stop=True).then_inc(summed, 1)
            pe.wait_ge(counted, ROUNDS + 2)
            pe.matmul(pC[:, 2:3], below[:], row[:], start=True, stop=True).then_inc(summed, 1)
            pe.wait_ge(counted, ROUNDS + 3)
            for h in range(2):
                last = pe.transpose(pP[0:LQ, h * 128:(h + 1) * 128], sel[:, h * LQ:(h + 1) * LQ], T.ident[:])
            last.then_inc(summed, 1)
            for e in range(NE):
                pe.wait_ge(l_ready, e + 1)
                for b in range(B):
                    last = pe.matmul(pR[:, e * 35:(e + 1) * 35], L[e % 2][:, b, :],
                                     A[:, e * B + b].rearrange("p c g -> p (c g)"), start=(b == 0), stop=(b == B - 1))
                last.then_inc(l_used, 1)

        @block.vector
        def _(dve):
            n = [0]

            def link(ins):
                n[0] += 1
                ins.then_inc(v, 1)
                dve.wait_ge(v, n[0])

            link(dve.tensor_scalar(en[:].rearrange("p (e b) -> p e b", e=NE), T.lg[:].rearrange("p (b e) -> p e b", e=NE),
                                   -87.0, None, ALU.max))
            dve.wait_ge(act_done, 1)
            link(dve.tensor_scalar(en[:], en[:], 1.0, None, ALU.add))
            link(dve.reciprocal(S[:], en[:]))
            link(dve.tensor_scalar(Sr[:].rearrange("p (h c) -> p h c", h=2), S[:].rearrange("p (c h) -> p h c", h=2),
                                   2.0 ** 64, 2.0 ** -62, ALU.mult, ALU.max))
            link(dve.tensor_copy(S1[:], S[:]))
            link(dve.tensor_tensor(S[:], S[:], S1[:], ALU.subtract))
            link(dve.tensor_copy(S2[:], S[:]))
            link(dve.tensor_tensor(S3[:], S[:], S2[:], ALU.subtract))
            dve.wait_ge(pe_done, 1)
            link(dve.tensor_copy(ST[:], pT[:, 0:2 * LQ]))
            link(dve.memset(held[0][:, 3:4], 2.0 ** -62))
            dve.wait_ge(factors_set, 15)
            link(dve.tensor_scalar(tries[:], factors[:, 0, :], held[0][:, 3:4], None, ALU.mult))

            def counts():
                for j in range(3):
                    ins = dve.tensor_scalar(junk[:, j], ST[:], tries[:, j:j + 1], None, ALU.is_ge, ALU.add,
                                            accum_out=cnt[:, j:j + 1])
                ins.then_inc(counted, 1)

            def best(k, at, r):
                dve.wait_ge(summed, k + 1)
                dve.scalar_tensor_tensor(held[r][:, 0:3], pC[:, 0:3], float(CAP), tries[:], ALU.is_ge, ALU.mult)\
                   .then_inc(v, 1)
                dve.wait_ge(v, at + 1)
                dve.tensor_reduce(held[1 - r][:, 3:4], held[r][:], mybir.AxisListType.X, ALU.max).then_inc(v, 1)
                dve.wait_ge(v, at + 2)

            for k in range(4):
                counts()
                best(k, n[0], k % 2)
                n[0] += 2
                now = held[1 - k % 2][:, 3:4]
                if k < 3:
                    link(dve.tensor_scalar(tries[:], factors[:, k + 1, :], now, None, ALU.mult))
            link(dve.tensor_scalar(power[:].bitcast(I32), now.bitcast(I32), 0x7F800000, None, ALU.bitwise_and))
            link(dve.tensor_scalar(gap[:], factors[:, 4, :], power[:], None, ALU.mult))
            link(dve.tensor_scalar(tries[:], gap[:], now, None, ALU.add))
            base = n[0]

            def fraction(k, at, r):
                counts()
                dve.tensor_scalar(gap[:], gap[:], 0.25, None, ALU.mult).then_inc(v, 1)
                best(k, at + 1, r)
                dve.tensor_scalar(tries[:], gap[:], held[1 - r][:, 3:4], None, ALU.add).then_inc(v, 1)
                dve.wait_ge(v, at + 4)

            fraction(4, base, 0)
            with dve.Fori(0, (ROUNDS - 5) // 2) as i:
                for r in range(2):
                    fraction(i * 2 + 5 + r, i * 8 + (base + 4 + 4 * r), 1 - r)
            n[0] = base + 4 * (ROUNDS - 4)
            cand = held[1][:, 3:4]
            dve.tensor_scalar(gt[:], ST[:], cand, None, ALU.is_gt, ALU.add, accum_out=cnt[:, 0:1])
            dve.tensor_scalar(eq[:], ST[:], cand, None, ALU.is_equal, ALU.add, accum_out=ceq[:]).then_inc(counted, 1)
            dve.wait_ge(counted, ROUNDS + 1)
            link(dve.tensor_tensor_scan(cum[:], ones[:], eq[:], 0.0, ALU.mult, ALU.add))
            dve.wait_ge(summed, ROUNDS + 1)
            link(dve.tensor_scalar(need[:], pC[:, 0:1], -1.0, float(CAP), ALU.mult, ALU.add))
            link(dve.tensor_copy(off[:], pC[:, 1:2]))
            link(dve.tensor_scalar(cum[:], cum[:], off[:], need[:], ALU.add, ALU.is_le))
            link(dve.tensor_tensor(cum[:], cum[:], eq[:], ALU.mult))
            link(dve.tensor_tensor(sel[:], cum[:], gt[:], ALU.add))
            link(dve.tensor_tensor_scan(cum[:], ones[:], sel[:], 0.0, ALU.mult, ALU.add))
            dve.tensor_copy(row[:], cum[:, 2 * LQ - 1:2 * LQ]).then_inc(counted, 1)
            dve.wait_ge(summed, ROUNDS + 2)
            link(dve.tensor_scalar(off[:], pC[:, 2:3], -(BIG + 1.0), None, ALU.add))
            link(dve.scalar_tensor_tensor(sel[:], cum[:], off[:], sel[:], ALU.add, ALU.mult))
            dve.tensor_scalar(sel[:], sel[:], BIG, None, ALU.add).then_inc(counted, 1)
            dve.wait_ge(summed, ROUNDS + 3)
            link(dve.tensor_copy(pi[:].rearrange("p (c h) -> p h c", h=2), pP[0:LQ, 0:EB].rearrange("p (h c) -> p h c", h=2)))
            link(dve.tensor_scalar(hi_i[:], pi[:], 7, None, ALU.logical_shift_right))
            link(dve.tensor_scalar(lo_i[:], pi[:], 127, None, ALU.bitwise_and))
            link(dve.tensor_copy(hi[:], hi_i[:]))
            link(dve.tensor_copy(lo[:], lo_i[:]))

            def wide(ap):
                return ap.unsqueeze(2).to_broadcast([LQ, EB, NG])

            dve.wait_ge(consts, 9)
            link(dve.tensor_tensor(hot[:], wide(hi[:]), iota_g[:].unsqueeze(1).to_broadcast([LQ, EB, NG]), ALU.is_equal))
            link(dve.tensor_tensor(A[:, :, 1, :], hot[:], wide(S1[:]), ALU.mult))
            for e in range(NE):
                ins = dve.tensor_tensor(A[:, e * B:(e + 1) * B, 0, :], hot[:, e * B:(e + 1) * B],
                                        iota_b[:].unsqueeze(2).to_broadcast([LQ, B, NG]), ALU.mult)
            link(ins)
            link(dve.tensor_tensor(A[:, :, 2, :], hot[:], wide(S2[:]), ALU.mult))
            link(dve.tensor_tensor(A[:, :, 3, :], hot[:], wide(S3[:]), ALU.mult))
            link(dve.tensor_scalar(A[:, :, 4, :], hot[:], iota_p[:], None, ALU.mult))
            for e in range(NE):
                if e >= 2:
                    dve.wait_ge(l_used, e - 1)
                for b in range(B):
                    ins = dve.tensor_scalar(L[e % 2][:, b, :], iota_l[:], lo[:, e * B + b:e * B + b + 1], None, ALU.is_equal)
                ins.then_inc(l_ready, 1)
            dve.wait_ge(l_used, NE)
            link(dve.tensor_copy(rt[:].rearrange("p e c g -> p (e c g)"), pR[:, 0:NE * 35]))
            link(dve.scalar_tensor_tensor(T.idx[:], rt[:, :, 0, :], float(LQ), rt[:, :, 4, :], ALU.mult, ALU.add))
            link(dve.tensor_tensor(T.gate[:], rt[:, :, 1, :], rt[:, :, 2, :], ALU.add))
            link(dve.tensor_tensor(T.gate[:], T.gate[:], rt[:, :, 3, :], ALU.add))
            link(dve.tensor_scalar(T.gate[:], T.gate[:], T.gf[:], None, ALU.mult))


def experts(nc, T, xn, W1, b1, W2, b2, out):
    NG = CAP // 128
    CHUNK = [(0, 4), (4, NG)]
    with ExitStack() as ctx:
        sem = Sems(nc, ctx, "e")

        def sb(name, shape, dt=F32):
            return ctx.enter_context(nc.sbuf_tensor("e_" + name, shape, dt))

        def banks(name, n=2):
            return [ctx.enter_context(nc.psum_tensor(f"e_{name}{i}", [128, 512], F32)) for i in range(n)]

        w1, w2 = sb("w1", [128, 2, FF]), sb("w2", [128, 8, D])
        w1h, w1l = ([sb(f"w1{p}{i}", [128, 2, FF], F32R) for i in range(2)] for p in "hl")
        w2h, w2l = ([sb(f"w2{p}{i}", [128, 8, D], F32R) for i in range(2)] for p in "hl")
        b1raw, b1s = sb("b1raw", [64, 128]), sb("b1s", [128, 64])
        b1s_of = [sb(f"b1e{i}", [128, 8]) for i in range(2)]
        b2s = [sb(f"b2s{i}", [128, D]) for i in range(2)]
        idx, gate = [sb(f"idx{i}", [128, NG], I32) for i in range(2)], [sb(f"gate{i}", [128, NG]) for i in range(2)]
        ex = sb("ex", [128, NG, D])
        exh, exl = sb("exh", [128, 2, CAP], F32R), sb("exl", [128, 2, CAP], F32R)
        hid = [sb(f"hid{i}", [128, 512]) for i in range(2)]
        hh, hl = sb("hh", [128, 8, CAP], F32R), sb("hl", [128, 8, CAP], F32R)
        y = [sb(f"y{i}", [128, D]) for i in range(NG)]
        p1, p2, pT = banks("p1"), banks("p2"), banks("pT")
        w_loaded, w_high, w_low = sem("w_loaded"), sem("w_high"), sem("w_low")
        b1_loaded, b1_t, b1_c, b1_e = sem("b1_loaded"), sem("b1_t"), sem("b1_c"), sem("b1_e")
        b2_loaded = [sem("b2_loaded0"), sem("b2_loaded1")]
        idx_ready, gathered, added = sem("idx_ready"), sem("gathered"), sem("added")
        xt_ready, xh_done, xl_done = sem("xt_ready"), sem("xh_done"), sem("xl_done")
        h_ready, gelu_done, hh_done, hl_done = sem("h_ready"), sem("gelu_done"), sem("hh_done"), sem("hl_done")
        y_ready, y_read, y_done, passed = sem("y_ready"), sem("y_read"), sem("y_done"), sem("passed")
        block = ctx.enter_context(nc.Block())

        def run(eng, step):
            def static(s):
                step(s // 2, s % 2, lambda off: 0 <= s + off < NE)

            static(-1)
            static(0)
            with eng.Fori(0, (NE - 2) // 2) as i:
                for r in (1, 2):
                    step(i, r, lambda off: True)
            static(NE - 1)

        def count(i, r, off, per, add):
            return i * (2 * per) + ((r + off) * per + add)

        def fills(i, r, off, per, add=0):
            return i * per + ((r + off) // 2 * per + add)

        @block.sync
        def _(sp):
            sp.dma_start(b1raw[:], b1.rearrange("e (c p) -> (e c) p", p=128)).then_inc(b1_loaded, 16)

            def step(i, r, live):
                if live(1):
                    wait_alone(sp, w_high, count(i, r, 0, 4, 4), passed)
                    wait_alone(sp, w_low, count(i, r, 0, 4, 4), passed)
                    e1, e2 = bass.ds(count(i, r, 1, D, 0), D), bass.ds(count(i, r, 1, FF, 0), FF)
                    sp.dma_start(w1[:], W1.rearrange("e p f -> (e p) f")[e1].rearrange("(k p) f -> p k f", k=2))\
                      .then_inc(w_loaded, 16)
                    sp.dma_start(w2[:], W2.rearrange("e f d -> (e f) d")[e2].rearrange("(k p) d -> p k d", k=8))\
                      .then_inc(w_loaded, 16)
                    wait_alone(sp, y_read, count(i, r, -1, NG, NG), passed)
                    sp.dma_start(b2s[(r + 1) % 2][:], b2[bass.ds(count(i, r, 1, 1, 0), 1)].rearrange("a d -> (a d)")
                                 .partition_broadcast(128)).then_inc(b2_loaded[(r + 1) % 2], 16)

            run(sp, step)

        @block.gpsimd
        def _(pool):
            def step(i, r, live):
                if live(1):
                    p = (r + 1) % 2
                    wait_alone(pool, y_done, count(i, r, -1, NG, NG), passed)
                    wait_alone(pool, added, count(i, r, -1, 16 * NG, 16 * NG), passed)
                    e7 = bass.ds(count(i, r, 1, NG, 0), NG)
                    pool.tensor_copy(idx[p][:], T.idx[:].rearrange("p e g -> p (e g)")[:, e7]).then_inc(idx_ready, 1)
                    pool.tensor_copy(gate[p][:], T.gate[:].rearrange("p e g -> p (e g)")[:, e7]).then_inc(idx_ready, 1)
                    wait_alone(pool, idx_ready, count(i, r, 1, 2, 2), passed)
                    wait_alone(pool, xt_ready, count(i, r, 0, 4, 4), passed)
                    for g in range(NG):
                        pool.indirect_dma_start(out=ex[:, g, :], out_offset=None, in_=xn,
                                                in_offset=bass.IndirectOffsetOnAxis(ap=idx[p][:, g:g + 1], axis=0))\
                            .then_inc(gathered, 16)
                    for k in range(4):
                        src, h, l = ((w1, w1h[p], w1l[p]) if k < 2 else (w2, w2h[p], w2l[p]))
                        part = (slice(None), k) if k < 2 else (slice(None), slice(4 * (k - 2), 4 * (k - 1)))
                        wait_alone(pool, w_high, count(i, r, 1, 4, k + 1), passed)
                        pool.tensor_tensor(l[part], src[part], h[part].bitcast(F32), ALU.subtract).then_inc(w_low, 1)
                if live(0):
                    for g in range(NG):
                        wait_alone(pool, y_read, count(i, r, 0, NG, g + 1), passed)
                        pool.tensor_scalar(y[g][:], y[g][:], gate[r % 2][:, g:g + 1], None, ALU.mult).then_inc(y_done, 1)
                    wait_alone(pool, added, count(i, r, -1, 16 * NG, 16 * NG), passed)
                    for g in range(NG):
                        wait_alone(pool, y_done, count(i, r, 0, NG, g + 1), passed)
                        pool.indirect_dma_start(out=out, out_offset=bass.IndirectOffsetOnAxis(ap=idx[r % 2][:, g:g + 1], axis=0),
                                                in_=y[g][:], in_offset=None, compute_op=ALU.add).then_inc(added, 16)

            run(pool, step)
            pool.wait_ge(added, NE * NG * 16)

        @block.scalar
        def _(act):
            act.wait_ge(b1_t, 1)
            act.activation(b1s[:], pT[0][:, 0:64], ACT.Copy).then_inc(b1_c, 1)
            act.wait_ge(b1_c, 1)

            def step(i, r, live):
                if live(0):
                    b1e = b1s_of[r % 2]
                    act.activation(b1e[:], b1s[:, bass.ds(count(i, r, 0, 8, 0), 8)], ACT.Copy).then_inc(b1_e, 1)
                    act.wait_ge(b1_e, count(i, r, 0, 1, 1))
                    for c, (g0, g1) in enumerate(CHUNK):
                        n = (g1 - g0) * 128
                        for f in range(8):
                            k = 8 * c + f
                            act.wait_ge(h_ready, count(i, r, 0, 16, k + 1))
                            if k >= 2:
                                act.wait_ge(hl_done, count(i, r, 0, 16, k - 1))
                            act.activation(hid[f % 2][:, 0:n], p1[f % 2][:, 0:n], ACT.Gelu, bias=b1e[:, f:f + 1])\
                               .then_inc(gelu_done, 1)
                if live(1):
                    p = (r + 1) % 2
                    act.wait_ge(w_loaded, count(i, r, 1, 32, 32))
                    for k in range(4):
                        src, h = ((w1, w1h[p]) if k < 2 else (w2, w2h[p]))
                        part = (slice(None), k) if k < 2 else (slice(None), slice(4 * (k - 2), 4 * (k - 1)))
                        act.activation(h[part], src[part], ACT.Copy).then_inc(w_high, 1)
                    for k in range(4):
                        c, kk = divmod(k, 2)
                        g0, g1 = CHUNK[c]
                        act.wait_ge(xt_ready, count(i, r, 1, 4, k + 1))
                        act.activation(exh[:, kk, g0 * 128:g1 * 128], pT[kk][:, 0:(g1 - g0) * 128], ACT.Copy)\
                           .then_inc(xh_done, 1)

            run(act, step)

        @block.vector
        def _(dve):
            def step(i, r, live):
                if live(0):
                    for c, (g0, g1) in enumerate(CHUNK):
                        n = (g1 - g0) * 128
                        for f in range(8):
                            k, cols = 8 * c + f, slice(g0 * 128, g1 * 128)
                            dve.wait_ge(gelu_done, count(i, r, 0, 16, k + 1))
                            dve.tensor_copy(hh[:, f, cols], hid[f % 2][:, 0:n]).then_inc(hh_done, 1)
                            dve.wait_ge(hh_done, count(i, r, 0, 16, k + 1))
                            dve.tensor_tensor(hl[:, f, cols], hid[f % 2][:, 0:n], hh[:, f, cols].bitcast(F32),
                                              ALU.subtract).then_inc(hl_done, 1)
                    dve.wait_ge(b2_loaded[r % 2], fills(i, r, 0, 16, 16))

                    def results(g0, g1):
                        for g in range(g0, g1):
                            dve.wait_ge(y_ready, count(i, r, 0, NG, g + 1))
                            wait(dve, added, count(i, r, -1, 16 * NG, 16 * NG))
                            dve.tensor_tensor(y[g][:], p2[g % 2][:, 0:D], b2s[r % 2][:], ALU.add).then_inc(y_read, 1)

                    results(0, 4)
                if live(1):
                    for k in range(4):
                        c, kk = divmod(k, 2)
                        g0, g1 = CHUNK[c]
                        dve.wait_ge(xh_done, count(i, r, 1, 4, k + 1))
                        dve.tensor_tensor(exl[:, kk, g0 * 128:g1 * 128], pT[kk][:, 0:(g1 - g0) * 128],
                                          exh[:, kk, g0 * 128:g1 * 128].bitcast(F32), ALU.subtract).then_inc(xl_done, 1)
                if live(0):
                    results(4, NG)

            run(dve, step)

        @block.tensor
        def _(pe):
            pe.wait_ge(b1_loaded, 16)
            pe.transpose(pT[0][:, 0:64], b1raw[:], T.ident[0:64, 0:64]).then_inc(b1_t, 1)
            pe.wait_ge(b1_c, 1)

            def step(i, r, live):
                if live(0):
                    wh, wl, p = w1h[r % 2], w1l[r % 2], r % 2
                    pe.wait_ge(w_low, count(i, r, 0, 4, 4))
                    for c, (g0, g1) in enumerate(CHUNK):
                        n, cols = (g1 - g0) * 128, slice(g0 * 128, g1 * 128)
                        pe.wait_ge(xl_done, count(i, r, 0, 4, 2 * c + 2))
                        for f in range(8):
                            if 8 * c + f >= 2:
                                pe.wait_ge(gelu_done, count(i, r, 0, 16, 8 * c + f - 1))
                            fs, j = slice(f * 128, (f + 1) * 128), 0
                            for k in range(2):
                                for w, v in ((wh, exh), (wh, exl), (wl, exh)):
                                    last = pe.matmul(p1[f % 2][:, 0:n], w[:, k, fs], v[:, k, cols], start=(j == 0), stop=(j == 5))
                                    j += 1
                            last.then_inc(h_ready, 1)

                def second(g0, g1):
                    for g in range(g0, g1):
                        if g in (0, 4):
                            pe.wait_ge(hl_done, count(i, r, 0, 16, 8 if g == 0 else 16))
                        wait(pe, y_read, count(i, r, 0, NG, g - 1))
                        j, rows = 0, slice(g * 128, (g + 1) * 128)
                        for f in range(8):
                            for v, w in ((hh, w2h[r % 2]), (hh, w2l[r % 2]), (hl, w2h[r % 2])):
                                last = pe.matmul(p2[g % 2][:, 0:D], v[:, f, rows], w[:, f, :], start=(j == 0), stop=(j == 23))
                                j += 1
                        last.then_inc(y_ready, 1)

                if live(0):
                    second(0, 4)
                if live(1):
                    pe.wait_ge(gathered, count(i, r, 1, 16 * NG, 16 * NG))
                    for k in range(4):
                        c, kk = divmod(k, 2)
                        wait(pe, xl_done, count(i, r, 1, 4, k - 1))
                        for g in range(*CHUNK[c]):
                            last = pe.transpose(pT[kk][:, (g - CHUNK[c][0]) * 128:(g - CHUNK[c][0] + 1) * 128],
                                                ex[:, g, kk * 128:(kk + 1) * 128], T.ident[:])
                        last.then_inc(xt_ready, 1)
                if live(0):
                    second(4, NG)

            run(pe, step)


def flamingo_gated_layer(nc, x, ctx_512, g_xattn, g_ffn, Wq, bq, Wk, bk, Wv, bv, Wo, bo, Wg, W1, b1, W2, b2, out):
    T = Tiles()
    x, out = x.rearrange("b p d -> (b p) d"), out.rearrange("b p d -> (b p) d")
    xn = nc.dram_tensor("xn_scratch", [TOK, D], F32, kind="Internal").ap()
    with ExitStack() as ctx:
        T.lg = ctx.enter_context(nc.sbuf_tensor("lg", [LQ, B * NE], F32))
        T.idx = ctx.enter_context(nc.sbuf_tensor("idx", [128, NE, CAP // 128], I32))
        T.gate = ctx.enter_context(nc.sbuf_tensor("gate", [128, NE, CAP // 128], F32))
        attn = ExitStack()
        constants(nc, T, ctx, attn, Wq, bq, Wk, bk, Wv, bv, Wo, bo, Wg, g_xattn, g_ffn)
        with attn as own:
            T.qp = own.enter_context(nc.sbuf_tensor("qp", [128, 3, 2, TOK], BF16))
            queries(nc, T, x.rearrange("(b p) d -> b p d", p=LQ))
            attention(nc, T, x, ctx_512, out, xn)
        routing(nc, T)
        experts(nc, T, xn, W1, b1, W2, b2, out)


_INS = ['x', 'ctx_512', 'g_xattn', 'g_ffn', 'L0_xattn_Wq', 'L0_xattn_bq', 'L0_xattn_Wk', 'L0_xattn_bk', 'L0_xattn_Wv',
        'L0_xattn_bv', 'L0_xattn_Wo', 'L0_xattn_bo', 'L0_ffn_Wg', 'L0_ffn_W1', 'L0_ffn_b1', 'L0_ffn_W2', 'L0_ffn_b2']
_OUTS = [((B, LQ, D), 'float32')]


def kernel(**inputs):
    import numpy as _np
    import concourse.bacc as _bacc
    from concourse import mybir as _mybir
    from concourse.bass_utils import run_bass_kernel_spmd as _run

    nc = _bacc.Bacc("TRN2", target_bir_lowering=False, num_devices=1)
    arrays, args = {}, []
    for name in _INS:
        a = _np.ascontiguousarray(inputs[name])
        arrays[f"in_{name}_dram"] = a
        args.append(nc.dram_tensor(f"in_{name}_dram", a.shape, _mybir.dt.from_np(a.dtype), kind="ExternalInput").ap())
    for i, (shape, dtype) in enumerate(_OUTS):
        dt = _mybir.dt.from_np(_np.dtype(dtype))
        args.append(nc.dram_tensor(f"out_{i}_dram", shape, dt, kind="ExternalOutput").ap())
    flamingo_gated_layer(nc, *args)
    r = _run(nc, [arrays], core_ids=[0])
    got = tuple(r.results[0][f"out_{i}_dram"] for i in range(len(_OUTS)))
    return got[0]
```

```python
import concourse.bass as bass
from concourse import mybir
from contextlib import ExitStack

F32 = mybir.dt.float32
F32R = mybir.dt.float32r
BF16 = mybir.dt.bfloat16
I32 = mybir.dt.int32
ALU = mybir.AluOpType
ACT = mybir.ActivationFunctionType
AXX = mybir.AxisListType.X

B, LQ, D = 32, 112, 256
LK, C = 375, 128
H, DK = 16, 16
NE, FF = 8, 1024
TOK = B * LQ
CAP = TOK * 2 // NE
NG = CAP // 128
EPS = 1e-5

KCH = [(0, 128), (128, 128), (256, LK - 256)]
PAIRED = LK - LK % 2
KPAD = 384
K_SLOT = [0, 0, 0, 1, 1, 2]
Q_SLOT = [0, 1, 2, 0, 1, 0]
ROWS = 16 * len(K_SLOT)
VW = 64


def wait(eng, sem, count):
    if not (isinstance(count, int) and count <= 0):
        eng.wait_ge(sem, count)


def wait_alone(eng, sem, count, passed):
    wait(eng, sem, count)
    if not isinstance(count, int):
        eng.sem_inc(passed, 1)


class Sems:

    def __init__(self, nc, ctx, stage):
        self.nc, self.ctx, self.stage, self.made = nc, ctx, stage, {}

    def __call__(self, name):
        if name not in self.made:
            self.made[name] = self.ctx.enter_context(self.nc.semaphore(f"{self.stage}_{name}"))
        return self.made[name]


def queries(nc, T, x):
    G, NB = B // 4, 4 * LQ
    with ExitStack() as ctx:
        sem = Sems(nc, ctx, "q")

        def sb(name, shape, dt=F32):
            return ctx.enter_context(nc.sbuf_tensor("q_" + name, shape, dt))

        def banks(name, n=2):
            return [ctx.enter_context(nc.psum_tensor(f"q_{name}{i}", [128, 512], F32)) for i in range(n)]

        xin = [sb(f"xin{i}", [LQ, 4, D]) for i in range(2)]
        xn = [sb(f"xn{i}", [LQ, 4, D]) for i in range(2)]
        st = sb("st", [LQ, 4, 6])
        mv = [sb(f"mv{i}", [LQ, 4, 2]) for i in range(2)]
        yt = [sb(f"yt{i}", [LQ, 4]) for i in range(2)]
        std = sb("std", [LQ, 4])
        y0 = sb("y0", [LQ, 4])
        rstd = sb("rstd", [LQ, 4])
        xnT = sb("xnT", [128, 2, NB])
        q32 = [sb(f"q32_{i}", [128, 2, NB]) for i in range(2)]
        pT = banks("pT")
        pQ = banks("pQ")
        x_loaded = [sem("x_loaded0"), sem("x_loaded1")]
        chain, var_ready, std_ready, xn_ready = sem("chain"), sem("var_ready"), sem("std_ready"), sem("xn_ready")
        xt_ready, xt_copied, q_ready, q_copied = sem("xt_ready"), sem("xt_copied"), sem("q_ready"), sem("q_copied")
        q_high, q_rest, q_mid, q_cut = sem("q_high"), sem("q_rest"), sem("q_mid"), sem("q_cut")
        passed, passed_p = sem("passed"), sem("passed_p")
        block = ctx.enter_context(nc.Block())

        def groups(eng, body):
            body(0, 0)
            with eng.Fori(0, G // 2 - 1) as i:
                for r in range(2):
                    body(i * 2 + 1 + r, 1 - r)
            body(G - 1, 1)

        def tokens(g):
            return bass.ds(g * NB, NB)

        @block.sync
        def _(sp):
            def group(g, r):
                wait(sp, xn_ready, g + 1)
                sp.dma_start(xin[r][:], x[bass.ds(g * 4, 4)].rearrange("b p d -> p b d")).then_inc(x_loaded[r], 16)

            groups(sp, group)

        @block.vector
        def _(dve):
            STATS, NORM = 9, 4

            def statistics(g, g16, r):
                dve.wait_ge(x_loaded[r], g16)
                for b in range(4):
                    dve.bn_stats(st[:, b, :], xin[r][:, b, :]).then_inc(chain, 1)
                wait_alone(dve, chain, g * (STATS + NORM) + 4, passed)
                for b in range(4):
                    dve.bn_aggr(mv[r][:, b, :], st[:, b, :]).then_inc(chain, 1)
                wait_alone(dve, chain, g * (STATS + NORM) + 8, passed)
                dve.tensor_scalar(yt[r][:], mv[r][:, :, 1], EPS, None, ALU.add).then_inc(chain, 1)
                wait_alone(dve, chain, g * (STATS + NORM) + 9, passed)
                dve.sem_inc(var_ready, 1)

            def middle(g, r):
                dve.wait_ge(q_rest, g + 1)
                dve.tensor_copy(T.qp[:, 1, :, tokens(g)], q32[r][:]).then_inc(q_mid, 1)

            def group(g, r):
                links = g * (STATS + NORM) + STATS
                dve.wait_ge(std_ready, g + 1)
                dve.reciprocal(y0[:], std[:]).then_inc(chain, 1)
                wait_alone(dve, chain, links + 1, passed)
                dve.tensor_tensor(rstd[:], y0[:], y0[:], ALU.mult).then_inc(chain, 1)
                wait_alone(dve, chain, links + 2, passed)
                dve.scalar_tensor_tensor(rstd[:], rstd[:], -0.5, yt[r][:], ALU.mult, ALU.mult).then_inc(chain, 1)
                wait_alone(dve, chain, links + 3, passed)
                dve.scalar_tensor_tensor(rstd[:], rstd[:], 1.5, y0[:], ALU.add, ALU.mult).then_inc(chain, 1)
                wait_alone(dve, chain, links + 4, passed)
                wait(dve, xt_ready, g + 1)
                for b in range(4):
                    last = dve.tensor_scalar(xn[r][:, b, :], xin[r][:, b, :], mv[r][:, b, 0:1], rstd[:, b:b + 1],
                                             ALU.subtract, ALU.mult)
                last.then_inc(xn_ready, 1)
                if not (isinstance(g, int) and g == G - 1):
                    statistics(g + 1, loads(g, r), 1 - r)
                if not (isinstance(g, int) and g == 0):
                    middle(g - 1, 1 - r)

            def loads(g, r):
                return (g + 2 + r) * 8

            dve.sem_inc(xn_ready, 2)
            statistics(0, 16, 0)
            groups(dve, group)
            middle(G - 1, 1)

        @block.gpsimd
        def _(pool):
            def rest(g, r):
                wait_alone(pool, q_high, g + 1, passed_p)
                pool.tensor_tensor(q32[r][:], q32[r][:], T.qp[:, 0, :, tokens(g)], ALU.subtract).then_inc(q_rest, 1)

            def low(g, r):
                wait_alone(pool, q_mid, g + 1, passed_p)
                pool.tensor_tensor(T.qp[:, 2, :, tokens(g)], q32[r][:], T.qp[:, 1, :, tokens(g)],
                                   ALU.subtract).then_inc(q_cut, 1)

            def group(g, r):
                rest(g, r)
                if not (isinstance(g, int) and g == 0):
                    low(g - 1, 1 - r)

            groups(pool, group)
            low(G - 1, 1)

        @block.scalar
        def _(act):
            def root(g, r):
                act.wait_ge(var_ready, g + 1)
                act.activation(std[:], yt[r][:], ACT.Sqrt).then_inc(std_ready, 1)

            def group(g, r):
                wait(act, xt_ready, g + 3)
                for k in range(2):
                    act.activation(xnT[:, k, :], pT[k][:, 0:NB], ACT.Copy).then_inc(xt_copied, 1)
                if not (isinstance(g, int) and g == G - 1):
                    act.wait_ge(xn_ready, g + 3)
                    root(g + 1, 1 - r)
                wait(act, q_cut, g + 1)
                for t in range(2):
                    act.wait_ge(q_ready, g * 2 + t + 1)
                    act.activation(q32[r][:, t, :], pQ[t][:, 0:NB], ACT.Identity, bias=T.bq[:, t:t + 1],
                                   scale=float(DK) ** -0.5).then_inc(q_copied, 1)
                act.wait_ge(q_copied, g * 2 + 2)
                act.activation(T.qp[:, 0, :, tokens(g)], q32[r][:], ACT.Copy).then_inc(q_high, 1)

            act.sem_inc(q_cut, 2)
            root(0, 0)
            groups(act, group)

        @block.tensor
        def _(pe):
            def transposes(g, r):
                pe.wait_ge(xn_ready, g + 3)
                for k in range(2):
                    for b in range(4):
                        last = pe.transpose(pT[k][:, b * LQ:(b + 1) * LQ], xn[r][:, b, k * 128:(k + 1) * 128],
                                            T.ident[0:LQ, 0:LQ])
                last.then_inc(xt_ready, 1)

            def group(g, r):
                wait(pe, q_copied, g * 2)
                for k in range(2):
                    pe.wait_ge(xt_copied, g * 2 + 1 + k)
                    for t in range(2):
                        last = pe.matmul(pQ[t][:, 0:NB], T.wq[:, k, t, :], xnT[:, k, :], start=(k == 0),
                                         stop=(k == 1))
                        if k == 1:
                            last.then_inc(q_ready, 1)
                if not (isinstance(g, int) and g == G - 1):
                    transposes(g + 1, 1 - r)

            pe.sem_inc(xt_ready, 2)
            transposes(0, 0)
            groups(pe, group)


def attention(nc, T, x, ctx_in, x1_out, xn_out):
    with ExitStack() as ctx:
        sem = Sems(nc, ctx, "a")

        def sb(name, shape, dt=F32):
            return ctx.enter_context(nc.sbuf_tensor("a_" + name, shape, dt))

        def banks(name, n=2):
            return [ctx.enter_context(nc.psum_tensor(f"a_{name}{i}", [128, 512], F32)) for i in range(n)]

        craw = [sb(f"craw{i}", [128, 3, C]) for i in range(2)]
        cT = [sb(f"cT{i}", [128, LK]) for i in range(4)]
        k32 = sb("k32", [128, 2, LK])
        kp = [sb(f"kp{i}", [128, 3, 2, LK], BF16) for i in range(2)]
        kst, V = T.kst, T.V
        qst = sb("qst", [ROWS + 2, H, 4 * LQ], BF16)
        P = [sb(f"P{i}", [128, 3, 4 * LQ]) for i in range(2)]
        O = sb("O", [128, 2, 4 * LQ])
        nm = sb("nm", [LQ, H])
        mm = sb("mm", [LQ, 2, H], BF16)
        mT = sb("mT", [2 * H, LQ], BF16)
        rd = [sb(f"rd{i}", [LQ, 2, 2, 2]) for i in range(2)]
        cc = [sb(f"cc{i}", [LQ, D]) for i in range(2)]
        ccT = sb("ccT", [128, 2 * LQ])
        xb = [sb(f"xb{i}", [LQ, D]) for i in range(2)]
        x1 = [sb(f"x1_{i}", [LQ, D]) for i in range(2)]
        x2 = [sb(f"x2_{i}", [LQ, D]) for i in range(2)]
        x2T = sb("x2T", [128, 2 * LQ])
        stats, mv = sb("stats", [LQ, 6]), sb("mv", [LQ, 2])
        var, y, yy = sb("var", [LQ, 1]), sb("y", [LQ, 1]), sb("yy", [LQ, 1])
        pT = banks("pT")
        pS = banks("pS")
        pO = banks("pO")
        pM = banks("pM")

        ctx_loaded = [sem("ctx_loaded0"), sem("ctx_loaded1")]
        kst_loaded = [sem(f"kst_loaded{i}") for i in range(4)]
        qst_loaded = [sem("qst_loaded0"), sem("qst_loaded1")]
        mrow_loaded = [sem("mrow_loaded0"), sem("mrow_loaded1")]
        t_ready, s_ready, o_ready = sem("t_ready"), sem("s_ready"), sem("o_ready")
        ct_ready, k_ready, v_ready = sem("ct_ready"), sem("k_ready"), sem("v_ready")
        ot_ready, mt_ready = sem("ot_ready"), sem("mt_ready")
        exp_done, ct_copied, k_copied, o_copied, mt_copied = (sem("exp_done"), sem("ct_copied"), sem("k_copied"),
                                                            sem("o_copied"), sem("mt_copied"))
        s_used, m_split, v_copied, ot_used = sem("s_used"), sem("m_split"), sem("v_copied"), sem("ot_used")
        k_cut, kchain, k_high = sem("k_cut"), sem("kchain"), sem("k_high")
        cct_ready, cct_copied, wo_ready, x1_ready = sem("cct_ready"), sem("cct_copied"), sem("wo_ready"), sem("x1_ready")
        xt_ready, xt_copied, lg_ready, lg_copied = sem("xt_ready"), sem("xt_copied"), sem("lg_ready"), sem("lg_copied")
        wo_read, x2_ready, ln = sem("wo_read"), sem("x2_ready"), sem("ln")
        xb_loaded = [sem("xb_loaded0"), sem("xb_loaded1")]
        stored = [sem("stored0"), sem("stored1")]
        passed_dve = sem("passed_dve")
        passed, passed_sp = sem("passed"), sem("passed_sp")
        m_high, rd_ready = sem("m_high"), sem("rd_ready")

        S_HEADS = [[8], [9, 10], [11, 12], [13], [14], [15], [0, 1], [2], [3], [4], [5, 6], [7]]

        def run(eng, step):
            def static(m):
                step(m // 4, m % 4, lambda off: 0 <= m + off < B)

            for m in range(-4, 1):
                static(m)
            with eng.Fori(0, B // 4 - 2) as i:
                for r in range(1, 5):
                    step(i, r, lambda off: True)
            for m in range(B - 7, B + 1):
                static(m)

        def count(i, r, off, per, add):
            return i * (4 * per) + ((r + off) * per + add)

        def fills(i, r, off, every, per, add=0):
            return i * (4 // every * per) + ((r + off) // every * per + add)

        PIECES = [(ct_copied, 4, 1, 1), (k_copied, 4, 2, 1), (k_copied, 4, 2, 2), (v_copied, 2, 2, 1),
                  (v_copied, 2, 2, 2), (ot_used, 0, 2, 1), (ot_used, 0, 2, 2), (xt_copied, -1, 1, 1),
                  (mt_copied, 2, 1, 1), (cct_copied, 0, 1, 1), (wo_read, 0, 1, 1), (lg_copied, -1, 1, 1)]

        block = ctx.enter_context(nc.Block())

        @block.sync
        def _(sp):
            def step(i, r, live):
                if live(4):
                    wait_alone(sp, ct_ready, count(i, r, 2, 1, 1), passed_sp)
                    n = count(i, r, 4, LK, 0)
                    buf, src = r % 2, ctx_in.rearrange("b k c -> (b k) c")
                    sp.dma_start(craw[buf][:, 0:2, :], src[bass.ds(n, 256)].rearrange("(c p) d -> p c d", c=2))\
                      .then_inc(ctx_loaded[buf], 16)
                    sp.dma_start(craw[buf][0:KCH[2][1], 2, :], src[bass.ds(n + 256, KCH[2][1])])\
                      .then_inc(ctx_loaded[buf], 16)
                if r % 2 == 1 and live(3):
                    half = (r + 3) % 4 // 2
                    cols = slice(half * 2 * LQ, (half + 1) * 2 * LQ)
                    wait_alone(sp, t_ready, count(i, r, 0, 12, 12), passed_sp)
                    for s in range(len(Q_SLOT)):
                        src = T.qp[:, Q_SLOT[s], :, bass.ds(count(i, r, 3, LQ, 0), 2 * LQ)]
                        sp.dma_start(qst[16 * s:16 * s + 16, :, cols], src).then_inc(qst_loaded[half], 16)
                if live(3):
                    wait_alone(sp, k_cut, count(i, r, 3, 1, 1), passed_sp)
                    wait_alone(sp, mt_copied, count(i, r, 1, 1, 1), passed_sp)
                    for s in range(len(K_SLOT)):
                        sp.dma_start(kst[(r + 3) % 4][16 * s:16 * s + 16, :, 0:LK], kp[(r + 3) % 2][:, K_SLOT[s]])\
                          .then_inc(kst_loaded[(r + 3) % 4], 16)
                if live(1):
                    wait_alone(sp, x1_ready, count(i, r, -1, 1, 1), passed_sp)
                    sp.dma_start(xb[(r + 1) % 2][:], x[bass.ds(count(i, r, 1, LQ, 0), LQ)])\
                      .then_inc(xb_loaded[(r + 1) % 2], 16)
                if live(-1):
                    wait_alone(sp, x2_ready, count(i, r, -1, 1, 1), passed_sp)
                    rows = bass.ds(count(i, r, -1, LQ, 0), LQ)
                    sp.dma_start(x1_out[rows], x1[(r - 1) % 2][:]).then_inc(stored[(r - 1) % 2], 16)
                    sp.dma_start(xn_out[rows], x2[(r - 1) % 2][:]).then_inc(stored[(r - 1) % 2], 16)
                if live(2):
                    wait(sp, mt_copied, count(i, r, 2, 1, 1))
                    c0 = (r + 2) % 4 * LQ
                    sp.dma_start(qst[ROWS:ROWS + 2, :, c0:c0 + LQ], mT[:]).then_inc(mrow_loaded[(r + 2) % 2], 16)

            run(sp, step)
            for p in range(2):
                sp.wait_ge(stored[p], B // 2 * 32)

        @block.gpsimd
        def _(pool):
            def step(i, r, live):
                if not live(4):
                    return
                out, at = kp[(r + 4) % 2], [0]
                wait(pool, k_high, count(i, r, 4, 1, 1))

                def link(ins):
                    at[0] += 1
                    ins.then_inc(kchain, 1)
                    wait_alone(pool, kchain, count(i, r, 4, 2, at[0]), passed)

                link(pool.tensor_tensor(k32[:], k32[:], out[:, 0], ALU.subtract))
                link(pool.tensor_copy(out[:, 1], k32[:]))
                pool.tensor_tensor(out[:, 2], k32[:], out[:, 1], ALU.subtract).then_inc(k_cut, 1)

            run(pool, step)

        @block.scalar
        def _(act):
            def step(i, r, live):
                for u in range(12):
                    if live(1):
                        act.wait_ge(t_ready, count(i, r, 1, 12, u + 1))
                        quad, c = divmod(u, 3)
                        act.activation(P[quad % 2][:, c, :], pT[u % 2][:, 0:4 * LQ], ACT.Exp).then_inc(exp_done, 1)
                    if u == 7 and live(-1):
                        act.wait_ge(xt_ready, count(i, r, -1, 1, 1))
                        act.activation(x2T[:], pM[1][:, 0:2 * LQ], ACT.Copy).then_inc(xt_copied, 1)
                    if u == 11 and live(-1):
                        act.wait_ge(lg_ready, count(i, r, -1, 1, 1))
                        act.activation(T.lg[:, bass.ds(count(i, r, -1, NE, 0), NE)], pM[1][0:LQ, 0:NE], ACT.Copy)\
                           .then_inc(lg_copied, 1)
                    if u == 9 and live(0):
                        act.wait_ge(cct_ready, count(i, r, 0, 1, 1))
                        act.activation(ccT[:], pM[1][:, 0:2 * LQ], ACT.Copy).then_inc(cct_copied, 1)
                    if u == 0 and live(4):
                        act.wait_ge(ct_ready, count(i, r, 4, 1, 1))
                        act.activation(cT[r % 4][:], pM[0][:, 0:LK], ACT.Copy).then_inc(ct_copied, 1)
                    if u in (1, 2) and live(4):
                        t = u - 1
                        wait(act, k_cut, count(i, r, 4, 1, 0))
                        act.wait_ge(k_ready, count(i, r, 4, 2, t + 1))
                        act.activation(k32[:, t, :], pM[u % 2][:, 0:LK], ACT.Identity, bias=T.bk[:, t:t + 1])\
                           .then_inc(k_copied, 1)
                    if u == 2 and live(4):
                        act.wait_ge(k_copied, count(i, r, 4, 2, 2))
                        wait(act, kst_loaded[(r + 2) % 4], fills(i, r, 2, 4, 96, 96))
                        act.activation(kp[r % 2][:, 0], k32[:], ACT.Copy).then_inc(k_high, 1)
                    if u in (3, 4) and live(2):
                        act.wait_ge(v_ready, count(i, r, 2, 2, u - 2))
                        for c in ((0, 1) if u == 3 else (2,)):
                            n = KCH[c][1]
                            v = V[(r + 2) % 2][0:n, c, :, 0:34].rearrange("p g (s w) -> p g s w", s=2)[:, :, :, 0:DK]
                            src = pM[u % 2][0:n, (c % 2) * D:(c % 2 + 1) * D]
                            ins = act.activation(v, src.rearrange("p (g s w) -> p g s w", g=8, s=2), ACT.Copy)
                        ins.then_inc(v_copied, 1)
                    if u == 3 and live(0):
                        act.wait_ge(o_ready, count(i, r, 0, 2, 2))
                        act.activation(O[:, 1, :], pO[1][:, 0:4 * LQ], ACT.Copy).then_inc(o_copied, 1)
                    if u == 9 and live(1):
                        act.wait_ge(o_ready, count(i, r, 1, 2, 1))
                        act.activation(O[:, 0, :], pO[0][:, 0:4 * LQ], ACT.Copy).then_inc(o_copied, 1)
                    if u == 8 and live(2):
                        act.wait_ge(mt_ready, count(i, r, 2, 1, 1))
                        wait(act, mrow_loaded[(r + 1) % 2], fills(i, r, 1, 2, 16, 16))
                        act.activation(mT[:], pM[0][0:2 * H, 0:LQ // 2].bitcast(BF16), ACT.Copy).then_inc(mt_copied, 1)

            run(act, step)

        @block.vector
        def _(dve):
            def score_max(i, r, off, h):
                dve.wait_ge(s_ready, count(i, r, off, H, h + 1))
                if h == 0:
                    wait(dve, m_split, count(i, r, off, 1, 0))
                dve.tensor_reduce(nm[:, h:h + 1], pS[h % 2][0:LQ, 0:LK], AXX, ALU.max, negate=True).then_inc(s_used, 1)

            def layernorm(i, r, k):
                p, yb = (r - 1) % 2, y[:].bitcast(I32)
                if k == 0:
                    wait_alone(dve, ln, count(i, r, -1, 14, 1), passed_dve)
                    ins = dve.bn_aggr(mv[:], stats[:])
                else:
                    dve.wait_ge(ln, count(i, r, -1, 14, k + 1))
                if k == 1:
                    ins = dve.tensor_scalar(var[:], mv[:, 1:2], EPS, None, ALU.add)
                elif k == 2:
                    ins = dve.tensor_scalar(yb, var[:].bitcast(I32), 1, None, ALU.logical_shift_right)
                elif k == 3:
                    ins = dve.tensor_scalar(yb, yb, -1.0, float(0x5f3759df), ALU.mult, ALU.add)
                elif k == 13:
                    ins = dve.tensor_scalar(x2[p][:], x1[p][:], mv[:, 0:1], y[:], ALU.subtract, ALU.mult)
                elif k % 3 == 1:
                    ins = dve.tensor_tensor(yy[:], y[:], y[:], ALU.mult)
                elif k % 3 == 2:
                    ins = dve.scalar_tensor_tensor(yy[:], yy[:], -0.5, var[:], ALU.mult, ALU.mult)
                elif k:
                    ins = dve.scalar_tensor_tensor(y[:], yy[:], 1.5, y[:], ALU.add, ALU.mult)
                ins.then_inc(x2_ready if k == 13 else ln, 1)

            def step(i, r, live):
                for u in range(12):
                    if u < 7 and live(-1):
                        layernorm(i, r, 2 * u)
                    if u < 6 and live(2):
                        for h in S_HEADS[u]:
                            score_max(i, r, 2, h)
                    if u >= 6 and live(3):
                        for h in S_HEADS[u]:
                            score_max(i, r, 3, h)
                    if u < 7 and live(-1):
                        layernorm(i, r, 2 * u + 1)
                    if u == 5 and live(2):
                        dve.wait_ge(s_used, count(i, r, 2, H, H))
                        wait(dve, mt_ready, count(i, r, 2, 1, 0))
                        dve.tensor_copy(mm[:, 0, :], nm[:]).then_inc(m_high, 1)
                        dve.wait_ge(m_high, count(i, r, 2, 1, 1))
                        dve.tensor_tensor(mm[:, 1, :], nm[:], mm[:, 0, :], ALU.subtract).then_inc(m_split, 1)
                    if u in (5, 6) and live(0):
                        hb = u - 5
                        dve.wait_ge(ot_ready, count(i, r, 0, 2, hb + 1))
                        src = pM[u % 2][0:LQ, 0:512].rearrange("p (i s j w) -> p s i j w", i=2, s=2, j=2)
                        out = cc[r % 2][:, hb * 128:(hb + 1) * 128]\
                            .rearrange("p (i j s w) -> p s i j w", i=2, j=2, s=2)
                        for s in range(2):
                            dve.reciprocal(rd[hb][:, s], src[:, s, :, :, 17 * s + DK]).then_inc(rd_ready, 1)
                        dve.wait_ge(rd_ready, count(i, r, 0, 4, 2 * hb + 2))
                        for s in range(2):
                            ins = dve.tensor_tensor(out[:, s], src[:, s, :, :, 17 * s:17 * s + DK],
                                                    rd[hb][:, s].unsqueeze(3).to_broadcast([LQ, 2, 2, DK]), ALU.mult)
                        ins.then_inc(ot_used, 1)

                    if u == 10 and live(0):
                        xo, p = x1[r % 2], r % 2
                        wait(dve, stored[p], fills(i, r, -2, 2, 32, 32))
                        dve.wait_ge(wo_ready, count(i, r, 0, 1, 1))
                        dve.tensor_tensor(xo[:], pM[0][0:LQ, 0:D], T.bo[:], ALU.add).then_inc(wo_read, 1)
                        dve.wait_ge(wo_read, count(i, r, 0, 1, 1))
                        dve.wait_ge(xb_loaded[p], fills(i, r, 0, 2, 16, 16))
                        dve.scalar_tensor_tensor(xo[:], xo[:], T.gx[0:LQ], xb[p][:], ALU.mult, ALU.add).then_inc(x1_ready, 1)
                        dve.wait_ge(x1_ready, count(i, r, 0, 1, 1))
                        dve.bn_stats(stats[:], xo[:]).then_inc(ln, 1)

            run(dve, step)

        @block.tensor
        def _(pe):
            def bank_free(i, r, u, live):
                back, k = 0, u - 2
                while back < 6:
                    if k < 0:
                        back, k = back + 1, k + 12
                    sem_, off, per, nth = PIECES[k]
                    if live(off - back):
                        wait(pe, sem_, count(i, r, off - back, per, nth))
                        return
                    k -= 2

            def piece(i, r, u, bank):
                if u == 7:
                    pe.wait_ge(x2_ready, count(i, r, -1, 1, 1))
                    for k in range(2):
                        last = pe.transpose(bank[:, k * LQ:(k + 1) * LQ], x2[(r - 1) % 2][:, k * 128:(k + 1) * 128],
                                            T.ident[0:LQ, 0:LQ])
                    last.then_inc(xt_ready, 1)
                elif u == 0:
                    pe.wait_ge(ctx_loaded[r % 2], fills(i, r, 4, 2, 32, 32))
                    for c, (k0, n) in enumerate(KCH):
                        last = pe.transpose(bank[:, k0:k0 + n], craw[r % 2][0:n, c, :], T.ident[0:n, 0:n])
                    last.then_inc(ct_ready, 1)
                elif u in (1, 2):
                    pe.wait_ge(ct_copied, count(i, r, 4, 1, 1))
                    pe.matmul(bank[:, 0:LK], T.wk[:, u - 1, :], cT[r % 4][:], start=True, stop=True)\
                      .then_inc(k_ready, 1)
                elif u in (3, 4):
                    for c in ((0, 1) if u == 3 else (2,)):
                        k0, n = KCH[c]
                        last = pe.matmul(bank[0:n, (c % 2) * D:(c % 2 + 1) * D], cT[(r + 2) % 4][:, k0:k0 + n], T.wv[:],
                                         start=True, stop=True)
                    last.then_inc(v_ready, 1)
                elif u in (5, 6):
                    pe.wait_ge(o_copied, count(i, r, 0, 2, u - 4))
                    for k in range(4):
                        last = pe.transpose(bank[0:LQ, k * 128:(k + 1) * 128], O[:, u - 5, k * LQ:(k + 1) * LQ],
                                            T.ident[:])
                    last.then_inc(ot_ready, 1)
                elif u == 8:
                    pe.wait_ge(m_split, count(i, r, 2, 1, 1))
                    pe.transpose(bank[0:2 * H, 0:LQ // 2].bitcast(BF16), mm[:].rearrange("p a h -> p (a h)"),
                                 T.identb[0:LQ, 0:LQ]).then_inc(mt_ready, 1)
                elif u == 9:
                    pe.wait_ge(ot_used, count(i, r, 0, 2, 2))
                    for k in range(2):
                        last = pe.transpose(bank[:, k * LQ:(k + 1) * LQ], cc[r % 2][:, k * 128:(k + 1) * 128],
                                            T.ident[0:LQ, 0:LQ])
                    last.then_inc(cct_ready, 1)
                elif u == 10:
                    pe.wait_ge(cct_copied, count(i, r, 0, 1, 1))
                    for k in range(2):
                        last = pe.matmul(bank[0:LQ, 0:D], ccT[:, k * LQ:(k + 1) * LQ], T.wo[:, k, :], start=(k == 0),
                                         stop=(k == 1))
                    last.then_inc(wo_ready, 1)
                else:
                    pe.wait_ge(xt_copied, count(i, r, -1, 1, 1))
                    for k in range(2):
                        last = pe.matmul(bank[0:LQ, 0:NE], x2T[:, k * LQ:(k + 1) * LQ], T.wg[:, k, :], start=(k == 0),
                                         stop=(k == 1))
                    last.then_inc(lg_ready, 1)

            def step(i, r, live):
                for u in range(12):
                    quad, c = divmod(u, 3)
                    if live(1):
                        if u == 0:
                            pe.wait_ge(mrow_loaded[(r + 1) % 2], fills(i, r, 1, 2, 16, 16))
                        wait(pe, exp_done, count(i, r, 1, 12, u - 1))
                        cols = slice((r + 1) % 4 * LQ, ((r + 1) % 4 + 1) * LQ)
                        for j in range(4):
                            h = 4 * quad + j
                            last = pe.matmul(pT[u % 2][:, j * LQ:(j + 1) * LQ],
                                             kst[(r + 1) % 4][:, h, c * 128:(c + 1) * 128], qst[:, h, cols],
                                             start=True, stop=True)
                        last.then_inc(t_ready, 1)
                    off, heads = 2 if u < 6 else 3, S_HEADS[u]
                    if live(off):
                        if u == 6:
                            pe.wait_ge(kst_loaded[(r + 3) % 4], fills(i, r, 3, 4, 96, 96))
                            pe.wait_ge(qst_loaded[(r + 3) % 4 // 2], fills(i, r, 3, 4, 96, 96))
                        cols = slice((r + off) % 4 * LQ, ((r + off) % 4 + 1) * LQ)
                        for h in heads:
                            wait(pe, s_used, count(i, r, off, H, h - 1))
                            pe.matmul(pS[h % 2][0:LQ, 0:LK], qst[0:ROWS, h, cols], kst[(r + off) % 4][0:ROWS, h, 0:LK],
                                      start=True, stop=True).then_inc(s_ready, 1)
                    q2, b2 = (quad - 1, 1) if quad else (3, 0)
                    if live(b2):
                        pe.wait_ge(exp_done, count(i, r, b2, 12, 3 * q2 + c + 1))
                        if q2 == 0 and c == 0:
                            pe.wait_ge(v_copied, count(i, r, b2, 2, 2))
                        if q2 % 2 == 0 and c == 0:
                            wait(pe, o_copied, count(i, r, b2, 2, -1 + q2 // 2))
                        n = KCH[c][1]
                        for jt in range(2):
                            last = pe.matmul(pO[q2 // 2][64 * jt:64 * jt + VW, q2 % 2 * 2 * LQ:(q2 % 2 + 1) * 2 * LQ],
                                             V[(r + b2) % 2][0:n, c, 2 * q2 + jt, :],
                                             P[q2 % 2][0:n, c, jt * 2 * LQ:(jt + 1) * 2 * LQ],
                                             start=(c == 0), stop=(c == 2), skip_group_check=True)
                        if q2 % 2 == 1 and c == 2:
                            last.then_inc(o_ready, 1)
                    if live(PIECES[u][1]):
                        bank_free(i, r, u, live)
                        piece(i, r, u, pM[u % 2])

            run(pe, step)


class Tiles:
    pass


def constants(nc, T, ctx, attn, Wq, bq, Wk, bk, Wv, bv, Wo, bo, Wg, g_xattn, g_ffn):
    def sb(name, shape, dt=F32):
        return ctx.enter_context(nc.sbuf_tensor(name, shape, dt))

    T.ident, T.identb = sb("ident", [128, 128]), sb("identb", [128, 128], BF16)
    T.gf = sb("gf", [128, 1])

    def sb(name, shape, dt=F32):
        return attn.enter_context(nc.sbuf_tensor(name, shape, dt))

    T.wq, T.wk, T.wv = sb("wq", [128, 2, 2, 128]), sb("wk", [128, 2, 128]), sb("wv", [128, D])
    T.wo, T.wg = sb("wo", [128, 2, D]), sb("wg", [128, 2, NE])
    T.bq, T.bk, T.bo = sb("bq", [128, 2]), sb("bk", [128, 2]), sb("bo", [LQ, D])
    T.gx = sb("gx", [128, 1])
    T.kst = [sb(f"kst{i}", [ROWS + 2, H, KPAD], BF16) for i in range(4)]
    T.V = [sb(f"V{i}", [128, 3, H // 2, VW]) for i in range(2)]
    with ExitStack() as own:
        sem = Sems(nc, own, "c")
        wq_raw = own.enter_context(nc.sbuf_tensor("wq_raw", [128, 2, D], F32))
        wk_raw = own.enter_context(nc.sbuf_tensor("wk_raw", [128, D], F32))
        bq_raw = own.enter_context(nc.sbuf_tensor("bq_raw", [128, 2], F32))
        g_raw = own.enter_context(nc.sbuf_tensor("g_raw", [128, 2], F32))
        bv_raw = own.enter_context(nc.sbuf_tensor("bv_raw", [128, 2], F32))
        bv_wide = own.enter_context(nc.sbuf_tensor("bv_wide", [128, 2, LQ], F32))
        pB = own.enter_context(nc.psum_tensor("c_pB", [128, 512], F32))
        loaded, bq_loaded, zeroed = sem("loaded"), sem("bq_loaded"), sem("zeroed")
        bv_ready, bo_ready, vzeroed = sem("bv_ready"), sem("bo_ready"), sem("vzeroed")
        block = own.enter_context(nc.Block())

        @block.sync
        def _(sp):
            sp.dma_start(wq_raw[:], Wq.rearrange("(k p) n -> p k n", p=128)).then_inc(loaded, 16)
            sp.dma_start(wk_raw[:], Wk).then_inc(loaded, 16)
            sp.dma_start(T.wv[:], Wv).then_inc(loaded, 16)
            sp.dma_start(T.wo[:], Wo.rearrange("(k p) n -> p k n", p=128)).then_inc(loaded, 16)
            sp.dma_start(T.wg[:], Wg.rearrange("(k p) n -> p k n", p=128)).then_inc(loaded, 16)
            sp.wait_ge(loaded, 8 * 16 + 2 * 16)

        @block.scalar
        def _(act):
            act.dma_start(bq_raw[:], bq.rearrange("(h t d) -> d h t", h=8, t=2),
                          allow_slow_non_contiguous=True).then_inc(bq_loaded, 16)
            act.dma_start(T.bk[:], bk.rearrange("(h t d) -> d h t", h=8, t=2),
                          allow_slow_non_contiguous=True).then_inc(loaded, 16)
            act.dma_start(bv_raw[:], bv.rearrange("(k p) -> p k", p=128),
                          allow_slow_non_contiguous=True).then_inc(loaded, 16)
            act.dma_start(T.bo[:], bo.partition_broadcast(LQ)).then_inc(loaded, 16)
            act.dma_start(g_raw[:, 0:1], g_xattn.partition_broadcast(128)).then_inc(loaded, 16)
            act.dma_start(g_raw[:, 1:2], g_ffn.partition_broadcast(128)).then_inc(loaded, 16)
            act.wait_ge(bq_loaded, 16)
            act.activation(T.bq[:], bq_raw[:], ACT.Copy, scale=float(DK) ** -0.5)
            act.wait_ge(loaded, 10 * 16)
            act.activation(T.gx[:], g_raw[:, 0:1], ACT.Tanh)
            act.activation(T.gf[:], g_raw[:, 1:2], ACT.Tanh)

        @block.gpsimd
        def _(pool):
            for m in (T.ident, T.identb):
                pool.memset(m[:], 0.0).then_inc(zeroed, 1)
            for v in T.V:
                pool.memset(v[:], 0.0).then_inc(zeroed, 1)
            for k in T.kst:
                pool.memset(k[:, :, LK:KPAD], 0.0)
            pool.wait_ge(zeroed, 4)
            for v in T.V:
                for s in range(2):
                    pool.memset(v[:, :, :, 17 * s + DK:17 * s + DK + 1], 1.0)
            for m in (T.ident, T.identb):
                pool.affine_select(out=m[:], in_=m[:], compare_op=ALU.not_equal, fill=1.0, base=0,
                                   pattern=[[-1, 128]], channel_multiplier=1)

        @block.tensor
        def _(pe):
            pe.wait_ge(bv_ready, 1)
            pe.wait_ge(loaded, 10 * 16)
            for k in range(2):
                last = pe.matmul(pB[0:LQ, 0:D], bv_wide[:, k, :], T.wo[:, k, :], start=(k == 0), stop=(k == 1))
            last.then_inc(bo_ready, 1)

        @block.vector
        def _(dve):
            one = 0x3F803F80
            for k in T.kst:
                dve.memset(k[ROWS:ROWS + 2, :, 0:PAIRED].bitcast(I32), one)
                dve.memset(k[ROWS:ROWS + 2, :, PAIRED:LK], 1.0)
            dve.wait_ge(loaded, 10 * 16)
            dve.tensor_copy(bv_wide[:], bv_raw[:].unsqueeze(2).to_broadcast([128, 2, LQ])).then_inc(bv_ready, 1)
            dve.wait_ge(bo_ready, 1)
            dve.tensor_tensor(T.bo[:], pB[0:LQ, 0:D], T.bo[:], ALU.add)
            for k in range(2):
                dve.tensor_copy(T.wq[:, k].rearrange("p t (d h) -> p t d h", h=8),
                                wq_raw[:, k].rearrange("p (h t d) -> p t d h", h=8, t=2))
            dve.tensor_copy(T.wk[:].rearrange("p t (d h) -> p t d h", h=8),
                            wk_raw[:].rearrange("p (h t d) -> p t d h", h=8, t=2))


def feed_forward_tiles(nc, T, ctx):
    def sb(name, shape, dt=F32):
        return ctx.enter_context(nc.sbuf_tensor(name, shape, dt))

    T.w1, T.w2 = sb("w1", [128, 2, FF]), sb("w2", [128, 8, D])
    T.w1h, T.w1l = ([sb(f"w1{p}{i}", [128, 2, FF], F32R) for i in range(2)] for p in "hl")
    T.w2h, T.w2l = ([sb(f"w2{p}{i}", [128, 8, D], F32R) for i in range(2)] for p in "hl")
    T.parts, T.place = sb("parts", [LQ, NE, 3, B], BF16), sb("place", [LQ, NE, 2, B])
    T.parts_e, T.place_e = sb("parts_e", [LQ, 3, B], BF16), sb("place_e", [LQ, 2, B])
    T.iota_b, T.iota_g, T.iota_p = sb("iota_b", [LQ, B]), sb("iota_g", [LQ, NG]), sb("iota_p", [LQ, 1])
    T.iota_l = sb("iota_l", [LQ, 128], BF16)
    T.hot, T.A = sb("hot", [LQ, B, NG], BF16), sb("A", [LQ, B, 5, NG], BF16)
    T.L = [sb(f"L{i}", [LQ, B // 4, 128], BF16) for i in range(2)]
    T.rt = sb("rt", [128, 5, NG])
    T.idx, T.gate = sb("idx", [128, NG], I32), sb("gate", [128, NG])
    sem = Sems(nc, ctx, "f")
    T.w_loaded, T.w_high, T.w_low = sem("w_loaded"), sem("w_high"), sem("w_low")
    T.listing, T.l_ready, T.l_used, T.idx_ready = sem("listing"), sem("l_ready"), sem("l_used"), sem("idx_ready")
    T.passed = sem("passed")


LISTING = 11


def list_start(dve, T, at, expert):
    def link(k, ins):
        ins.then_inc(T.listing, 1)
        dve.wait_ge(T.listing, at(LISTING, k))

    wait(dve, T.l_used, at(4, 0))
    dve.tensor_copy(T.parts_e[:].rearrange("p c b -> p (c b)"),
                    T.parts[:].rearrange("p e c b -> p (e c b)")[:, bass.ds(expert(3 * B), 3 * B)]).then_inc(T.listing, 1)
    link(2, dve.tensor_copy(T.place_e[:].rearrange("p c b -> p (c b)"),
                            T.place[:].rearrange("p e c b -> p (e c b)")[:, bass.ds(expert(2 * B), 2 * B)]))
    link(3, dve.tensor_tensor(T.hot[:], T.place_e[:, 0].unsqueeze(2).to_broadcast([LQ, B, NG]),
                              T.iota_g[:].unsqueeze(1).to_broadcast([LQ, B, NG]), ALU.is_equal))
    dve.tensor_tensor(T.A[:, :, 0, :], T.hot[:], T.iota_b[:].unsqueeze(2).to_broadcast([LQ, B, NG]), ALU.mult)\
       .then_inc(T.listing, 1)
    dve.tensor_tensor(T.A[:, :, 1:4, :].rearrange("p b c g -> p c b g"), T.hot[:].unsqueeze(1).to_broadcast([LQ, 3, B, NG]),
                      T.parts_e[:].unsqueeze(3).to_broadcast([LQ, 3, B, NG]), ALU.mult).then_inc(T.listing, 1)
    dve.tensor_scalar(T.A[:, :, 4, :], T.hot[:], T.iota_p[:], None, ALU.mult).then_inc(T.listing, 1)


def list_rows(dve, T, at, j):
    wait(dve, T.l_used, at(4, j - 1))
    for b in range(B // 4):
        k = j * (B // 4) + b
        last = dve.tensor_scalar(T.L[j % 2][:, b, :], T.iota_l[:], T.place_e[:, 1, k:k + 1], None, ALU.is_equal)
    last.then_inc(T.l_ready, 1)


def list_products(pe, T, at, pR, j):
    pe.wait_ge(T.l_ready, at(4, j + 1))
    if j == 0:
        pe.wait_ge(T.listing, at(LISTING, 6))
    for b in range(B // 4):
        k = j * (B // 4) + b
        last = pe.matmul(pR[:, 0:5 * NG], T.L[j % 2][:, b, :], T.A[:, k].rearrange("p c g -> p (c g)"),
                         start=(k == 0), stop=(k == B - 1))
    last.then_inc(T.l_used, 1)


def list_end(dve, T, at, pR):
    def link(k, ins):
        ins.then_inc(T.listing, 1)
        dve.wait_ge(T.listing, at(LISTING, k))

    dve.wait_ge(T.l_used, at(4, 4))
    link(7, dve.tensor_copy(T.rt[:].rearrange("p c g -> p (c g)"), pR[:, 0:5 * NG]))
    wait(dve, T.idx_ready, at(2, 0))
    link(8, dve.scalar_tensor_tensor(T.idx[:], T.rt[:, 0, :], float(LQ), T.rt[:, 4, :], ALU.mult, ALU.add))
    link(9, dve.tensor_tensor(T.gate[:], T.rt[:, 1, :], T.rt[:, 2, :], ALU.add))
    link(10, dve.tensor_tensor(T.gate[:], T.gate[:], T.rt[:, 3, :], ALU.add))
    dve.tensor_scalar(T.gate[:], T.gate[:], T.gf[:], None, ALU.mult).then_inc(T.listing, 1)


def weights_high(act, T, p, at):
    act.wait_ge(T.w_loaded, at(32, 32))
    for k in range(4):
        src, h = ((T.w1, T.w1h[p]) if k < 2 else (T.w2, T.w2h[p]))
        part = (slice(None), k) if k < 2 else (slice(None), slice(4 * (k - 2), 4 * (k - 1)))
        act.activation(h[part], src[part], ACT.Copy).then_inc(T.w_high, 1)


def weights_low(pool, T, p, at):
    for k in range(4):
        src, h, l = ((T.w1, T.w1h[p], T.w1l[p]) if k < 2 else (T.w2, T.w2h[p], T.w2l[p]))
        part = (slice(None), k) if k < 2 else (slice(None), slice(4 * (k - 2), 4 * (k - 1)))
        wait_alone(pool, T.w_high, at(4, k + 1), T.passed)
        pool.tensor_tensor(l[part], src[part], h[part].bitcast(F32), ALU.subtract).then_inc(T.w_low, 1)


def load_weights(sp, T, W1, W2, rows1, rows2):
    sp.dma_start(T.w1[:], W1.rearrange("e p f -> (e p) f")[rows1].rearrange("(k p) f -> p k f", k=2))\
      .then_inc(T.w_loaded, 16)
    sp.dma_start(T.w2[:], W2.rearrange("e f d -> (e f) d")[rows2].rearrange("(k p) d -> p k d", k=8))\
      .then_inc(T.w_loaded, 16)


def routing(nc, T, W1, W2):
    EB = NE * B
    BIG = 4096.0
    with ExitStack() as ctx:
        sem = Sems(nc, ctx, "r")

        def sb(name, shape, dt=F32):
            return ctx.enter_context(nc.sbuf_tensor("r_" + name, shape, dt))

        def banks(name, n=2):
            return [ctx.enter_context(nc.psum_tensor(f"r_{name}{i}", [128, 512], F32)) for i in range(n)]

        en = sb("en", [LQ, EB])
        S = sb("S", [LQ, EB])
        Sr = sb("Sr", [LQ, EB])
        ST = sb("ST", [128, 2 * LQ])
        junk = sb("junk", [128, 3, 2 * LQ], BF16)
        tries, gap = sb("tries", [128, 3]), sb("gap", [128, 3])
        held = [sb(f"held{i}", [128, 4]) for i in range(2)]
        power = sb("power", [128, 1])
        factors = sb("factors", [128, 5, 3])
        cnt, ceq, row = sb("cnt", [128, 3], BF16), sb("ceq", [128, 1], BF16), sb("row", [128, 1], BF16)
        need, off = sb("need", [128, 1]), sb("off", [128, 1])
        gt, eq, cum, sel, ones = (sb(n, [128, 2 * LQ]) for n in ("gt", "eq", "cum", "sel", "ones"))
        same, below = sb("same", [128, 128], BF16), sb("below", [128, 128], BF16)
        pi, hi_i, lo_i = (sb(n, [LQ, EB], I32) for n in ("pi", "hi_i", "lo_i"))
        pT, pC, pP, pR = banks("pT", 1)[0], banks("pC", 1)[0], banks("pP", 1)[0], banks("pR", 1)[0]
        v, pe_done, act_done, consts = sem("v"), sem("pe_done"), sem("act_done"), sem("consts")
        factors_set = sem("factors_set")
        counted, summed = sem("counted"), sem("summed")
        block = ctx.enter_context(nc.Block())
        FACTORS = [[2.0 ** 32, 2.0 ** 64, 2.0 ** 96], [2.0 ** 8, 2.0 ** 16, 2.0 ** 24], [4.0, 16.0, 64.0],
                   [1.5, 2.0, 3.0], [0.125, 0.25, 0.375]]
        ROUNDS = 4 + 11

        def at(per, add):
            return add

        @block.sync
        def _(sp):
            load_weights(sp, T, W1, W2, slice(0, D), slice(0, FF))
            sp.wait_ge(T.w_loaded, 32)

        @block.gpsimd
        def _(pool):
            def then(ins):
                ins.then_inc(consts, 1)
                then.n += 1
                pool.wait_ge(consts, then.n)
            then.n = 0

            for k, row_of in enumerate(FACTORS):
                for j, f in enumerate(row_of):
                    pool.memset(factors[:, k, j:j + 1], f).then_inc(factors_set, 1)
            then(pool.iota(T.iota_b[:], pattern=[[1, B]], base=0, channel_multiplier=0, allow_small_or_imprecise_dtypes=True))
            then(pool.iota(T.iota_g[:], pattern=[[1, NG]], base=0, channel_multiplier=0, allow_small_or_imprecise_dtypes=True))
            then(pool.iota(T.iota_p[:], pattern=[[0, 1]], base=0, channel_multiplier=1, allow_small_or_imprecise_dtypes=True))
            then(pool.iota(T.iota_l[:], pattern=[[1, 128]], base=0, channel_multiplier=0, allow_small_or_imprecise_dtypes=True))
            then(pool.memset(ones[:], 1.0))
            then(pool.memset(same[:], 1.0))
            Q = B // 2
            blocks = same[:].rearrange("p (e q) -> p e q", q=Q)
            then(pool.affine_select(out=blocks, in_=blocks, compare_op=ALU.is_ge, fill=0.0, base=0,
                                    pattern=[[-Q, NE], [0, Q]], channel_multiplier=1))
            then(pool.affine_select(out=blocks, in_=blocks, compare_op=ALU.is_ge, fill=0.0, base=Q - 1,
                                    pattern=[[Q, NE], [0, Q]], channel_multiplier=-1))
            then(pool.affine_select(out=below[:], in_=same[:], compare_op=ALU.is_ge, fill=0.0, base=-1,
                                    pattern=[[1, 128]], channel_multiplier=-1))
            weights_low(pool, T, 0, at)

        @block.scalar
        def _(act):
            act.wait_ge(v, 1)
            act.activation(en[:].rearrange("p (e b) -> p e b", e=NE), en[:].rearrange("p (e b) -> p e b", e=NE), ACT.Exp, scale=-1.0)\
               .then_inc(act_done, 1)
            weights_high(act, T, 0, at)

        @block.tensor
        def _(pe):
            pe.wait_ge(v, 4)
            for h in range(2):
                last = pe.transpose(pT[:, h * LQ:(h + 1) * LQ], Sr[:, h * 128:(h + 1) * 128], T.ident[0:LQ, 0:LQ])
            last.then_inc(pe_done, 1)
            pe.wait_ge(consts, 9)

            def total(k):
                pe.wait_ge(counted, k)
                pe.matmul(pC[:, 0:3], same[:], cnt[:], start=True, stop=True).then_inc(summed, 1)

            for k in range(5):
                total(k + 1)
            with pe.Fori(0, (ROUNDS - 5) // 2) as i:
                for r in range(2):
                    total(i * 2 + 6 + r)
            pe.wait_ge(counted, ROUNDS + 1)
            pe.matmul(pC[:, 0:1], same[:], cnt[:, 0:1], start=True, stop=True)
            pe.matmul(pC[:, 1:2], below[:], ceq[:], start=True, stop=True).then_inc(summed, 1)
            pe.wait_ge(counted, ROUNDS + 2)
            pe.matmul(pC[:, 2:3], below[:], row[:], start=True, stop=True).then_inc(summed, 1)
            pe.wait_ge(counted, ROUNDS + 3)
            for h in range(2):
                last = pe.transpose(pP[0:LQ, h * 128:(h + 1) * 128], sel[:, h * LQ:(h + 1) * LQ], T.ident[:])
            last.then_inc(summed, 1)
            for j in range(4):
                list_products(pe, T, at, pR, j)

        @block.vector
        def _(dve):
            n = [0]

            def link(ins):
                n[0] += 1
                ins.then_inc(v, 1)
                dve.wait_ge(v, n[0])

            link(dve.tensor_scalar(en[:].rearrange("p (e b) -> p e b", e=NE), T.lg[:].rearrange("p (b e) -> p e b", e=NE),
                                   -87.0, None, ALU.max))
            dve.wait_ge(act_done, 1)
            link(dve.tensor_scalar(en[:], en[:], 1.0, None, ALU.add))
            link(dve.reciprocal(S[:], en[:]))
            link(dve.tensor_scalar(Sr[:].rearrange("p (h c) -> p h c", h=2), S[:].rearrange("p (c h) -> p h c", h=2),
                                   2.0 ** 64, 2.0 ** -62, ALU.mult, ALU.max))
            def by_expert(ap):
                return ap.rearrange("p (e b) -> p e b", e=NE)

            first, second, third = (T.parts[:, :, k, :] for k in range(3))
            link(dve.tensor_copy(first, by_expert(S[:])))
            link(dve.tensor_tensor(by_expert(S[:]), by_expert(S[:]), first, ALU.subtract))
            link(dve.tensor_copy(second, by_expert(S[:])))
            link(dve.tensor_tensor(third, by_expert(S[:]), second, ALU.subtract))
            dve.wait_ge(pe_done, 1)
            link(dve.tensor_copy(ST[:], pT[:, 0:2 * LQ]))
            link(dve.memset(held[0][:, 3:4], 2.0 ** -62))
            dve.wait_ge(factors_set, 15)
            link(dve.tensor_scalar(tries[:], factors[:, 0, :], held[0][:, 3:4], None, ALU.mult))

            def counts():
                for j in range(3):
                    ins = dve.tensor_scalar(junk[:, j], ST[:], tries[:, j:j + 1], None, ALU.is_ge, ALU.add,
                                            accum_out=cnt[:, j:j + 1])
                ins.then_inc(counted, 1)

            def best(k, at, r):
                dve.wait_ge(summed, k + 1)
                dve.scalar_tensor_tensor(held[r][:, 0:3], pC[:, 0:3], float(CAP), tries[:], ALU.is_ge, ALU.mult)\
                   .then_inc(v, 1)
                dve.wait_ge(v, at + 1)
                dve.tensor_reduce(held[1 - r][:, 3:4], held[r][:], mybir.AxisListType.X, ALU.max).then_inc(v, 1)
                dve.wait_ge(v, at + 2)

            for k in range(4):
                counts()
                best(k, n[0], k % 2)
                n[0] += 2
                now = held[1 - k % 2][:, 3:4]
                if k < 3:
                    link(dve.tensor_scalar(tries[:], factors[:, k + 1, :], now, None, ALU.mult))
            link(dve.tensor_scalar(power[:].bitcast(I32), now.bitcast(I32), 0x7F800000, None, ALU.bitwise_and))
            link(dve.tensor_scalar(gap[:], factors[:, 4, :], power[:], None, ALU.mult))
            link(dve.tensor_scalar(tries[:], gap[:], now, None, ALU.add))
            base = n[0]

            def fraction(k, at, r):
                counts()
                dve.tensor_scalar(gap[:], gap[:], 0.25, None, ALU.mult).then_inc(v, 1)
                best(k, at + 1, r)
                dve.tensor_scalar(tries[:], gap[:], held[1 - r][:, 3:4], None, ALU.add).then_inc(v, 1)
                dve.wait_ge(v, at + 4)

            fraction(4, base, 0)
            with dve.Fori(0, (ROUNDS - 5) // 2) as i:
                for r in range(2):
                    fraction(i * 2 + 5 + r, i * 8 + (base + 4 + 4 * r), 1 - r)
            n[0] = base + 4 * (ROUNDS - 4)
            cand = held[1][:, 3:4]
            dve.tensor_scalar(gt[:], ST[:], cand, None, ALU.is_gt, ALU.add, accum_out=cnt[:, 0:1])
            dve.tensor_scalar(eq[:], ST[:], cand, None, ALU.is_equal, ALU.add, accum_out=ceq[:]).then_inc(counted, 1)
            dve.wait_ge(counted, ROUNDS + 1)
            link(dve.tensor_tensor_scan(cum[:], ones[:], eq[:], 0.0, ALU.mult, ALU.add))
            dve.wait_ge(summed, ROUNDS + 1)
            link(dve.tensor_scalar(need[:], pC[:, 0:1], -1.0, float(CAP), ALU.mult, ALU.add))
            link(dve.tensor_copy(off[:], pC[:, 1:2]))
            link(dve.tensor_scalar(cum[:], cum[:], off[:], need[:], ALU.add, ALU.is_le))
            link(dve.tensor_tensor(cum[:], cum[:], eq[:], ALU.mult))
            link(dve.tensor_tensor(sel[:], cum[:], gt[:], ALU.add))
            link(dve.tensor_tensor_scan(cum[:], ones[:], sel[:], 0.0, ALU.mult, ALU.add))
            dve.tensor_copy(row[:], cum[:, 2 * LQ - 1:2 * LQ]).then_inc(counted, 1)
            dve.wait_ge(summed, ROUNDS + 2)
            link(dve.tensor_scalar(off[:], pC[:, 2:3], -(BIG + 1.0), None, ALU.add))
            link(dve.scalar_tensor_tensor(sel[:], cum[:], off[:], sel[:], ALU.add, ALU.mult))
            dve.tensor_scalar(sel[:], sel[:], BIG, None, ALU.add).then_inc(counted, 1)
            dve.wait_ge(summed, ROUNDS + 3)
            link(dve.tensor_copy(pi[:].rearrange("p (c h) -> p h c", h=2), pP[0:LQ, 0:EB].rearrange("p (h c) -> p h c", h=2)))
            link(dve.tensor_scalar(hi_i[:], pi[:], 7, None, ALU.logical_shift_right))
            link(dve.tensor_scalar(lo_i[:], pi[:], 127, None, ALU.bitwise_and))
            link(dve.tensor_copy(T.place[:, :, 0, :], by_expert(hi_i[:])))
            link(dve.tensor_copy(T.place[:, :, 1, :], by_expert(lo_i[:])))
            dve.wait_ge(consts, 9)
            list_start(dve, T, at, lambda per: 0)
            for j in range(4):
                list_rows(dve, T, at, j)
            list_end(dve, T, at, pR)


def experts(nc, T, xn, W1, b1, W2, b2, out):
    CHUNK = [(0, 4), (4, NG)]
    with ExitStack() as ctx:
        sem = Sems(nc, ctx, "e")

        def sb(name, shape, dt=F32):
            return ctx.enter_context(nc.sbuf_tensor("e_" + name, shape, dt))

        def banks(name, n=2):
            return [ctx.enter_context(nc.psum_tensor(f"e_{name}{i}", [128, 512], F32)) for i in range(n)]

        b1raw, b1s = sb("b1raw", [64, 128]), sb("b1s", [128, 64])
        b1s_of = [sb(f"b1e{i}", [128, 8]) for i in range(2)]
        b2s = [sb(f"b2s{i}", [128, D]) for i in range(2)]
        idx, gate = [sb(f"idx{i}", [128, NG], I32) for i in range(2)], [sb(f"gate{i}", [128, NG]) for i in range(2)]
        ex = sb("ex", [128, NG, D])
        exh, exl = sb("exh", [128, 2, CAP], F32R), sb("exl", [128, 2, CAP], F32R)
        hid = [sb(f"hid{i}", [128, 512]) for i in range(2)]
        hh, hl = sb("hh", [128, 8, CAP], F32R), sb("hl", [128, 8, CAP], F32R)
        y = [sb(f"y{i}", [128, D]) for i in range(NG)]
        p1, p2, pT, pR = banks("p1"), banks("p2"), banks("pT"), banks("pR", 1)[0]
        b1_loaded, b1_t, b1_c, b1_e = sem("b1_loaded"), sem("b1_t"), sem("b1_c"), sem("b1_e")
        b2_loaded = [sem("b2_loaded0"), sem("b2_loaded1")]
        gathered, added = sem("gathered"), sem("added")
        xt_ready, xh_done, xl_done = sem("xt_ready"), sem("xh_done"), sem("xl_done")
        h_ready, gelu_done, hh_done, hl_done = sem("h_ready"), sem("gelu_done"), sem("hh_done"), sem("hl_done")
        y_ready, y_read, y_done, passed = sem("y_ready"), sem("y_read"), sem("y_done"), sem("passed")
        block = ctx.enter_context(nc.Block())

        def run(eng, step):
            def static(s):
                step(s // 2, s % 2, lambda off: 0 <= s + off < NE)

            static(-1)
            static(0)
            with eng.Fori(0, (NE - 4) // 2) as i:
                for r in (1, 2):
                    step(i, r, lambda off: True)
            for s in range(NE - 3, NE):
                static(s)

        def count(i, r, off, per, add):
            return i * (2 * per) + ((r + off) * per + add)

        def of(i, r, off):
            return lambda per, add: count(i, r, off, per, add)

        def fills(i, r, off, per, add=0):
            return i * per + ((r + off) // 2 * per + add)

        @block.sync
        def _(sp):
            sp.dma_start(b1raw[:], b1.rearrange("e (c p) -> (e c) p", p=128)).then_inc(b1_loaded, 16)

            def step(i, r, live):
                if live(0) and live(1):
                    wait_alone(sp, T.w_high, count(i, r, 0, 4, 4), passed)
                    wait_alone(sp, T.w_low, count(i, r, 0, 4, 4), passed)
                    load_weights(sp, T, W1, W2, bass.ds(count(i, r, 1, D, 0), D), bass.ds(count(i, r, 1, FF, 0), FF))
                if live(1):
                    wait_alone(sp, y_read, count(i, r, -1, NG, NG), passed)
                    sp.dma_start(b2s[(r + 1) % 2][:], b2[bass.ds(count(i, r, 1, 1, 0), 1)].rearrange("a d -> (a d)")
                                 .partition_broadcast(128)).then_inc(b2_loaded[(r + 1) % 2], 16)

            run(sp, step)

        @block.gpsimd
        def _(pool):
            def step(i, r, live):
                if live(1):
                    p = (r + 1) % 2
                    wait_alone(pool, y_done, count(i, r, -1, NG, NG), passed)
                    wait_alone(pool, added, count(i, r, -1, 16 * NG, 16 * NG), passed)
                    wait_alone(pool, T.listing, count(i, r, 1, LISTING, LISTING), passed)
                    pool.tensor_copy(idx[p][:], T.idx[:]).then_inc(T.idx_ready, 1)
                    pool.tensor_copy(gate[p][:], T.gate[:]).then_inc(T.idx_ready, 1)
                    wait_alone(pool, T.idx_ready, count(i, r, 1, 2, 2), passed)
                    wait_alone(pool, xt_ready, count(i, r, 0, 4, 4), passed)
                    for g in range(NG):
                        pool.indirect_dma_start(out=ex[:, g, :], out_offset=None, in_=xn,
                                                in_offset=bass.IndirectOffsetOnAxis(ap=idx[p][:, g:g + 1], axis=0))\
                            .then_inc(gathered, 16)
                    if live(0):
                        weights_low(pool, T, p, of(i, r, 1))
                if live(0):
                    for g in range(NG):
                        wait_alone(pool, y_read, count(i, r, 0, NG, g + 1), passed)
                        pool.tensor_scalar(y[g][:], y[g][:], gate[r % 2][:, g:g + 1], None, ALU.mult).then_inc(y_done, 1)
                    wait_alone(pool, added, count(i, r, -1, 16 * NG, 16 * NG), passed)
                    for g in range(NG):
                        wait_alone(pool, y_done, count(i, r, 0, NG, g + 1), passed)
                        pool.indirect_dma_start(out=out, out_offset=bass.IndirectOffsetOnAxis(ap=idx[r % 2][:, g:g + 1], axis=0),
                                                in_=y[g][:], in_offset=None, compute_op=ALU.add).then_inc(added, 16)

            run(pool, step)
            pool.wait_ge(added, NE * NG * 16)

        @block.scalar
        def _(act):
            act.wait_ge(b1_t, 1)
            act.activation(b1s[:], pT[0][:, 0:64], ACT.Copy).then_inc(b1_c, 1)
            act.wait_ge(b1_c, 1)

            def step(i, r, live):
                if live(0):
                    b1e = b1s_of[r % 2]
                    act.activation(b1e[:], b1s[:, bass.ds(count(i, r, 0, 8, 0), 8)], ACT.Copy).then_inc(b1_e, 1)
                    act.wait_ge(b1_e, count(i, r, 0, 1, 1))
                    for c, (g0, g1) in enumerate(CHUNK):
                        n = (g1 - g0) * 128
                        for f in range(8):
                            k = 8 * c + f
                            act.wait_ge(h_ready, count(i, r, 0, 16, k + 1))
                            if k >= 2:
                                act.wait_ge(hl_done, count(i, r, 0, 16, k - 1))
                            act.activation(hid[f % 2][:, 0:n], p1[f % 2][:, 0:n], ACT.Gelu, bias=b1e[:, f:f + 1])\
                               .then_inc(gelu_done, 1)
                if live(1):
                    if live(0):
                        weights_high(act, T, (r + 1) % 2, of(i, r, 1))
                    for k in range(4):
                        c, kk = divmod(k, 2)
                        g0, g1 = CHUNK[c]
                        act.wait_ge(xt_ready, count(i, r, 1, 4, k + 1))
                        act.activation(exh[:, kk, g0 * 128:g1 * 128], pT[kk][:, 0:(g1 - g0) * 128], ACT.Copy)\
                           .then_inc(xh_done, 1)

            run(act, step)

        @block.vector
        def _(dve):
            def step(i, r, live):
                if live(0):
                    for c, (g0, g1) in enumerate(CHUNK):
                        n = (g1 - g0) * 128
                        for f in range(8):
                            k, cols = 8 * c + f, slice(g0 * 128, g1 * 128)
                            dve.wait_ge(gelu_done, count(i, r, 0, 16, k + 1))
                            dve.tensor_copy(hh[:, f, cols], hid[f % 2][:, 0:n]).then_inc(hh_done, 1)
                            dve.wait_ge(hh_done, count(i, r, 0, 16, k + 1))
                            dve.tensor_tensor(hl[:, f, cols], hid[f % 2][:, 0:n], hh[:, f, cols].bitcast(F32),
                                              ALU.subtract).then_inc(hl_done, 1)
                    dve.wait_ge(b2_loaded[r % 2], fills(i, r, 0, 16, 16))

                    def results(g0, g1):
                        for g in range(g0, g1):
                            dve.wait_ge(y_ready, count(i, r, 0, NG, g + 1))
                            wait(dve, added, count(i, r, -1, 16 * NG, 16 * NG))
                            dve.tensor_tensor(y[g][:], p2[g % 2][:, 0:D], b2s[r % 2][:], ALU.add).then_inc(y_read, 1)

                new = of(i, r, 2)
                if live(2):
                    list_start(dve, T, new, lambda per: count(i, r, 2, per, 0))
                for g in range(4):
                    if live(0):
                        results(g, g + 1)
                    if live(2):
                        list_rows(dve, T, new, g)
                if live(2) and not live(0):
                    list_end(dve, T, new, pR)

                def tokens_low(c):
                    g0, g1 = CHUNK[c]
                    for kk in range(2):
                        dve.wait_ge(xh_done, count(i, r, 1, 4, 2 * c + kk + 1))
                        dve.tensor_tensor(exl[:, kk, g0 * 128:g1 * 128], pT[kk][:, 0:(g1 - g0) * 128],
                                          exh[:, kk, g0 * 128:g1 * 128].bitcast(F32), ALU.subtract).then_inc(xl_done, 1)
                if live(1):
                    tokens_low(0)
                if live(0):
                    results(4, 5)
                    if live(2):
                        list_end(dve, T, new, pR)
                if live(1):
                    tokens_low(1)
                if live(0):
                    results(5, NG)

            run(dve, step)

        @block.tensor
        def _(pe):
            pe.wait_ge(b1_loaded, 16)
            pe.transpose(pT[0][:, 0:64], b1raw[:], T.ident[0:64, 0:64]).then_inc(b1_t, 1)
            pe.wait_ge(b1_c, 1)

            def step(i, r, live):
                if live(0):
                    wh, wl = T.w1h[r % 2], T.w1l[r % 2]
                    pe.wait_ge(T.w_low, count(i, r, 0, 4, 4))
                    for c, (g0, g1) in enumerate(CHUNK):
                        n, cols = (g1 - g0) * 128, slice(g0 * 128, g1 * 128)
                        pe.wait_ge(xl_done, count(i, r, 0, 4, 2 * c + 2))
                        for f in range(8):
                            if 8 * c + f >= 2:
                                pe.wait_ge(gelu_done, count(i, r, 0, 16, 8 * c + f - 1))
                            fs, j = slice(f * 128, (f + 1) * 128), 0
                            for k in range(2):
                                for w, v in ((wh, exh), (wh, exl), (wl, exh)):
                                    last = pe.matmul(p1[f % 2][:, 0:n], w[:, k, fs], v[:, k, cols], start=(j == 0), stop=(j == 5))
                                    j += 1
                            last.then_inc(h_ready, 1)

                def second(g0, g1):
                    for g in range(g0, g1):
                        if g in (0, 4):
                            pe.wait_ge(hl_done, count(i, r, 0, 16, 8 if g == 0 else 16))
                        wait(pe, y_read, count(i, r, 0, NG, g - 1))
                        j, rows = 0, slice(g * 128, (g + 1) * 128)
                        for f in range(8):
                            for v, w in ((hh, T.w2h[r % 2]), (hh, T.w2l[r % 2]), (hl, T.w2h[r % 2])):
                                last = pe.matmul(p2[g % 2][:, 0:D], v[:, f, rows], w[:, f, :], start=(j == 0), stop=(j == 23))
                                j += 1
                        last.then_inc(y_ready, 1)

                new = of(i, r, 2)
                for g in range(4):
                    if live(0):
                        second(g, g + 1)
                    if live(2) and (g > 0 or not live(0)):
                        list_products(pe, T, new, pR, g - 1 if live(0) else g)
                def transposes(c):
                    for kk in range(2):
                        wait(pe, xl_done, count(i, r, 1, 4, 2 * c + kk - 1))
                        for g in range(*CHUNK[c]):
                            last = pe.transpose(pT[kk][:, (g - CHUNK[c][0]) * 128:(g - CHUNK[c][0] + 1) * 128],
                                                ex[:, g, kk * 128:(kk + 1) * 128], T.ident[:])
                        last.then_inc(xt_ready, 1)

                if live(1):
                    pe.wait_ge(gathered, count(i, r, 1, 16 * NG, 16 * NG))
                    transposes(0)
                if live(0):
                    second(4, 5)
                    if live(2):
                        list_products(pe, T, new, pR, 3)
                if live(1):
                    transposes(1)
                if live(0):
                    second(5, NG)

            run(pe, step)


def flamingo_gated_layer(nc, x, ctx_512, g_xattn, g_ffn, Wq, bq, Wk, bk, Wv, bv, Wo, bo, Wg, W1, b1, W2, b2, out):
    T = Tiles()
    x, out = x.rearrange("b p d -> (b p) d"), out.rearrange("b p d -> (b p) d")
    xn = nc.dram_tensor("xn_scratch", [TOK, D], F32, kind="Internal").ap()
    with ExitStack() as ctx:
        T.lg = ctx.enter_context(nc.sbuf_tensor("lg", [LQ, B * NE], F32))
        attn = ExitStack()
        constants(nc, T, ctx, attn, Wq, bq, Wk, bk, Wv, bv, Wo, bo, Wg, g_xattn, g_ffn)
        with attn as own:
            T.qp = own.enter_context(nc.sbuf_tensor("qp", [128, 3, 2, TOK], BF16))
            queries(nc, T, x.rearrange("(b p) d -> b p d", p=LQ))
            attention(nc, T, x, ctx_512, out, xn)
        feed_forward_tiles(nc, T, ctx)
        routing(nc, T, W1, W2)
        experts(nc, T, xn, W1, b1, W2, b2, out)


_INS = ['x', 'ctx_512', 'g_xattn', 'g_ffn', 'L0_xattn_Wq', 'L0_xattn_bq', 'L0_xattn_Wk', 'L0_xattn_bk', 'L0_xattn_Wv',
        'L0_xattn_bv', 'L0_xattn_Wo', 'L0_xattn_bo', 'L0_ffn_Wg', 'L0_ffn_W1', 'L0_ffn_b1', 'L0_ffn_W2', 'L0_ffn_b2']
_OUTS = [((B, LQ, D), 'float32')]


def kernel(**inputs):
    import numpy as _np
    import concourse.bacc as _bacc
    from concourse import mybir as _mybir
    from concourse.bass_utils import run_bass_kernel_spmd as _run

    nc = _bacc.Bacc("TRN2", target_bir_lowering=False, num_devices=1)
    arrays, args = {}, []
    for name in _INS:
        a = _np.ascontiguousarray(inputs[name])
        arrays[f"in_{name}_dram"] = a
        args.append(nc.dram_tensor(f"in_{name}_dram", a.shape, _mybir.dt.from_np(a.dtype), kind="ExternalInput").ap())
    for i, (shape, dtype) in enumerate(_OUTS):
        dt = _mybir.dt.from_np(_np.dtype(dtype))
        args.append(nc.dram_tensor(f"out_{i}_dram", shape, dt, kind="ExternalOutput").ap())
    flamingo_gated_layer(nc, *args)
    r = _run(nc, [arrays], core_ids=[0])
    got = tuple(r.results[0][f"out_{i}_dram"] for i in range(len(_OUTS)))
    return got[0]
```
